# Optimizing a Trainium2 kernel written in Bass

```python
import numpy as np
import jax
import jax.numpy as jnp

def _softmax(x, axis=-1):
    return jax.nn.softmax(x, axis=axis)

def _gelu(x):
    return jax.nn.gelu(x, approximate=True)

def _silu(x):
    return jax.nn.silu(x)

def _sigmoid(x):
    return jax.nn.sigmoid(x)

def _layernorm(x, axis=-1, eps=1e-05):
    m = jnp.mean(x, axis=axis, keepdims=True)
    v = jnp.var(x, axis=axis, keepdims=True)
    return (x - m) / jnp.sqrt(v + eps)

def _scatter_add(tgt, idx, src, axis=0):
    return tgt.at[idx].add(src)

def _segment_sum(src, seg, n):
    return jax.ops.segment_sum(src, seg, n)
kernel_name = 'mk_gnn_preln_d4_gnn_r32_ad1756'

def setup_inputs(seed: int=0):
    np.random.seed(seed)
    _w = jnp.asarray

    def _rec_inputs():
        import jax
        import jax.numpy as jnp
        _gk = jax.random.key(seed)
        x = 8.953e-05 + 1 * jax.random.normal(jax.random.fold_in(_gk, 1), (3125, 32), jnp.float32)
        src = jax.random.randint(jax.random.fold_in(_gk, 2), (100000,), 0, 3125, jnp.int32)
        dst = jax.random.randint(jax.random.fold_in(_gk, 3), (100000,), 0, 3125, jnp.int32)
        _o = jnp.argsort(dst, stable=True)
        src = src[_o]
        dst = dst[_o]
        edge_attr_2 = jax.random.uniform(jax.random.fold_in(_gk, 11), (100000, 2), jnp.float32, 0.0, 1)
        edge_attr_3 = 0.000844983 + 0.999762 * jax.random.normal(jax.random.fold_in(_gk, 12), (100000, 3), jnp.float32)
        edge_weight = jax.random.uniform(jax.random.fold_in(_gk, 14), (100000,), jnp.float32, 0.0, 1)
        node_vec1 = jax.random.uniform(jax.random.fold_in(_gk, 15), (3125, 1), jnp.float32, 0.0, 1)
        return (x, src, dst, edge_attr_2, edge_attr_3, edge_weight, node_vec1)
    x, src, dst, edge_attr_2, edge_attr_3, edge_weight, node_vec1 = _rec_inputs()

    def _L0_gnn_setup():
        import jax, jax.numpy as jnp
        import numpy as np
        from math import factorial, pi, sqrt
        MUL = 8
        RS = [(MUL, 0), (MUL, 1)]
        N_NODES = 625
        N_EDGES = 20000
        FEAT_DIM = sum((m * (2 * l + 1) for m, l in RS))
        R_DIM = sum((mo * mi * (2 * min(lo, li) + 1) for mo, lo in RS for mi, li in RS))
        HIDDEN = 64

        def _cg(j1, j2, j3, m1, m2, m3):
            if m1 + m2 != m3:
                return 0.0
            f = factorial
            pre = sqrt((2 * j3 + 1) * f(j3 + j1 - j2) * f(j3 - j1 + j2) * f(j1 + j2 - j3) / f(j1 + j2 + j3 + 1))
            pre *= sqrt(f(j3 + m3) * f(j3 - m3) * f(j1 - m1) * f(j1 + m1) * f(j2 - m2) * f(j2 + m2))
            kmin = max(0, j2 - j3 - m1, j1 - j3 + m2)
            kmax = min(j1 + j2 - j3, j1 - m1, j2 + m2)
            s = 0.0
            for k in range(kmin, kmax + 1):
                s += (-1) ** k / (f(k) * f(j1 + j2 - j3 - k) * f(j1 - m1 - k) * f(j2 + m2 - k) * f(j3 - j2 + m1 + k) * f(j3 - j1 - m2 + k))
            return pre * s

        def _w3j_complex(l1, l2, l3):
            w = np.zeros((2 * l1 + 1, 2 * l2 + 1, 2 * l3 + 1))
            for m1 in range(-l1, l1 + 1):
                for m2 in range(-l2, l2 + 1):
                    m3 = -(m1 + m2)
                    if abs(m3) <= l3:
                        w[m1 + l1, m2 + l2, m3 + l3] = (-1) ** (l1 - l2 - m3) / sqrt(2 * l3 + 1) * _cg(l1, l2, l3, m1, m2, -m3)
            return w

        def _A(l):
            A = np.zeros((2 * l + 1, 2 * l + 1), dtype=complex)
            A[l, l] = 1.0
            for m in range(1, l + 1):
                A[l + m, l + m] = (-1) ** m / sqrt(2)
                A[l + m, l - m] = 1.0 / sqrt(2)
                A[l - m, l - m] = 1j / sqrt(2)
                A[l - m, l + m] = -1j * (-1) ** m / sqrt(2)
            return A

        def real_w3j(l1, l2, l3):
            wc = _w3j_complex(l1, l2, l3).astype(complex)
            wr = np.einsum('abc,ma,nb,oc->mno', wc, _A(l1).conj(), _A(l2).conj(), _A(l3).conj())
            i = int(np.argmax(np.abs(wr)))
            ph = wr.flat[i] / abs(wr.flat[i])
            wr = wr / ph
            assert np.abs(wr.imag).max() < 1e-10
            return np.real(wr).astype(np.float32)
        _W3J = {}
        for _mo, _lo in RS:
            for _mi, _li in RS:
                for _lf in range(abs(_lo - _li), _lo + _li + 1):
                    if (_lo, _lf, _li) not in _W3J:
                        _W3J[_lo, _lf, _li] = jnp.asarray(real_w3j(_lo, _lf, _li))
        _NORM = []
        for _mo, _lo in RS:
            _num = sum((mi * (2 * min(_lo, li) + 1) for mi, li in RS))
            _NORM.append(sqrt(4.0 * pi) * sqrt(2.0 * _lo + 1.0) / sqrt(_num))
        _F_OFFS = [0] + list(np.cumsum([mi * (2 * li + 1) for mi, li in RS]))

        def spherical_harmonics(rel_vec):
            r = rel_vec / jnp.linalg.norm(rel_vec, axis=-1, keepdims=True)
            x, y, z = (r[:, 0], r[:, 1], r[:, 2])
            y0 = jnp.full_like(x, 0.5 / sqrt(pi))[:, None]
            c1 = sqrt(3.0 / (4.0 * pi))
            y1 = c1 * jnp.stack([y, z, x], axis=-1)
            c2a = 0.5 * sqrt(15.0 / pi)
            c2b = 0.25 * sqrt(5.0 / pi)
            c2c = 0.25 * sqrt(15.0 / pi)
            y2 = jnp.stack([c2a * x * y, c2a * y * z, c2b * (3.0 * z * z - 1.0), c2a * x * z, c2c * (x * x - y * y)], axis=-1)
            return jnp.concatenate([y0, y1, y2], axis=-1)
        key = jax.random.key(seed)
        ks = jax.random.split(key, 6)
        features = jax.random.normal(ks[0], (N_NODES, FEAT_DIM), dtype=jnp.float32)
        abs_distances = jax.random.uniform(ks[1], (N_EDGES,), dtype=jnp.float32, minval=0.1, maxval=1.0)
        rel_vec = jax.random.normal(ks[2], (N_EDGES, 3), dtype=jnp.float32)
        edge_index = jax.random.randint(ks[3], (2, N_EDGES), 0, N_NODES, dtype=jnp.int32)
        w1 = jax.random.normal(ks[4], (1, HIDDEN), dtype=jnp.float32)
        b1 = jnp.zeros((HIDDEN,), jnp.float32)
        w2 = jax.random.normal(ks[5], (HIDDEN, R_DIM), dtype=jnp.float32) / sqrt(HIDDEN)
        b2 = jnp.zeros((R_DIM,), jnp.float32)
        return {'features': features, 'abs_distances': abs_distances, 'rel_vec': rel_vec, 'edge_index': edge_index, 'w1': w1, 'b1': b1, 'w2': w2, 'b2': b2}
    _L0_gnn_all = _L0_gnn_setup()
    _L0_gnn_in = {k: v for k, v in _L0_gnn_all.items() if k in ('w1', 'b1', 'w2', 'b2')}
    del _L0_gnn_all

    def _L1_gnn_setup():
        import jax, jax.numpy as jnp
        import numpy as np
        D = 3
        KS = 5
        K = KS ** D
        S = 2 ** D
        _COMBOS = np.array([[s >> d & 1 for d in range(D)] for s in range(S)], dtype=np.int32)
        _STRIDES = np.array([KS ** (D - 1 - d) for d in range(D)], dtype=np.int32)

        def spline_basis(pseudo):
            pos = pseudo * (KS - 1)
            i0 = jnp.clip(jnp.floor(pos), 0, KS - 2).astype(jnp.int32)
            frac = pos - i0
            combos = jnp.asarray(_COMBOS)
            basis = jnp.prod(jnp.where(combos[None] == 1, frac[:, None, :], 1.0 - frac[:, None, :]), axis=-1)
            idx = jnp.sum((i0[:, None, :] + combos[None]) * jnp.asarray(_STRIDES)[None, None, :], axis=-1)
            return (basis, idx)

        def spline_conv(x, row, col, basis, idx, W, b):
            N = x.shape[0]
            Fout = W.shape[2]
            z = jnp.einsum('ni,kio->nko', x, W).reshape(N * K, Fout)
            gathered = z[col[:, None] * K + idx]
            msg = jnp.einsum('es,eso->eo', basis, gathered)
            out = jax.ops.segment_sum(msg, row, num_segments=N)
            deg = jax.ops.segment_sum(jnp.ones_like(msg[:, 0]), row, num_segments=N)
            return out / jnp.maximum(deg, 1.0)[:, None] + b
        key = jax.random.key(seed)
        ks = jax.random.split(key, 13)
        N, E, Fin, Fout = (625, 10000, 32, 32)

        def u(k, shape, size):
            bound = 1.0 / np.sqrt(size)
            return jax.random.uniform(k, shape, jnp.float32, -bound, bound)
        return dict(x=jax.random.normal(ks[0], (N, Fin), jnp.float32), edge_index=jax.random.randint(ks[1], (2, E), 0, N, dtype=jnp.int32), pseudo=jax.random.uniform(ks[2], (E, D), jnp.float32), stn1_w=u(ks[3], (K, 1, 64), 1 * S), stn1_b=u(ks[4], (64,), 1 * S), stn2_w=u(ks[5], (K, 64, 64), 64 * S), stn2_b=u(ks[6], (64,), 64 * S), stn3_w=u(ks[7], (64, 64), 64), stn3_b=u(ks[8], (64,), 64), stn4_w=u(ks[9], (64, 3), 64), stn4_b=u(ks[10], (3,), 64), conv_w=u(ks[11], (K, Fin, Fout), Fin * S), conv_b=u(ks[12], (Fout,), Fin * S))
    _L1_gnn_all = _L1_gnn_setup()
    _L1_gnn_in = {k: v for k, v in _L1_gnn_all.items() if k in ('stn1_w', 'stn1_b', 'stn2_w', 'stn2_b', 'stn3_w', 'stn3_b', 'stn4_w', 'stn4_b', 'conv_w', 'conv_b')}
    del _L1_gnn_all

    def _L2_gnn_setup():
        import jax, jax.numpy as jnp
        import numpy as np
        N_NODES = 3125
        N_EDGES = 100000
        IN_CH = 32
        OUT_CH = 32
        DIM = 2
        KSIZE = 3

        def _basis(pseudo):
            p = jnp.clip(pseudo, 0.0, 1.0)
            grid = jnp.linspace(0.0, 1.0, KSIZE, dtype=p.dtype)
            dist = jnp.abs(p[:, :, None] - grid[None, None, :])
            b = jnp.maximum(1.0 - dist * (KSIZE - 1), 0.0)
            basis = jnp.einsum('ea,eb->eab', b[:, 0], b[:, 1])
            return basis.reshape(p.shape[0], -1)
        key = jax.random.key(seed)
        k1, k2, k3, k4, k5, k6 = jax.random.split(key, 6)
        x = jax.random.normal(k1, (N_NODES, IN_CH), dtype=jnp.float32)
        pseudo = jax.random.uniform(k2, (N_EDGES, DIM), dtype=jnp.float32)
        weight = jax.random.normal(k3, (KSIZE * KSIZE, IN_CH, OUT_CH), dtype=jnp.float32) / np.sqrt(IN_CH)
        root_w = jax.random.normal(k4, (OUT_CH, IN_CH), dtype=jnp.float32) / np.sqrt(IN_CH)
        root_b = jax.random.normal(k5, (OUT_CH,), dtype=jnp.float32) * 0.01
        edge_index = jax.random.randint(k6, (2, N_EDGES), 0, N_NODES, dtype=jnp.int64)
        return {'x': x, 'pseudo': pseudo, 'weight': weight, 'root_w': root_w, 'root_b': root_b, 'edge_index': edge_index}
    _L2_gnn_all = _L2_gnn_setup()
    _L2_gnn_in = {k: v for k, v in _L2_gnn_all.items() if k in ('weight', 'root_w', 'root_b')}
    del _L2_gnn_all

    def _L3_gnn_setup():
        import jax, jax.numpy as jnp
        import numpy as np
        N = 3125
        E = 50000
        D_IN = 32
        D_OUT = 32
        key = jax.random.key(seed)
        k0, k1, k2, k3 = jax.random.split(key, 4)
        x = jax.random.normal(k0, (N, D_IN), dtype=jnp.float32)
        mask = jax.random.randint(k1, (N, 1), 0, 2).astype(jnp.float32)
        edge_index = jax.random.randint(k2, (2, E), 0, N, dtype=jnp.int32)
        W = jax.random.normal(k3, (D_OUT, D_IN), dtype=jnp.float32) / np.sqrt(D_IN)
        b = jnp.zeros((D_OUT,), dtype=jnp.float32)
        return {'x': x, 'mask': mask, 'W': W, 'b': b, 'edge_index': edge_index}
    _L3_gnn_all = _L3_gnn_setup()
    _L3_gnn_in = {k: v for k, v in _L3_gnn_all.items() if k in ('W', 'b')}
    del _L3_gnn_all
    return {'x': x, 'src': src, 'dst': dst, 'edge_attr_2': edge_attr_2, 'edge_attr_3': edge_attr_3, 'edge_weight': edge_weight, 'node_vec1': node_vec1, 'L0_gnn_w1': _L0_gnn_in['w1'], 'L0_gnn_b1': _L0_gnn_in['b1'], 'L0_gnn_w2': _L0_gnn_in['w2'], 'L0_gnn_b2': _L0_gnn_in['b2'], 'L1_gnn_stn1_w': _L1_gnn_in['stn1_w'], 'L1_gnn_stn1_b': _L1_gnn_in['stn1_b'], 'L1_gnn_stn2_w': _L1_gnn_in['stn2_w'], 'L1_gnn_stn2_b': _L1_gnn_in['stn2_b'], 'L1_gnn_stn3_w': _L1_gnn_in['stn3_w'], 'L1_gnn_stn3_b': _L1_gnn_in['stn3_b'], 'L1_gnn_stn4_w': _L1_gnn_in['stn4_w'], 'L1_gnn_stn4_b': _L1_gnn_in['stn4_b'], 'L1_gnn_conv_w': _L1_gnn_in['conv_w'], 'L1_gnn_conv_b': _L1_gnn_in['conv_b'], 'L2_gnn_weight': _L2_gnn_in['weight'], 'L2_gnn_root_w': _L2_gnn_in['root_w'], 'L2_gnn_root_b': _L2_gnn_in['root_b'], 'L3_gnn_W': _L3_gnn_in['W'], 'L3_gnn_b': _L3_gnn_in['b']}

def reference(x, src, dst, edge_attr_2, edge_attr_3, edge_weight, node_vec1, L0_gnn_w1, L0_gnn_b1, L0_gnn_w2, L0_gnn_b2, L1_gnn_stn1_w, L1_gnn_stn1_b, L1_gnn_stn2_w, L1_gnn_stn2_b, L1_gnn_stn3_w, L1_gnn_stn3_b, L1_gnn_stn4_w, L1_gnn_stn4_b, L1_gnn_conv_w, L1_gnn_conv_b, L2_gnn_weight, L2_gnn_root_w, L2_gnn_root_b, L3_gnn_W, L3_gnn_b):
    import jax
    import jax.numpy as jnp

    def _L0_gnn_ref(features, abs_distances, rel_vec, edge_index, w1, b1, w2, b2):
        import jax, jax.numpy as jnp
        import numpy as np
        from math import factorial, pi, sqrt
        MUL = 8
        RS = [(MUL, 0), (MUL, 1)]
        N_NODES = 625
        N_EDGES = 20000
        FEAT_DIM = sum((m * (2 * l + 1) for m, l in RS))
        R_DIM = sum((mo * mi * (2 * min(lo, li) + 1) for mo, lo in RS for mi, li in RS))
        HIDDEN = 64

        def _cg(j1, j2, j3, m1, m2, m3):
            if m1 + m2 != m3:
                return 0.0
            f = factorial
            pre = sqrt((2 * j3 + 1) * f(j3 + j1 - j2) * f(j3 - j1 + j2) * f(j1 + j2 - j3) / f(j1 + j2 + j3 + 1))
            pre *= sqrt(f(j3 + m3) * f(j3 - m3) * f(j1 - m1) * f(j1 + m1) * f(j2 - m2) * f(j2 + m2))
            kmin = max(0, j2 - j3 - m1, j1 - j3 + m2)
            kmax = min(j1 + j2 - j3, j1 - m1, j2 + m2)
            s = 0.0
            for k in range(kmin, kmax + 1):
                s += (-1) ** k / (f(k) * f(j1 + j2 - j3 - k) * f(j1 - m1 - k) * f(j2 + m2 - k) * f(j3 - j2 + m1 + k) * f(j3 - j1 - m2 + k))
            return pre * s

        def _w3j_complex(l1, l2, l3):
            w = np.zeros((2 * l1 + 1, 2 * l2 + 1, 2 * l3 + 1))
            for m1 in range(-l1, l1 + 1):
                for m2 in range(-l2, l2 + 1):
                    m3 = -(m1 + m2)
                    if abs(m3) <= l3:
                        w[m1 + l1, m2 + l2, m3 + l3] = (-1) ** (l1 - l2 - m3) / sqrt(2 * l3 + 1) * _cg(l1, l2, l3, m1, m2, -m3)
            return w

        def _A(l):
            A = np.zeros((2 * l + 1, 2 * l + 1), dtype=complex)
            A[l, l] = 1.0
            for m in range(1, l + 1):
                A[l + m, l + m] = (-1) ** m / sqrt(2)
                A[l + m, l - m] = 1.0 / sqrt(2)
                A[l - m, l - m] = 1j / sqrt(2)
                A[l - m, l + m] = -1j * (-1) ** m / sqrt(2)
            return A

        def real_w3j(l1, l2, l3):
            wc = _w3j_complex(l1, l2, l3).astype(complex)
            wr = np.einsum('abc,ma,nb,oc->mno', wc, _A(l1).conj(), _A(l2).conj(), _A(l3).conj())
            i = int(np.argmax(np.abs(wr)))
            ph = wr.flat[i] / abs(wr.flat[i])
            wr = wr / ph
            assert np.abs(wr.imag).max() < 1e-10
            return np.real(wr).astype(np.float32)
        _W3J = {}
        for _mo, _lo in RS:
            for _mi, _li in RS:
                for _lf in range(abs(_lo - _li), _lo + _li + 1):
                    if (_lo, _lf, _li) not in _W3J:
                        _W3J[_lo, _lf, _li] = jnp.asarray(real_w3j(_lo, _lf, _li))
        _NORM = []
        for _mo, _lo in RS:
            _num = sum((mi * (2 * min(_lo, li) + 1) for mi, li in RS))
            _NORM.append(sqrt(4.0 * pi) * sqrt(2.0 * _lo + 1.0) / sqrt(_num))
        _F_OFFS = [0] + list(np.cumsum([mi * (2 * li + 1) for mi, li in RS]))

        def spherical_harmonics(rel_vec):
            r = rel_vec / jnp.linalg.norm(rel_vec, axis=-1, keepdims=True)
            x, y, z = (r[:, 0], r[:, 1], r[:, 2])
            y0 = jnp.full_like(x, 0.5 / sqrt(pi))[:, None]
            c1 = sqrt(3.0 / (4.0 * pi))
            y1 = c1 * jnp.stack([y, z, x], axis=-1)
            c2a = 0.5 * sqrt(15.0 / pi)
            c2b = 0.25 * sqrt(5.0 / pi)
            c2c = 0.25 * sqrt(15.0 / pi)
            y2 = jnp.stack([c2a * x * y, c2a * y * z, c2b * (3.0 * z * z - 1.0), c2a * x * z, c2c * (x * x - y * y)], axis=-1)
            return jnp.concatenate([y0, y1, y2], axis=-1)
        src, dst = (edge_index[0], edge_index[1])
        R = jax.nn.relu(abs_distances[:, None] @ w1 + b1) @ w2 + b2
        Y = spherical_harmonics(rel_vec)
        Fj = features[src]
        E = Fj.shape[0]
        msg_blocks = []
        r_off = 0
        for i, (mo, lo) in enumerate(RS):
            acc = jnp.zeros((E, mo, 2 * lo + 1), dtype=features.dtype)
            for j, (mi, li) in enumerate(RS):
                n_lf = 2 * min(lo, li) + 1
                sz = mo * mi * n_lf
                Rb = R[:, r_off:r_off + sz].reshape(E, mo, mi, n_lf)
                r_off += sz
                Fb = Fj[:, _F_OFFS[j]:_F_OFFS[j + 1]].reshape(E, mi, 2 * li + 1)
                for k, lf in enumerate(range(abs(lo - li), lo + li + 1)):
                    C = _W3J[lo, lf, li]
                    Yf = Y[:, lf * lf:(lf + 1) * (lf + 1)]
                    acc = acc + _NORM[i] * jnp.einsum('euv,ef,evi,ofi->euo', Rb[..., k], Yf, Fb, C)
            msg_blocks.append(acc.reshape(E, -1))
        msg = jnp.concatenate(msg_blocks, axis=-1)
        out = jnp.zeros((features.shape[0], msg.shape[1]), dtype=features.dtype)
        out = out.at[dst].add(msg)
        return out

    def _L1_gnn_ref(x, edge_index, pseudo, stn1_w, stn1_b, stn2_w, stn2_b, stn3_w, stn3_b, stn4_w, stn4_b, conv_w, conv_b):
        import jax, jax.numpy as jnp
        import numpy as np
        D = 3
        KS = 5
        K = KS ** D
        S = 2 ** D
        _COMBOS = np.array([[s >> d & 1 for d in range(D)] for s in range(S)], dtype=np.int32)
        _STRIDES = np.array([KS ** (D - 1 - d) for d in range(D)], dtype=np.int32)

        def spline_basis(pseudo):
            pos = pseudo * (KS - 1)
            i0 = jnp.clip(jnp.floor(pos), 0, KS - 2).astype(jnp.int32)
            frac = pos - i0
            combos = jnp.asarray(_COMBOS)
            basis = jnp.prod(jnp.where(combos[None] == 1, frac[:, None, :], 1.0 - frac[:, None, :]), axis=-1)
            idx = jnp.sum((i0[:, None, :] + combos[None]) * jnp.asarray(_STRIDES)[None, None, :], axis=-1)
            return (basis, idx)

        def spline_conv(x, row, col, basis, idx, W, b):
            N = x.shape[0]
            Fout = W.shape[2]
            z = jnp.einsum('ni,kio->nko', x, W).reshape(N * K, Fout)
            gathered = z[col[:, None] * K + idx]
            msg = jnp.einsum('es,eso->eo', basis, gathered)
            out = jax.ops.segment_sum(msg, row, num_segments=N)
            deg = jax.ops.segment_sum(jnp.ones_like(msg[:, 0]), row, num_segments=N)
            return out / jnp.maximum(deg, 1.0)[:, None] + b
        N = x.shape[0]
        row, col = (edge_index[0], edge_index[1])
        basis, idx = spline_basis(pseudo)
        h = jnp.ones((N, 1), x.dtype)
        h = jax.nn.elu(spline_conv(h, row, col, basis, idx, stn1_w, stn1_b))
        h = jax.nn.elu(spline_conv(h, row, col, basis, idx, stn2_w, stn2_b))
        h = jax.nn.elu(h @ stn3_w + stn3_b)
        t = h @ stn4_w + stn4_b
        new_pseudo = jnp.clip(pseudo + t[col] - t[row], 0.0, 1.0)
        basis2, idx2 = spline_basis(new_pseudo)
        return spline_conv(x, row, col, basis2, idx2, conv_w, conv_b)

    def _L2_gnn_ref(x, pseudo, weight, root_w, root_b, edge_index):
        import jax, jax.numpy as jnp
        import numpy as np
        N_NODES = 3125
        N_EDGES = 100000
        IN_CH = 32
        OUT_CH = 32
        DIM = 2
        KSIZE = 3

        def _basis(pseudo):
            p = jnp.clip(pseudo, 0.0, 1.0)
            grid = jnp.linspace(0.0, 1.0, KSIZE, dtype=p.dtype)
            dist = jnp.abs(p[:, :, None] - grid[None, None, :])
            b = jnp.maximum(1.0 - dist * (KSIZE - 1), 0.0)
            basis = jnp.einsum('ea,eb->eab', b[:, 0], b[:, 1])
            return basis.reshape(p.shape[0], -1)
        row, col = (edge_index[0], edge_index[1])
        basis = _basis(pseudo)
        messages = jnp.einsum('ek,ei,kio->eo', basis, x[row], weight)
        out = jnp.zeros((x.shape[0], weight.shape[2]), dtype=x.dtype).at[col].add(messages)
        degree = jnp.zeros((x.shape[0],), dtype=x.dtype).at[col].add(jnp.ones_like(col, dtype=x.dtype))
        out = out / jnp.maximum(degree, 1.0)[:, None]
        out = out + x @ root_w.T + root_b
        return out

    def _L3_gnn_ref(x, mask, W, b, edge_index):
        import jax, jax.numpy as jnp
        import numpy as np
        N = 3125
        E = 50000
        D_IN = 32
        D_OUT = 32
        row, col = (edge_index[0], edge_index[1])
        n = x.shape[0]
        x = jnp.nan_to_num(x)
        deg = jax.ops.segment_sum(jnp.ones(row.shape[0], x.dtype), row, num_segments=n)
        dis = jnp.where(deg > 0, jax.lax.rsqrt(deg), 0.0)
        w = dis[row] * dis[col]

        def spmm(v):
            return jax.ops.segment_sum(w[:, None] * v[col], row, num_segments=n)
        numerator = spmm(jnp.ones_like(x)) * spmm(mask * x)
        denominator = spmm(mask)
        den_safe = jnp.where(denominator == 0, 1.0, denominator)
        ratio = jnp.where(denominator == 0, 0.0, numerator / den_safe)
        return ratio @ W.T + b
    edge_index = jnp.stack([src, dst])
    h = jnp.maximum(_layernorm(x, axis=-1), 0.0)
    x = x + _L0_gnn_ref(h, edge_weight, edge_attr_3, edge_index, L0_gnn_w1, L0_gnn_b1, L0_gnn_w2, L0_gnn_b2)
    h = jnp.maximum(_layernorm(x, axis=-1), 0.0)
    x = x + _L1_gnn_ref(h, edge_index, edge_attr_3, L1_gnn_stn1_w, L1_gnn_stn1_b, L1_gnn_stn2_w, L1_gnn_stn2_b, L1_gnn_stn3_w, L1_gnn_stn3_b, L1_gnn_stn4_w, L1_gnn_stn4_b, L1_gnn_conv_w, L1_gnn_conv_b)
    h = jnp.maximum(_layernorm(x, axis=-1), 0.0)
    x = x + _L2_gnn_ref(h, edge_attr_2, L2_gnn_weight, L2_gnn_root_w, L2_gnn_root_b, edge_index)
    h = jnp.maximum(_layernorm(x, axis=-1), 0.0)
    x = x + _L3_gnn_ref(h, node_vec1, L3_gnn_W, L3_gnn_b, edge_index)
    return x

_drawn_inputs = setup_inputs


def setup_inputs(seed=0):
    import zlib

    import numpy as np

    out = dict(_drawn_inputs(seed))
    spreads = {'L0_gnn_b1': (0.0, 0.1), 'L0_gnn_b2': (0.0, 0.1), 'L3_gnn_b': (0.0, 0.345)}
    factors = {'edge_attr_2': 3.172,
     'node_vec1': 32.691,
     'L1_gnn_stn1_w': 4.754,
     'L1_gnn_stn1_b': 53.981,
     'L1_gnn_stn2_w': 4.973,
     'L1_gnn_stn2_b': 64.0,
     'L1_gnn_stn3_w': 4.449,
     'L1_gnn_stn3_b': 64.0,
     'L1_gnn_stn4_w': 3.829,
     'L1_gnn_stn4_b': 8.0,
     'L1_gnn_conv_w': 3.135,
     'L1_gnn_conv_b': 6.016,
     'L2_gnn_root_b': 22.729}
    for name, (base, spread) in spreads.items():
        noise = np.random.default_rng([zlib.crc32(name.encode()), seed]).standard_normal(out[name].shape)
        drawn = base * np.exp(spread * noise) if base else spread * noise
        out[name] = jnp.asarray(drawn.astype(out[name].dtype))
    for name, factor in factors.items():
        out[name] = (out[name] * factor).astype(out[name].dtype)
    return out
```

```python
from contextlib import ExitStack
from math import pi, sqrt

import concourse.bass as bass
from concourse import mybir

F32 = mybir.dt.float32
BF16 = mybir.dt.bfloat16
FP16 = mybir.dt.float16
I32 = mybir.dt.int32
ALU = mybir.AluOpType
ACT = mybir.ActivationFunctionType
AX = mybir.AxisListType

P = 125
N = 3125
E = 100000
T = E // P
NT = N // P
C = 32
G = 4
NG = T // G
PAIRS = NG // 2
QW = 782
HW = QW // 2
NP4 = 4 * QW
KN = 125
LB = 100
NB = T // LB

NORM0 = sqrt(4 * pi) / sqrt(16.0)
NORM1 = sqrt(4 * pi) * sqrt(3.0) / sqrt(32.0)
Y0 = 0.5 / sqrt(pi)
C1 = sqrt(3.0 / (4.0 * pi))
PATH_00 = NORM0 * Y0
PATH_01 = NORM0 * C1 / sqrt(3.0)
PATH_10 = NORM1 * C1 / sqrt(3.0)
PATH_11_0 = NORM1 * Y0 / sqrt(3.0)
PATH_11_1 = NORM1 * C1 / sqrt(6.0)
PATH_11_2 = NORM1 * 0.5 * sqrt(15.0 / pi) / sqrt(10.0)


def build(nc, A, out):
    with ExitStack() as ctx:
        def sb(name, shape, dt=F32):
            return ctx.enter_context(nc.sbuf_tensor(name, shape, dt))

        def sem(name):
            return ctx.enter_context(nc.semaphore(name))

        def dram(name, shape, dt=F32):
            return nc.dram_tensor(name, shape, dt, kind="Internal").ap()

        h0_tab = dram("h0_tab", (N, C))
        z2_tab = dram("z2_tab", (N * KN, 64))
        z3_tab = dram("z3_tab", (N * KN, 32))
        t_tab = dram("t_tab", (N, 3))
        zl2_tab = dram("zl2_tab", (N, 288))
        y3_tab = dram("y3_tab", (N, 34))

        X = sb("X", [P, NT, C])
        H = sb("H", [P, NT, C])
        srcf = sb("srcf", [P, T])
        dstf = sb("dstf", [P, T])
        src_q, src_r = sb("src_q", [P, T]), sb("src_r", [P, T])
        dst_q, dst_r = sb("dst_q", [P, T]), sb("dst_r", [P, T])
        idx2 = sb("idx2", [P, T, 2], I32)
        idx1s = sb("idx1s", [P, T], I32)
        idx1d = sb("idx1d", [P, T], I32)
        att3 = sb("att3", [P, T, 3])
        basis = sb("basis", [P, T * 9])
        unit = basis[:, 0:T * 5].rearrange("p (t k) -> p t k", k=5)
        basis8 = basis[:, 0:T * 8].rearrange("p (t k) -> p t k", k=8)
        basis9 = basis[:, :].rearrange("p (t k) -> p t k", k=9)
        ident = sb("ident", [128, 128])
        iota_i = sb("iota_i", [P, QW], I32)
        iota_h = sb("iota_h", [P, QW], FP16)
        quads_i = sb("quads_i", [P, G, 4, C], I32)
        quads = sb("quads", [P, G, 4, C])
        zeros = sb("zeros", [P, 392], BF16)
        nodeT = sb("nodeT", [65, NP4])
        rdegT = sb("rdegT", [64, NP4])
        deg_s = sb("deg_s", [P, NT])
        deg_d = sb("deg_d", [P, NT])
        small = sb("small", [128, 4 * C * NT])
        st1, st2, st3 = sb("st1", [P, NT]), sb("st2", [P, NT]), sb("st3", [P, NT])
        wbias = sb("wbias", [64, 4])
        WORK = 19900
        work = sb("work", [128, WORK])

        ps = ctx.enter_context(nc.psum_tensor("ps", [128, 8, 512], F32))

        at = [0]

        def carve(parts, shape, dt=F32):
            n = 1
            for d in shape:
                n *= d
            words = n if dt in (F32, I32) else (n + 1) // 2
            a = work[0:parts, at[0]:at[0] + words]
            at[0] += words
            assert at[0] <= WORK, at[0]
            if dt != F32:
                a = a.bitcast(dt)
            if len(shape) > 1:
                names = "abcde"[:len(shape)]
                a = a.rearrange("p (%s) -> p %s" % (" ".join(names), " ".join(names)),
                                **{k: d for k, d in zip(names, shape)})
            return a

        def bc(ap, shape):
            return ap.broadcast_to(shape)

        at[0] = 0
        stage_i = carve(LB, [2, NB, P], I32)
        stage_f = carve(LB, [2, NB, P])
        stage3 = carve(LB, [NB, P * 3])
        with nc.Block() as block:
            s = {k: sem("set_" + k) for k in ("load", "index", "const", "float", "turned", "copied", "quad", "step", "unit")}

            @block.sync
            def _(sp):
                for k, a in enumerate(("src", "dst")):
                    sp.dma_start(stage_i[:, k], A[a].rearrange("(b r p) -> r b p", r=LB, p=P)).then_inc(s["index"], 16)
                sp.dma_start(stage3, A["edge_attr_3"].rearrange("(b r p) c -> r b (p c)", r=LB, p=P)).then_inc(s["load"], 16)
                sp.dma_start(X[:, :, :], A["x"].rearrange("(j p) c -> p j c", p=P)).then_inc(s["load"], 16)
                for k, a in enumerate(("L1_gnn_stn1_b", "L1_gnn_stn2_b", "L1_gnn_stn3_b")):
                    sp.dma_start(wbias[:, k:k + 1], A[a].rearrange("(n a) -> n a", a=1)).then_inc(s["load"], 16)
                sp.wait_ge(s["load"], 80)

            @block.gpsimd
            def _(gp):
                gp.iota(iota_i[:, :], [[1, QW]], base=0, channel_multiplier=0).then_inc(s["const"], 1)
                gp.iota(quads_i[:, :, :, :], [[0, G], [1, 4], [0, C]], base=0, channel_multiplier=0).then_inc(s["const"], 1)
                gp.memset(ident[:, :], 0.0).then_inc(s["const"], 1)
                gp.wait_ge(s["const"], 3)
                gp.affine_select(out=ident[:, :], in_=ident[:, :], compare_op=ALU.not_equal, fill=1.0,
                                 base=0, pattern=[[-1, 128]], channel_multiplier=1).then_inc(s["const"], 1)

            @block.tensor
            def _(pe):
                pe.wait_ge(s["const"], 4)
                pe.wait_ge(s["float"], 1)
                for k in range(5):
                    if k == 2:
                        pe.wait_ge(s["load"], 80)
                    if k >= 4:
                        pe.wait_ge(s["copied"], k - 3)
                    for b in range(NB):
                        src = stage_f[:, k, b, :] if k < 2 else stage3[:, b, k - 2::3]
                        mm = pe.transpose(ps[0:P, 2 * (k % 4) + b // 4, (b % 4) * LB:(b % 4 + 1) * LB], src, ident[0:LB, 0:LB])
                    mm.then_inc(s["turned"], 1)

            @block.vector
            def _(v):
                v.wait_ge(s["index"], 32)
                v.tensor_copy(stage_f, stage_i).then_inc(s["float"], 1)
                v.wait_ge(s["const"], 4)
                v.tensor_copy(iota_h[:, :], iota_i[:, :])
                v.tensor_copy(quads[:, :, :, :], quads_i[:, :, :, :])
                v.memset(zeros[:, :], 0.0)
                for k in range(5):
                    v.wait_ge(s["turned"], k + 1)
                    src = ps[0:P, 2 * (k % 4):2 * (k % 4) + 2, 0:4 * LB]
                    to = (srcf[:, :], dstf[:, :], att3[:, :, 0], att3[:, :, 1], att3[:, :, 2])[k]
                    v.tensor_copy(to.rearrange("p (a b) -> p a b", a=2), src).then_inc(s["copied"], 1)
                v.wait_ge(s["copied"], 5)
                n = 0
                for f, q, r, i in ((srcf, src_q, src_r, idx1s), (dstf, dst_q, dst_r, idx1d)):
                    v.tensor_copy(i[:, :], f[:, :])
                    v.tensor_scalar(q[:, :], f[:, :], float(QW), None, ALU.is_ge).then_inc(s["quad"], 1)
                    for m in (2, 3):
                        n += 1
                        v.wait_ge(s["quad"], n)
                        v.scalar_tensor_tensor(q[:, :], f[:, :], float(m * QW), q[:, :], ALU.is_ge, ALU.add).then_inc(s["quad"], 1)
                    n += 1
                    v.wait_ge(s["quad"], n)
                    v.scalar_tensor_tensor(r[:, :], q[:, :], -float(QW), f[:, :], ALU.mult, ALU.add)

        def layer_norm(name):
            s = sem(name + "_steps")
            r = sem(name + "_root")
            sq = small[0:P, 0:NT * C].rearrange("p (j c) -> p j c", c=C)

            def vec(v):
                v.tensor_reduce(st1[:, :], X[:, :, :], AX.X, ALU.add).then_inc(s, 1)
                v.wait_ge(s, 1)
                v.tensor_scalar(st2[:, :], st1[:, :], 1.0 / C, None, ALU.mult).then_inc(s, 1)
                v.wait_ge(s, 2)
                v.tensor_tensor(H[:, :, :], X[:, :, :], bc(st2[:, :, None], [P, NT, C]), ALU.subtract).then_inc(s, 1)
                v.wait_ge(s, 3)
                v.tensor_tensor(sq, H[:, :, :], H[:, :, :], ALU.mult).then_inc(s, 1)
                v.wait_ge(s, 4)
                v.tensor_reduce(st1[:, :], sq, AX.X, ALU.add).then_inc(s, 1)
                v.wait_ge(s, 5)
                v.tensor_scalar(st1[:, :], st1[:, :], 1.0 / C, 1e-5, ALU.mult, ALU.add).then_inc(s, 1)
                v.wait_ge(r, 1)
                v.reciprocal(st3[:, :], st2[:, :]).then_inc(s, 1)
                v.wait_ge(s, 7)
                v.tensor_tensor(H[:, :, :], H[:, :, :], bc(st3[:, :, None], [P, NT, C]), ALU.mult).then_inc(s, 1)
                v.wait_ge(s, 8)
                v.tensor_scalar(H[:, :, :], H[:, :, :], 0.0, None, ALU.max).then_inc(s, 1)

            def sca(a):
                a.wait_ge(s, 6)
                a.activation(st2[:, :], st1[:, :], ACT.Sqrt).then_inc(r, 1)

            return s, vec, sca

        def spline_weights(v, s, base, pseudo, with_node, spline_tmp):
            cnt = [base]

            def done(ins):
                ins.then_inc(s, 1)
                cnt[0] += 1
                v.wait_ge(s, cnt[0])

            pos, i0, fr, b01, kn = spline_tmp
            done(v.tensor_scalar(pos, pseudo, 4.0, None, ALU.mult))
            done(v.tensor_scalar(i0, pos, 1.0, None, ALU.is_ge))
            for m in (2.0, 3.0):
                done(v.scalar_tensor_tensor(i0, pos, m, i0, ALU.is_ge, ALU.add))
            done(v.tensor_tensor(fr[:, :, :, 1], pos, i0, ALU.subtract))
            done(v.tensor_scalar(fr[:, :, :, 0], fr[:, :, :, 1], -1.0, 1.0, ALU.mult, ALU.add))
            done(v.tensor_tensor(b01, bc(fr[:, :, 0, :, None], [P, T, 2, 2]), bc(fr[:, :, 1, None, :], [P, T, 2, 2]), ALU.mult))
            bas8 = basis8.rearrange("p t (a b) -> p t a b", b=2)
            for d in range(2):
                done(v.tensor_tensor(bas8[:, :, :, d], b01.rearrange("p t a b -> p t (a b)"),
                                     bc(fr[:, :, 2, d:d + 1], [P, T, 4]), ALU.mult))
            done(v.scalar_tensor_tensor(kn, i0[:, :, 0], 5.0, i0[:, :, 1], ALU.mult, ALU.add))
            done(v.scalar_tensor_tensor(kn, kn, 5.0, i0[:, :, 2], ALU.mult, ALU.add))
            if with_node:
                done(v.scalar_tensor_tensor(kn, dstf[:, :], float(KN), kn, ALU.mult, ALU.add))
            done(v.tensor_copy(idx2[:, :, 0], kn))
            done(v.tensor_scalar(idx2[:, :, 1], kn, 25.0, None, ALU.add))
            return cnt[0]

        def two_step(eng, first, second):
            if first is None:
                with eng.Fori(0, PAIRS) as i:
                    for x in range(2):
                        second(x, i)
                return
            first(eng, 0, 0)
            with eng.Fori(0, PAIRS - 1) as i:
                first(eng, 1, i)
                second(0, i)
                first(eng, 0, i + 1)
                second(1, i)
            first(eng, 1, PAIRS - 1)
            second(0, PAIRS - 1)
            second(1, PAIRS - 1)

        edge_sems = {k: sem("edge_" + k) for k in ["window", "products"] + [
            f"{k}{x}" for k in ("message", "high", "residual", "middle", "low", "quads", "ready", "scattered",
                                "hidden", "radial", "radial_used") for x in (0, 1)]}

        def zero_edge_sems(sp):
            for k in edge_sems.values():
                sp.sem_clear(k)

        def edge_phase(name, table, idx, ng, run, F, extra, quad, rest, more):
            at[0] = keep
            U = F // 32
            FM = F + (2 if extra == "pair" else 0)
            NPASS = 3 * U + (1 if extra == "pair" else 0)
            gbuf = carve(P, [2, G * ng, run])
            win = carve(P, [2, G * ng], I32)
            prod = carve(P, [max(1, ng) * G * (8 if ng == 2 else 9) // ng, F]) if ng * run > 64 else None
            msg = carve(P, [2, G, FM])
            res = carve(P, [G, FM])
            part = carve(P, [2, 3, G, FM], BF16)
            stat = carve(P, [2, NPASS, G, 128], BF16)
            ohq = carve(P, [2, G, 128], BF16)
            ohr = carve(P, [2, G, QW], BF16)
            nacc = U + (1 if extra else 0)
            s = dict(edge_sems)
            for x in range(2):
                s[f"gathered{x}"] = sem(f"{name}_gathered{x}")
            env = dict(gbuf=gbuf, prod=prod, F=F, ng=ng, msg=msg, s=s, name=name)
            more(env)
            with nc.Block() as block:
                @block.gpsimd
                def _(gp):
                    def gather(x, i):
                        gp.tensor_copy(win[:, x, :], idx[:, bass.ds((2 * i + x) * (G * ng), G * ng)]).then_inc(s["window"], 1)
                        gp.wait_ge(s["window"], 2 * i + (x + 1))
                        gp.nop(nofuse=True)
                        for k in range(G * ng):
                            gp.indirect_dma_start(gbuf[:, x, k, :], None, table, bass.IndirectOffsetOnAxis(
                                ap=win[:, x, k:k + 1], axis=0)).then_inc(s[f"gathered{x}"], 16)

                    for x in range(2):
                        gather(x, 0)
                    with gp.Fori(1, PAIRS) as i:
                        for x in range(2):
                            gp.wait_ge(s[f"message{x}"], i)
                            gather(x, i)

                @block.vector
                def _(v):
                    if "v_begin" in env:
                        env["v_begin"](v)
                    if extra == "pair":
                        v.memset(stat[:, :, 3 * U, :, :], 0.0)
                    with v.Fori(0, PAIRS) as i:
                        for x in range(2):
                            g = 2 * i + x
                            env["message"](v, env, x, i, g)
                            v.wait_ge(s[f"scattered{x}"], i + 1)
                            v.tensor_tensor(ohq[:, x].rearrange("p g (q c) -> p g q c", c=C), quads[:, :, :, :],
                                            bc(quad[:, bass.ds(g * G, G)][:, :, None, None], [P, G, 4, C]),
                                            ALU.is_equal).then_inc(s[f"quads{x}"], 1)
                            for k in range(G):
                                v.tensor_scalar(ohr[:, x, k, :], iota_h[:, :], rest[:, bass.ds(g * G + k, 1)], None, ALU.is_equal)
                            v.wait_ge(s[f"high{x}"], i + 1)
                            v.tensor_tensor(res, msg[:, x], part[:, x, 0], ALU.subtract).then_inc(s[f"residual{x}"], 1)
                            v.wait_ge(s[f"quads{x}"], i + 1)

                            def spread(k, last=False):
                                for u in range(U):
                                    o = v.tensor_tensor(
                                        stat[:, x, 3 * u + k].rearrange("p g (q c) -> p g q c", c=C),
                                        ohq[:, x].rearrange("p g (q c) -> p g q c", c=C),
                                        bc(part[:, x, k, :, None, 32 * u:32 * u + 32], [P, G, 4, C]), ALU.mult)
                                if extra == "pair":
                                    o = v.tensor_tensor(
                                        stat[:, x, 3 * U].rearrange("p g (q c) -> p g q c", c=C)[:, :, :, 2 * k:2 * k + 2],
                                        ohq[:, x].rearrange("p g (q c) -> p g q c", c=C)[:, :, :, 0:2],
                                        bc(part[:, x, k, :, None, F:F + 2], [P, G, 4, 2]), ALU.mult)
                                if last:
                                    o.then_inc(s[f"ready{x}"], 1)

                            spread(0)
                            v.wait_ge(s[f"middle{x}"], i + 1)
                            v.tensor_tensor(part[:, x, 2], res, part[:, x, 1], ALU.subtract).then_inc(s[f"low{x}"], 1)
                            spread(1)
                            v.wait_ge(s[f"low{x}"], i + 1)
                            spread(2, last=True)

                @block.scalar
                def _(a):
                    def round_parts(x, i):
                        a.wait_ge(s[f"message{x}"], i + 1)
                        a.activation(part[:, x, 0], msg[:, x], ACT.Copy).then_inc(s[f"high{x}"], 1)
                        a.wait_ge(s[f"residual{x}"], i + 1)
                        a.activation(part[:, x, 1], res, ACT.Copy).then_inc(s[f"middle{x}"], 1)

                    two_step(a, env.get("a_first"), round_parts)

                @block.tensor
                def _(pe):
                    def scatter(x, i):
                        pe.wait_ge(s[f"ready{x}"], i + 1)
                        for k in range(G):
                            jobs = [(p // 3, stat[:, x, p, k, :]) for p in range(3 * U)]
                            if extra == "pair":
                                jobs.append((U, stat[:, x, 3 * U, k, :]))
                            if extra == "ones":
                                jobs.append((U, ohq[:, x, k, :]))
                            for u, w in jobs:
                                for h in range(2):
                                    mm = pe.matmul(ps[:, 2 * u + h, 0:HW], w, ohr[:, x, k, h * HW:(h + 1) * HW],
                                                   start=False, stop=False, skip_group_check=True)
                        mm.then_inc(s[f"scattered{x}"], 1)

                    for b in range(2 * nacc):
                        mm = pe.matmul(ps[:, b, 0:HW], zeros[:, 0:128], zeros[:, 0:HW], start=True, stop=False, skip_group_check=True)
                        if b < 2:
                            mm.then_inc(s[f"scattered{b}"], 1)
                    two_step(pe, env.get("pe_first"), scatter)
                    for b in range(2 * nacc):
                        pe.matmul(ps[:, b, 0:HW], zeros[:, 0:128], zeros[:, 0:HW], start=False, stop=True, skip_group_check=True)

                if "sp" in env:
                    @block.sync
                    def _(sp):
                        env["sp"](sp)

        def unit_to_rows(eng, bank, dst, row):
            for q in range(4):
                for h in range(2):
                    c0 = q * QW + h * HW
                    o = eng(dst[row:row + 32, c0:c0 + HW], ps[32 * q:32 * q + 32, bank + h, 0:HW])
            return o

        def turn_to_nodes(pe, table, bank):
            for j in range(NT):
                mm = pe.transpose(ps[0:P, bank + j // 16, (j % 16) * 32:(j % 16) * 32 + 32], table[0:32, j * P:(j + 1) * P],
                                  ident[0:32, 0:32])
            return mm

        def nodes_of(bank):
            return ps[0:P, bank:bank + 2, :].rearrange("p b (j c) -> p (b j) c", c=32)[:, 0:NT, :]

        def turn_to_features(pe, nodes):
            for j in range(NT):
                mm = pe.transpose(ps[0:32, j // 4, (j % 4) * P:(j % 4 + 1) * P], nodes[:, j, :], ident[0:P, 0:P])
            return mm

        def copy_features(v, dst):
            v.tensor_copy(dst[0:32, 0:24 * P].rearrange("p (b n) -> p b n", b=6), ps[0:32, 0:6, 0:4 * P])
            return v.tensor_copy(dst[0:32, 24 * P:N], ps[0:32, 6, 0:P])

        at[0] = 0
        w2mix = carve(65, [384])
        w1c = carve(64, [2])
        hid = carve(65, [2, G * P])
        wrow = carve(64, [2, G * P])
        keep = at[0]
        w2all = carve(65, [384])
        norm2, square = carve(P, [T]), carve(P, [T])
        with nc.Block() as block:
            ns, vec_norm, sca_norm = layer_norm("norm0")
            s = {k: sem("l0_" + k) for k in ("weights", "unit", "root", "store", "mix")}

            @block.sync
            def _(sp):
                sp.dma_start(w2all[0:64, :], A["L0_gnn_w2"]).then_inc(s["weights"], 16)
                sp.dma_start(w2all[64:65, :], A["L0_gnn_b2"].rearrange("(a n) -> a n", a=1)).then_inc(s["weights"], 16)
                sp.dma_start(w1c[:, 0:1], A["L0_gnn_w1"].rearrange("a n -> n a")).then_inc(s["weights"], 16)
                sp.dma_start(w1c[:, 1:2], A["L0_gnn_b1"].rearrange("(n a) -> n a", a=1)).then_inc(s["weights"], 16)
                sp.wait_ge(ns, 9)
                sp.dma_start(h0_tab.rearrange("(j p) c -> p j c", p=P), H[:, :, :]).then_inc(s["store"], 16)
                sp.wait_ge(s["store"], 16)

            @block.scalar
            def _(a):
                sca_norm(a)
                a.wait_ge(s["unit"], 5)
                a.activation(square, norm2, ACT.Sqrt).then_inc(s["root"], 1)

            @block.vector
            def _(v):
                vec_norm(v)
                v.memset(hid[64:65, :, :], 1.0)
                n = 0
                v.tensor_tensor(norm2, att3[:, :, 0], att3[:, :, 0], ALU.mult).then_inc(s["unit"], 1)
                for k in (1, 2):
                    n += 1
                    v.wait_ge(s["unit"], n)
                    v.tensor_tensor(square, att3[:, :, k], att3[:, :, k], ALU.mult).then_inc(s["unit"], 1)
                    n += 1
                    v.wait_ge(s["unit"], n)
                    v.tensor_tensor(norm2, norm2, square, ALU.add).then_inc(s["unit"], 1)
                v.wait_ge(s["root"], 1)
                v.reciprocal(norm2, square).then_inc(s["unit"], 1)
                v.wait_ge(s["unit"], 6)
                for to, k in enumerate((1, 2, 0, 1, 2)):
                    v.tensor_tensor(unit[:, :, to], att3[:, :, k], norm2, ALU.mult)
                v.wait_ge(s["weights"], 64)
                w01 = w2all[:, 0:192].rearrange("h (b u w) -> h b u w", b=3, u=8)
                w11 = w2all[:, 192:384].rearrange("h (u w k) -> h u w k", u=8, k=3)
                m1 = w2mix[:, 0:256].rearrange("h (r u x w) -> h r u x w", r=2, u=8, x=2)
                m2 = w2mix[:, 256:384].rearrange("h (r u w) -> h r u w", r=2, u=8)
                v.tensor_scalar(m1[:, 0, :, 0, :], w01[:, 0], PATH_00, None, ALU.mult)
                v.tensor_scalar(m1[:, 0, :, 1, :], w01[:, 1], PATH_01, None, ALU.mult)
                v.tensor_scalar(m1[:, 1, :, 0, :], w01[:, 2], PATH_10, None, ALU.mult)
                v.tensor_scalar(m1[:, 1, :, 1, :], w11[:, :, :, 2], PATH_11_2, None, ALU.mult)
                v.tensor_scalar(m2[:, 1], w11[:, :, :, 1], PATH_11_1, None, ALU.mult)
                v.tensor_scalar(m2[:, 0], w11[:, :, :, 2], -PATH_11_2 / 3.0, None, ALU.mult).then_inc(s["mix"], 1)
                v.wait_ge(s["mix"], 1)
                v.scalar_tensor_tensor(m2[:, 0], w11[:, :, :, 0], PATH_11_0, m2[:, 0], ALU.mult, ALU.add)

        def layer0(env):
            s, name = env["s"], env["name"]
            x16 = carve(P, [G, 16])
            dots = carve(P, [G, 8, 3])
            prod1 = carve(P, [G, 16, 16])
            prod2 = carve(P, [G, 16, 3, 8])
            red = carve(P, [G, 64])
            hx = carve(P, [G, 8, 5])
            c1, c2, c3 = carve(P, [G, 8, 3]), carve(P, [G, 8, 3]), carve(P, [G, 8, 3])
            for x in range(2):
                s[f"weight_row{x}"] = sem(f"weight_row{x}")
            we = A["edge_weight"].rearrange("(a n) -> a n", a=1)

            def sp_prog(sp):
                for x in range(2):
                    sp.dma_start(wrow[:, x, :], we[:, x * G * P:(x + 1) * G * P].broadcast_to([64, G * P])
                                 ).then_inc(s[f"weight_row{x}"], 16)
                with sp.Fori(1, PAIRS) as i:
                    for x in range(2):
                        sp.wait_ge(s[f"hidden{x}"], i)
                        sp.nop(nofuse=True)
                        sp.dma_start(wrow[:, x, :], we[:, bass.ds((2 * i + x) * (G * P), G * P)].broadcast_to([64, G * P])
                                     ).then_inc(s[f"weight_row{x}"], 16)

            def hidden(a, x, i):
                a.wait_ge(s[f"weight_row{x}"], 16 * i + 16)
                a.wait_ge(s[f"radial{x}"], 2 * i + 2)
                a.activation(hid[0:64, x, :], wrow[:, x, :], ACT.Relu, bias=w1c[:, 1:2], scale=w1c[:, 0:1]
                             ).then_inc(s[f"hidden{x}"], 1)

            def radial(pe, x, i):
                pe.wait_ge(s[f"hidden{x}"], i + 1)
                for half in range(2):
                    pe.wait_ge(s[f"radial_used{half}"], 2 * i + (x + 1))
                    for k in (2 * half, 2 * half + 1):
                        mm = pe.matmul(ps[0:P, 4 + k, 0:384], hid[:, x, k * P:(k + 1) * P], w2mix, start=True, stop=True,
                                       skip_group_check=True)
                    mm.then_inc(s[f"radial{x}"], 1)

            def v_begin(v):
                for x in range(2):
                    v.sem_inc(s[f"radial{x}"], 2)
                    v.sem_inc(s[f"radial_used{x}"], 1)

            def message(v, env, x, i, g):
                n = [0]
                per = 6

                def done(ins):
                    ins.then_inc(s["products"], 1)
                    n[0] += 1
                    v.wait_ge(s["products"], g * per + n[0])

                rows = env["gbuf"][:, x]
                f1 = rows[:, :, 8:32].rearrange("p g (w o) -> p g w o", o=3)
                r = unit[:, bass.ds(g * G, G), :]
                v.wait_ge(s[f"gathered{x}"], 16 * G * i + 16 * G)
                v.tensor_copy(x16[:, :, 0:8], rows[:, :, 0:8])
                done(v.tensor_tensor(dots, f1, bc(r[:, :, None, 0:3], [P, G, 8, 3]), ALU.mult))
                done(v.tensor_reduce(x16[:, :, 8:16], dots, AX.X, ALU.add))
                for half in range(2):
                    t2 = slice(2 * half, 2 * half + 2)
                    v.wait_ge(s[f"radial{x}"], 2 * i + (3 + half))
                    rad = ps[0:P, 4 + 2 * half:6 + 2 * half, :]
                    for t in range(2):
                        k = 2 * half + t
                        v.tensor_tensor(prod1[:, k], rad[:, t, 0:256].rearrange("p (r c) -> p r c", c=16),
                                        bc(x16[:, k, None, :], [P, 16, 16]), ALU.mult)
                        o = v.tensor_tensor(prod2[:, k], bc(rad[:, t, 256:384].rearrange("p (r c) -> p r c", c=8)[:, :, None, :],
                                                            [P, 16, 3, 8]),
                                            bc(f1[:, k].rearrange("p w o -> p o w")[:, None, :, :], [P, 16, 3, 8]), ALU.mult)
                    o.then_inc(s[f"radial_used{half}"], 1)
                for half in range(2):
                    v.wait_ge(s[f"radial_used{half}"], g + 2)
                v.tensor_reduce(red[:, :, 0:16], prod1, AX.X, ALU.add)
                done(v.tensor_reduce(red[:, :, 16:64], prod2.rearrange("p g r o w -> p g (r o) w"), AX.X, ALU.add))
                gu = red[:, :, 16:40].rearrange("p g (u o) -> p g u o", o=3)
                hu = red[:, :, 40:64].rearrange("p g (u o) -> p g u o", o=3)
                qu = red[:, :, 8:16]
                v.tensor_copy(env["msg"][:, x, :, 0:8], red[:, :, 0:8])
                v.tensor_copy(hx[:, :, :, 0:3], hu)
                v.tensor_tensor(c3, bc(qu[:, :, :, None], [P, G, 8, 3]), bc(r[:, :, None, 0:3], [P, G, 8, 3]), ALU.mult)
                done(v.tensor_copy(hx[:, :, :, 3:5], hu[:, :, :, 0:2]))
                v.tensor_tensor(c1, bc(r[:, :, None, 1:4], [P, G, 8, 3]), hx[:, :, :, 2:5], ALU.mult)
                done(v.tensor_tensor(c2, bc(r[:, :, None, 2:5], [P, G, 8, 3]), hx[:, :, :, 1:4], ALU.mult))
                v.tensor_tensor(c3, c3, gu, ALU.add)
                done(v.tensor_tensor(c1, c1, c2, ALU.subtract))
                v.tensor_tensor(env["msg"][:, x, :, 8:32].rearrange("p g (u o) -> p g u o", o=3), c1, c3, ALU.add
                                ).then_inc(s[f"message{x}"], 1)
                v.wait_ge(s[f"message{x}"], i + 1)
                assert n[0] == per

            env.update(sp=sp_prog, a_first=hidden, v_begin=v_begin, pe_first=radial, message=message)

        edge_phase("e0", h0_tab, idx1s[:, :], 1, C, 32, "ones", dst_q, dst_r, layer0)

        at[0] = 0
        spline_tmp = (carve(P, [T, 3]), carve(P, [T, 3]), carve(P, [T, 3, 2]), carve(P, [T, 2, 2]), carve(P, [T]))
        with nc.Block() as block:
            s = {k: sem("n0_" + k) for k in ("sum", "deg", "turned", "spline")}

            @block.sync
            def _(sp):
                zero_edge_sems(sp)

            @block.scalar
            def _(a):
                unit_to_rows(lambda o, i: a.activation(o, i, ACT.Copy), 0, nodeT, 0).then_inc(s["sum"], 1)

            @block.tensor
            def _(pe):
                pe.wait_ge(s["sum"], 1)
                turn_to_nodes(pe, nodeT, 4).then_inc(s["turned"], 1)
                pe.wait_ge(s["deg"], 1)
                turn_to_nodes(pe, rdegT, 6).then_inc(s["turned"], 1)

            @block.vector
            def _(v):
                unit_to_rows(lambda o, i: v.tensor_copy(o, i), 2, rdegT, 0).then_inc(s["deg"], 1)
                v.wait_ge(s["turned"], 2)
                v.tensor_tensor(X[:, :, :], X[:, :, :], nodes_of(4), ALU.add)
                v.tensor_copy(deg_d[:, :], nodes_of(6)[:, :, 0])
                spline_weights(v, s["spline"], 0, att3[:, :, :], False, spline_tmp)

        def spline_conv(env):
            name, prod, gbuf, msg, F = env["name"], env["prod"], env["gbuf"], env["msg"], env["F"]
            s = env["s"]

            def message(v, env, x, i, g):
                rows = gbuf[:, x].rearrange("p (g k) n -> p (g k) n", k=2)
                weights = basis8[:, bass.ds(g * G, G), :].rearrange("p g (a b c) -> p (g a) b c", b=2, c=2)
                terms = prod.rearrange("p (a b c) f -> p a b c f", b=2, c=2)
                v.wait_ge(s[f"gathered{x}"], 2 * 16 * G * i + 2 * 16 * G)
                for d1 in range(2):
                    o = v.tensor_tensor(terms[:, :, d1], rows[:, :, 5 * F * d1:5 * F * d1 + 2 * F].rearrange("p a (c f) -> p a c f", c=2),
                                        bc(weights[:, :, d1, :, None], [P, 2 * G, 2, F]), ALU.mult)
                o.then_inc(s["products"], 1)
                v.wait_ge(s["products"], g + 1)
                v.tensor_reduce(msg[:, x], prod.rearrange("p (g k) f -> p g f k", k=8), AX.X, ALU.add).then_inc(s[f"message{x}"], 1)

            env["message"] = message

        def elu(s, table, rows, bias):
            low = small[0:rows, 0:NP4]

            def sca(a, start):
                a.wait_ge(s, start)
                a.activation(table[0:rows, :], table[0:rows, :], ACT.Identity, bias=bias).then_inc(s, 1)
                a.wait_ge(s, start + 2)
                a.activation(low, low, ACT.Exp).then_inc(s, 1)

            def vec(v, start):
                v.wait_ge(s, start + 1)
                v.tensor_scalar(low, table[0:rows, :], 0.0, None, ALU.min).then_inc(s, 1)
                v.wait_ge(s, start + 3)
                v.tensor_scalar(table[0:rows, :], table[0:rows, :], 0.0, None, ALU.max).then_inc(s, 1)
                v.wait_ge(s, start + 4)
                v.scalar_tensor_tensor(table[0:rows, :], low, -1.0, table[0:rows, :], ALU.add, ALU.add).then_inc(s, 1)

            return sca, vec

        keep = 0
        edge_phase("e1", A["L1_gnn_stn1_w"].rearrange("k a o -> k (a o)"), idx2[:, :, :].rearrange("p t k -> p (t k)"),
                   2, 7 * 64, 64, "ones", src_q, src_r, spline_conv)

        with nc.Block() as block:
            s = {k: sem("n1_" + k) for k in ("sum0", "sum1", "turned", "elu")}
            elu_a, elu_v = elu(s["elu"], nodeT, 64, wbias[:, 0:1])

            @block.sync
            def _(sp):
                zero_edge_sems(sp)

            @block.scalar
            def _(a):
                unit_to_rows(lambda o, i: a.activation(o, i, ACT.Copy), 0, nodeT, 0)
                unit_to_rows(lambda o, i: a.activation(o, i, ACT.Copy), 4, rdegT, 0).then_inc(s["sum0"], 1)
                elu_a(a, 1)

            @block.tensor
            def _(pe):
                pe.wait_ge(s["sum0"], 1)
                turn_to_nodes(pe, rdegT, 6).then_inc(s["turned"], 1)

            @block.vector
            def _(v):
                unit_to_rows(lambda o, i: v.tensor_copy(o, i), 2, nodeT, 32)
                v.wait_ge(s["sum0"], 1)
                v.tensor_copy(rdegT[32:64, :], rdegT[0:32, :]).then_inc(s["sum1"], 1)
                v.wait_ge(s["turned"], 1)
                v.wait_ge(s["sum1"], 1)
                v.tensor_copy(deg_s[:, :], nodes_of(6)[:, :, 0])
                v.tensor_scalar(rdegT[:, :], rdegT[:, :], 1.0, None, ALU.max).then_inc(s["sum1"], 1)
                v.wait_ge(s["sum1"], 2)
                v.reciprocal(rdegT[:, :], rdegT[:, :]).then_inc(s["sum1"], 1)
                v.wait_ge(s["sum1"], 3)
                v.tensor_tensor(nodeT[0:64, :], nodeT[0:64, :], rdegT[:, :], ALU.mult).then_inc(s["elu"], 1)
                elu_v(v, 1)

        def table_block(name, F, weight, z_tab, more_v=None):
            COLS = 500
            per = KN * F // COLS // 2
            half = per // 2
            at[0] = 0
            wbig = carve(F, [KN * F])
            zst = carve(P, [2, per * COLS])
            hj = carve(F, [P])
            z = z_tab.rearrange("(n k) o -> n (k o)", k=KN)
            with nc.Block() as block:
                s = {k: sem(name + "_" + k) for k in ("weight", "tile", "product", "out_a", "out_v", "stored0", "stored1")}

                @block.sync
                def _(sp):
                    sp.dma_start(wbig.rearrange("i (k o) -> i k o", k=KN), weight.rearrange("k i o -> i k o")).then_inc(s["weight"], 16)
                    with sp.Fori(0, NT) as j:
                        for h in range(2):
                            sp.wait_ge(s["out_a"], j * per + (4 + (h + 1) * half))
                            sp.wait_ge(s["out_v"], j * per + (4 + (h + 1) * half))
                            sp.nop(nofuse=True)
                            sp.dma_start(z[bass.ds(j * P, P), h * per * COLS:(h + 1) * per * COLS], zst[:, h, :]
                                         ).then_inc(s[f"stored{h}"], 16)
                    for h in range(2):
                        sp.wait_ge(s[f"stored{h}"], 16 * NT)

                @block.tensor
                def _(pe):
                    for e in ("out_a", "out_v"):
                        pe.sem_inc(s[e], 4)
                    pe.wait_ge(s["weight"], 16)
                    with pe.Fori(0, NT) as j:
                        pe.wait_ge(s["tile"], j + 1)
                        for h in range(2):
                            for c in range(per):
                                pe.wait_ge(s["out_v" if c % 2 else "out_a"], j * per + (h * half + c // 2 + 1))
                                pe.matmul(ps[0:P, (h * per + c) % 8, 0:COLS], hj,
                                          wbig[:, (h * per + c) * COLS:(h * per + c + 1) * COLS], start=True, stop=True,
                                          skip_group_check=True).then_inc(s["product"], 1)

                def copy_out(eng, copy, mine, done, j, first):
                    for h in range(2):
                        if not first:
                            eng.wait_ge(s[f"stored{h}"], 16 * j)
                        for c in range(mine, per, 2):
                            eng.wait_ge(s["product"], j * (2 * per) + (h * per + c + 1))
                            copy(zst[:, h, c * COLS:(c + 1) * COLS], ps[0:P, (h * per + c) % 8, 0:COLS]).then_inc(s[done], 1)

                @block.scalar
                def _(a):
                    copy = lambda o, i: a.activation(o, i, ACT.Copy)
                    copy(hj, nodeT[0:F, 0:P]).then_inc(s["tile"], 1)
                    copy_out(a, copy, 0, "out_a", 0, True)
                    with a.Fori(1, NT) as j:
                        a.wait_ge(s["product"], j * (2 * per))
                        copy(hj, nodeT[0:F, bass.ds(j * P, P)]).then_inc(s["tile"], 1)
                        copy_out(a, copy, 0, "out_a", j, False)

                @block.vector
                def _(v):
                    if more_v:
                        more_v(v)
                    copy = lambda o, i: v.tensor_copy(o, i)
                    copy_out(v, copy, 1, "out_v", 0, True)
                    with v.Fori(1, NT) as j:
                        copy_out(v, copy, 1, "out_v", j, False)

        def add_node(v):
            for k in range(2):
                v.scalar_tensor_tensor(idx2[:, :, k], dstf[:, :], float(KN), idx2[:, :, k], ALU.mult, ALU.add)

        table_block("z2", 64, A["L1_gnn_stn2_w"], z2_tab, add_node)
        keep = 0
        edge_phase("e2", z2_tab, idx2[:, :, :].rearrange("p t k -> p (t k)"), 2, 7 * 64, 64, None, src_q, src_r, spline_conv)

        at[0] = 0
        w3, w4, h3 = carve(64, [64]), carve(65, [3]), carve(65, [NP4])
        tn = carve(P, [NT, 3])
        with nc.Block() as block:
            s = {k: sem("n2_" + k) for k in ("load", "sum0", "sum1", "elu", "h3", "product", "ones", "t", "tn", "stored")}
            elu_a, elu_v = elu(s["elu"], nodeT, 64, wbias[:, 1:2])
            elu3_a, elu3_v = elu(s["h3"], h3, 64, wbias[:, 2:3])

            @block.sync
            def _(sp):
                zero_edge_sems(sp)
                sp.dma_start(w3, A["L1_gnn_stn3_w"]).then_inc(s["load"], 16)
                sp.dma_start(w4[0:64, :], A["L1_gnn_stn4_w"]).then_inc(s["load"], 16)
                sp.dma_start(w4[64:65, :], A["L1_gnn_stn4_b"].rearrange("(a n) -> a n", a=1)).then_inc(s["load"], 16)
                sp.wait_ge(s["tn"], 1)
                sp.dma_start(t_tab.rearrange("(j p) c -> p j c", p=P), tn).then_inc(s["stored"], 16)
                sp.wait_ge(s["stored"], 16)

            @block.scalar
            def _(a):
                unit_to_rows(lambda o, i: a.activation(o, i, ACT.Copy), 0, nodeT, 0).then_inc(s["sum0"], 1)
                elu_a(a, 1)
                a.wait_ge(s["product"], 1)
                a.activation(h3[0:64, :].rearrange("p (b n) -> p b n", b=8), ps[0:64, :, 0:HW], ACT.Copy).then_inc(s["h3"], 1)
                elu3_a(a, 1)

            @block.tensor
            def _(pe):
                pe.wait_ge(s["load"], 48)
                pe.wait_ge(s["elu"], 6)
                for b in range(8):
                    mm = pe.matmul(ps[0:64, b, 0:HW], w3, nodeT[0:64, b * HW:(b + 1) * HW], start=True, stop=True)
                mm.then_inc(s["product"], 1)
                pe.wait_ge(s["ones"], 1)
                pe.wait_ge(s["h3"], 6)
                for j in range(NT):
                    mm = pe.matmul(ps[0:P, 0, 3 * j:3 * j + 3], h3[:, j * P:(j + 1) * P], w4, start=True, stop=True)
                mm.then_inc(s["t"], 1)

            @block.vector
            def _(v):
                v.memset(h3[64:65, :], 1.0).then_inc(s["ones"], 1)
                unit_to_rows(lambda o, i: v.tensor_copy(o, i), 2, nodeT, 32).then_inc(s["sum1"], 1)
                v.wait_ge(s["sum0"], 1)
                v.wait_ge(s["sum1"], 1)
                v.tensor_tensor(nodeT[0:64, :], nodeT[0:64, :], rdegT[:, :], ALU.mult).then_inc(s["elu"], 1)
                elu_v(v, 1)
                elu3_v(v, 1)
                v.wait_ge(s["t"], 1)
                v.tensor_copy(tn, ps[0:P, 0, 0:3 * NT].rearrange("p (j c) -> p j c", c=3)).then_inc(s["tn"], 1)

        at[0] = 0
        both = carve(P, [T, 2], I32)
        win = carve(P, [2, 2 * G], I32)
        tg = carve(P, [2, 2 * G, 3])
        with nc.Block() as block:
            s = {k: sem("t_" + k) for k in ("both", "window", "gathered0", "gathered1", "plus", "used0", "used1")}

            @block.gpsimd
            def _(gp):
                idx = both.rearrange("p t k -> p (t k)")

                def gather(x, i):
                    gp.tensor_copy(win[:, x, :], idx[:, bass.ds((2 * i + x) * (2 * G), 2 * G)]).then_inc(s["window"], 1)
                    gp.wait_ge(s["window"], 2 * i + (x + 1))
                    gp.nop(nofuse=True)
                    for k in range(2 * G):
                        gp.indirect_dma_start(tg[:, x, k, :], None, t_tab, bass.IndirectOffsetOnAxis(
                            ap=win[:, x, k:k + 1], axis=0)).then_inc(s[f"gathered{x}"], 16)

                gp.wait_ge(s["both"], 1)
                for x in range(2):
                    gather(x, 0)
                with gp.Fori(1, PAIRS) as i:
                    for x in range(2):
                        gp.wait_ge(s[f"used{x}"], i)
                        gather(x, i)

            @block.vector
            def _(v):
                v.tensor_copy(both[:, :, 0], dstf[:, :])
                v.tensor_copy(both[:, :, 1], srcf[:, :]).then_inc(s["both"], 1)
                with v.Fori(0, PAIRS) as i:
                    for x in range(2):
                        g = 2 * i + x
                        t = tg[:, x].rearrange("p (g k) c -> p g k c", k=2)
                        a3 = att3[:, bass.ds(g * G, G), :]
                        v.wait_ge(s[f"gathered{x}"], 32 * G * i + 32 * G)
                        v.tensor_tensor(a3, a3, t[:, :, 0], ALU.add).then_inc(s["plus"], 1)
                        v.wait_ge(s["plus"], g + 1)
                        v.tensor_tensor(a3, a3, t[:, :, 1], ALU.subtract).then_inc(s[f"used{x}"], 1)
                for x in range(2):
                    v.wait_ge(s[f"used{x}"], PAIRS)
                v.tensor_scalar(att3[:, :, :], att3[:, :, :], 0.0, 1.0, ALU.max, ALU.min)

        at[0] = 0
        spline_tmp = (carve(P, [T, 3]), carve(P, [T, 3]), carve(P, [T, 3, 2]), carve(P, [T, 2, 2]), carve(P, [T]))
        with nc.Block() as block:
            ns, vec_norm, sca_norm = layer_norm("norm1")
            s = {k: sem("n3_" + k) for k in ("spline", "turned")}

            @block.scalar
            def _(a):
                sca_norm(a)

            @block.tensor
            def _(pe):
                pe.wait_ge(ns, 9)
                turn_to_features(pe, H).then_inc(s["turned"], 1)

            @block.vector
            def _(v):
                vec_norm(v)
                spline_weights(v, s["spline"], 0, att3[:, :, :], True, spline_tmp)
                v.wait_ge(s["turned"], 1)
                copy_features(v, nodeT)

        table_block("z3", 32, A["L1_gnn_conv_w"], z3_tab)
        keep = 0
        edge_phase("e3", z3_tab, idx2[:, :, :].rearrange("p t k -> p (t k)"), 2, 7 * 32, 32, None, src_q, src_r, spline_conv)

        at[0] = 0
        cb = carve(P, [C])
        wl2 = carve(33, [320])
        zl = carve(P, [NT, 288])
        root = carve(P, [NT, C])
        stage2 = carve(LB, [NB, P * 2])
        att2 = carve(P, [T, 2])
        hats = carve(P, [T, 2, 3])
        with nc.Block() as block:
            ns, vec_norm, sca_norm = layer_norm("norm2")
            s = {k: sem("n4_" + k) for k in ("load", "sum", "mean", "turned", "added", "features", "product", "copied",
                                              "stored", "att", "att_in", "hat")}

            @block.sync
            def _(sp):
                zero_edge_sems(sp)
                sp.dma_start(stage2, A["edge_attr_2"].rearrange("(b r p) c -> r b (p c)", r=LB, p=P)).then_inc(s["load"], 16)
                sp.dma_start(cb, A["L1_gnn_conv_b"].rearrange("(a n) -> a n", a=1).broadcast_to([P, C])).then_inc(s["load"], 16)
                sp.dma_start(wl2[0:32, 0:288].rearrange("i (k o) -> i k o", k=9), A["L2_gnn_weight"].rearrange("k i o -> i k o")
                             ).then_inc(s["load"], 16)
                sp.dma_start(wl2[0:32, 288:320], A["L2_gnn_root_w"]).then_inc(s["load"], 16)
                sp.dma_start(wl2[32:33, 288:320], A["L2_gnn_root_b"].rearrange("(a n) -> a n", a=1)).then_inc(s["load"], 16)
                sp.wait_ge(s["copied"], NT)
                sp.dma_start(zl2_tab.rearrange("(j p) c -> p j c", p=P), zl).then_inc(s["stored"], 16)
                sp.wait_ge(s["stored"], 16)

            @block.scalar
            def _(a):
                unit_to_rows(lambda o, i: a.activation(o, i, ACT.Copy), 0, nodeT, 0).then_inc(s["sum"], 1)
                sca_norm(a)

            @block.tensor
            def _(pe):
                pe.wait_ge(s["mean"], 1)
                turn_to_nodes(pe, nodeT, 4).then_inc(s["turned"], 1)
                pe.wait_ge(ns, 9)
                turn_to_features(pe, H).then_inc(s["turned"], 1)
                pe.wait_ge(s["features"], 1)
                pe.wait_ge(s["load"], 80)
                for j in range(NT):
                    if j >= 8:
                        pe.wait_ge(s["copied"], j - 7)
                    pe.matmul(ps[0:P, j % 8, 0:320], nodeT[0:33, j * P:(j + 1) * P], wl2, start=True, stop=True).then_inc(s["product"], 1)
                pe.wait_ge(s["copied"], NT)
                for k in range(2):
                    for b in range(NB):
                        mm = pe.transpose(ps[0:P, 2 * k + b // 4, (b % 4) * LB:(b % 4 + 1) * LB], stage2[:, b, k::2], ident[0:LB, 0:LB])
                    mm.then_inc(s["att"], 1)

            @block.vector
            def _(v):
                v.wait_ge(s["sum"], 1)
                v.tensor_tensor(nodeT[0:32, :], nodeT[0:32, :], rdegT[0:32, :], ALU.mult).then_inc(s["mean"], 1)
                v.wait_ge(s["load"], 80)
                v.tensor_tensor(X[:, :, :], X[:, :, :], bc(cb[:, None, :], [P, NT, C]), ALU.add).then_inc(s["added"], 1)
                v.wait_ge(s["added"], 1)
                v.wait_ge(s["turned"], 1)
                v.tensor_tensor(X[:, :, :], X[:, :, :], nodes_of(4), ALU.add).then_inc(s["added"], 1)
                v.wait_ge(s["added"], 2)
                vec_norm(v)
                v.memset(wl2[32:33, 0:288], 0.0)
                v.memset(nodeT[32:33, :], 1.0)
                v.wait_ge(s["turned"], 2)
                copy_features(v, nodeT).then_inc(s["features"], 1)
                for j in range(NT):
                    v.wait_ge(s["product"], j + 1)
                    v.tensor_copy(root[:, j, :], ps[0:P, j % 8, 288:320])
                    v.tensor_copy(zl[:, j, :], ps[0:P, j % 8, 0:288]).then_inc(s["copied"], 1)
                for k in range(2):
                    v.wait_ge(s["att"], k + 1)
                    v.tensor_copy(att2[:, :, k].rearrange("p (a b) -> p a b", a=2), ps[0:P, 2 * k:2 * k + 2, 0:4 * LB]).then_inc(s["att_in"], 1)
                v.wait_ge(s["att_in"], 2)
                v.tensor_scalar(att2, att2, 0.0, 1.0, ALU.max, ALU.min).then_inc(s["hat"], 1)
                v.wait_ge(s["hat"], 1)
                for k in range(3):
                    o = v.tensor_scalar(hats[:, :, :, k], att2, -0.5 * k, 2.0, ALU.add, ALU.mult)
                o.then_inc(s["hat"], 1)
                v.wait_ge(s["hat"], 2)
                v.scalar_tensor_tensor(hats, hats, -1.0, hats, ALU.mult, ALU.max).then_inc(s["hat"], 1)
                v.wait_ge(s["hat"], 3)
                v.tensor_scalar(hats, hats, -1.0, 1.0, ALU.mult, ALU.add).then_inc(s["hat"], 1)
                v.wait_ge(s["hat"], 4)
                v.tensor_scalar(hats, hats, 0.0, None, ALU.max).then_inc(s["hat"], 1)
                v.wait_ge(s["hat"], 5)
                for k in range(3):
                    v.tensor_tensor(basis9[:, :, 3 * k:3 * k + 3], hats[:, :, 1], bc(hats[:, :, 0, k:k + 1], [P, T, 3]), ALU.mult)
                v.tensor_copy(H[:, :, :], root)

        def nine_kernels(env):
            prod, gbuf, msg, s = env["prod"], env["gbuf"], env["msg"], env["s"]

            def message(v, env, x, i, g):
                weights = basis9[:, bass.ds(g * G, G), :].rearrange("p g k -> p (g k)")
                v.wait_ge(s[f"gathered{x}"], 16 * G * i + 16 * G)
                v.tensor_tensor(prod, gbuf[:, x].rearrange("p g (k f) -> p (g k) f", k=9), bc(weights[:, :, None], [P, G * 9, C]),
                                ALU.mult).then_inc(s["products"], 1)
                v.wait_ge(s["products"], g + 1)
                v.tensor_reduce(msg[:, x], prod.rearrange("p (g k) f -> p g f k", k=9), AX.X, ALU.add).then_inc(s[f"message{x}"], 1)

            env["message"] = message

        edge_phase("e4", zl2_tab, idx1s[:, :], 1, 288, 32, None, dst_q, dst_r, nine_kernels)

        at[0] = 0
        mask = carve(P, [NT])
        dis, dis_m, rd = carve(P, [NT]), carve(P, [NT]), carve(P, [NT])
        y3 = carve(P, [NT, 34])
        with nc.Block() as block:
            ns, vec_norm, sca_norm = layer_norm("norm3")
            s = {k: sem("n5_" + k) for k in ("load", "sum", "turned", "rd", "root", "dis", "added", "guard", "table", "stored")}

            @block.sync
            def _(sp):
                zero_edge_sems(sp)
                sp.dma_start(mask, A["node_vec1"]).then_inc(s["load"], 16)
                sp.wait_ge(s["table"], 1)
                sp.dma_start(y3_tab.rearrange("(j p) c -> p j c", p=P), y3).then_inc(s["stored"], 16)
                sp.wait_ge(s["stored"], 16)

            @block.scalar
            def _(a):
                unit_to_rows(lambda o, i: a.activation(o, i, ACT.Copy), 0, nodeT, 0).then_inc(s["sum"], 1)
                a.wait_ge(s["dis"], 1)
                a.activation(dis_m, dis, ACT.Sqrt).then_inc(s["root"], 1)
                sca_norm(a)

            @block.tensor
            def _(pe):
                pe.wait_ge(s["sum"], 1)
                turn_to_nodes(pe, nodeT, 4).then_inc(s["turned"], 1)

            @block.vector
            def _(v):
                v.tensor_scalar(dis, deg_s[:, :], 1.0, None, ALU.max).then_inc(s["dis"], 1)
                v.tensor_scalar(rd, deg_d[:, :], 1.0, None, ALU.max).then_inc(s["rd"], 1)
                v.tensor_tensor(X[:, :, :], X[:, :, :], H[:, :, :], ALU.add).then_inc(s["added"], 1)
                v.wait_ge(s["rd"], 1)
                v.reciprocal(rd, rd).then_inc(s["rd"], 1)
                v.wait_ge(s["root"], 1)
                v.reciprocal(dis, dis_m).then_inc(s["dis"], 1)
                v.wait_ge(s["dis"], 2)
                v.scalar_tensor_tensor(dis, deg_s[:, :], 0.0, dis, ALU.is_gt, ALU.mult).then_inc(s["dis"], 1)
                v.wait_ge(s["dis"], 3)
                v.wait_ge(s["load"], 16)
                v.tensor_tensor(dis_m, dis, mask, ALU.mult).then_inc(s["dis"], 1)
                v.wait_ge(s["rd"], 2)
                v.wait_ge(s["turned"], 1)
                v.tensor_tensor(H[:, :, :], nodes_of(4), bc(rd[:, :, None], [P, NT, C]), ALU.mult).then_inc(s["added"], 1)
                v.wait_ge(s["added"], 2)
                v.tensor_tensor(X[:, :, :], X[:, :, :], H[:, :, :], ALU.add).then_inc(s["added"], 1)
                v.wait_ge(s["added"], 3)
                vec_norm(v)
                v.wait_ge(ns, 9)
                big = 3.4028234663852886e38
                v.tensor_scalar(H[:, :, :], H[:, :, :], -big, big, ALU.max, ALU.min).then_inc(s["guard"], 1)
                v.wait_ge(s["guard"], 1)
                v.wait_ge(s["dis"], 4)
                v.tensor_copy(y3[:, :, 32], dis)
                v.tensor_copy(y3[:, :, 33], dis_m)
                v.tensor_tensor(y3[:, :, 0:32], H[:, :, :], bc(dis_m[:, :, None], [P, NT, C]), ALU.mult).then_inc(s["table"], 1)

        def plain(env):
            def message(v, env, x, i, g):
                v.wait_ge(env["s"][f"gathered{x}"], 16 * G * i + 16 * G)
                v.tensor_copy(env["msg"][:, x], env["gbuf"][:, x]).then_inc(env["s"][f"message{x}"], 1)

            env["message"] = message

        edge_phase("e5", y3_tab, idx1d[:, :], 1, 34, 32, "pair", src_q, src_r, plain)

        at[0] = 0
        dis2, dis_2, num, den, zero = (carve(P, [NT]) for _ in range(5))
        wl3, b3 = carve(32, [C]), carve(P, [C])
        res = carve(P, [NT, C])
        with nc.Block() as block:
            s = {k: sem("n6_" + k) for k in ("load", "sum", "pair", "turned", "step", "root", "ratio", "features", "product",
                                              "out", "stored")}

            @block.sync
            def _(sp):
                sp.dma_start(wl3, A["L3_gnn_W"]).then_inc(s["load"], 16)
                sp.dma_start(b3, A["L3_gnn_b"].rearrange("(a n) -> a n", a=1).broadcast_to([P, C])).then_inc(s["load"], 16)
                sp.wait_ge(s["out"], 3)
                sp.dma_start(out.rearrange("(j p) c -> p j c", p=P), X[:, :, :]).then_inc(s["stored"], 16)
                sp.wait_ge(s["stored"], 16)

            @block.scalar
            def _(a):
                unit_to_rows(lambda o, i: a.activation(o, i, ACT.Copy), 0, nodeT, 0).then_inc(s["sum"], 1)
                a.wait_ge(s["step"], 1)
                a.activation(dis_2, dis2, ACT.Sqrt).then_inc(s["root"], 1)

            @block.tensor
            def _(pe):
                pe.wait_ge(s["sum"], 1)
                turn_to_nodes(pe, nodeT, 4).then_inc(s["turned"], 1)
                pe.wait_ge(s["pair"], 1)
                turn_to_nodes(pe, rdegT, 6).then_inc(s["turned"], 1)
                pe.wait_ge(s["ratio"], 1)
                turn_to_features(pe, H).then_inc(s["turned"], 1)
                pe.wait_ge(s["features"], 1)
                pe.wait_ge(s["load"], 32)
                for j in range(NT):
                    mm = pe.matmul(ps[0:P, j // 16, (j % 16) * 32:(j % 16) * 32 + 32], nodeT[0:32, j * P:(j + 1) * P], wl3,
                                   start=True, stop=True)
                mm.then_inc(s["product"], 1)

            @block.vector
            def _(v):
                n = [0]

                def done(ins):
                    ins.then_inc(s["step"], 1)
                    n[0] += 1
                    v.wait_ge(s["step"], n[0])

                unit_to_rows(lambda o, i: v.tensor_copy(o, i), 2, rdegT, 0).then_inc(s["pair"], 1)
                done(v.tensor_scalar(dis2, deg_s[:, :], 1.0, None, ALU.max))
                v.wait_ge(s["root"], 1)
                done(v.reciprocal(dis2, dis_2))
                done(v.scalar_tensor_tensor(dis2, deg_s[:, :], 0.0, dis2, ALU.is_gt, ALU.mult))
                v.wait_ge(s["turned"], 2)
                pair = nodes_of(6)
                done(v.tensor_reduce(num, pair[:, :, 0:6:2], AX.X, ALU.add))
                done(v.tensor_reduce(den, pair[:, :, 1:6:2], AX.X, ALU.add))
                done(v.tensor_tensor(num, num, dis2, ALU.mult))
                done(v.tensor_tensor(den, den, dis2, ALU.mult))
                done(v.tensor_scalar(zero, den, 0.0, None, ALU.is_equal))
                done(v.tensor_tensor(den, den, zero, ALU.add))
                done(v.reciprocal(den, den))
                done(v.tensor_tensor(H[:, :, :], nodes_of(4), bc(dis2[:, :, None], [P, NT, C]), ALU.mult))
                done(v.tensor_tensor(H[:, :, :], H[:, :, :], bc(num[:, :, None], [P, NT, C]), ALU.mult))
                done(v.tensor_tensor(H[:, :, :], H[:, :, :], bc(den[:, :, None], [P, NT, C]), ALU.mult))
                done(v.tensor_scalar(zero, zero, -1.0, 1.0, ALU.mult, ALU.add))
                v.tensor_tensor(H[:, :, :], H[:, :, :], bc(zero[:, :, None], [P, NT, C]), ALU.mult).then_inc(s["ratio"], 1)
                v.wait_ge(s["turned"], 3)
                copy_features(v, nodeT).then_inc(s["features"], 1)
                v.wait_ge(s["load"], 32)
                v.tensor_tensor(X[:, :, :], X[:, :, :], bc(b3[:, None, :], [P, NT, C]), ALU.add).then_inc(s["out"], 1)
                v.wait_ge(s["product"], 1)
                v.wait_ge(s["out"], 1)
                v.tensor_tensor(X[:, :, :], X[:, :, :], nodes_of(0), ALU.add).then_inc(s["out"], 2)


NAMES = ["x", "src", "dst", "edge_attr_2", "edge_attr_3", "edge_weight", "node_vec1", "L0_gnn_w1", "L0_gnn_b1", "L0_gnn_w2",
         "L0_gnn_b2", "L1_gnn_stn1_w", "L1_gnn_stn1_b", "L1_gnn_stn2_w", "L1_gnn_stn2_b", "L1_gnn_stn3_w", "L1_gnn_stn3_b",
         "L1_gnn_stn4_w", "L1_gnn_stn4_b", "L1_gnn_conv_w", "L1_gnn_conv_b", "L2_gnn_weight", "L2_gnn_root_w", "L2_gnn_root_b",
         "L3_gnn_W", "L3_gnn_b"]


def kernel(**inputs):
    import numpy as _np
    import concourse.bacc as _bacc
    from concourse import mybir as _mybir
    from concourse.bass_utils import run_bass_kernel_spmd as _run

    nc = _bacc.Bacc("TRN2", target_bir_lowering=False, num_devices=1)
    arrays, tensors = {}, {}
    for name in NAMES:
        a = inputs[name]
        if name in ("L2_gnn_root_w", "L3_gnn_W"):
            a = _np.asarray(a).T
        if name == "node_vec1":
            a = _np.asarray(a).reshape(NT, P).T
        a = _np.ascontiguousarray(a)
        arrays[f"in_{name}"] = a
        tensors[name] = nc.dram_tensor(f"in_{name}", a.shape, _mybir.dt.from_np(a.dtype), kind="ExternalInput").ap()
    out = nc.dram_tensor("out_0", (N, C), _mybir.dt.float32, kind="ExternalOutput").ap()
    build(nc, tensors, out)
    r = _run(nc, [arrays], core_ids=[0])
    return r.results[0]["out_0"]
```

```python
from contextlib import ExitStack
from math import pi, sqrt

import concourse.bass as bass
from concourse import mybir

F32 = mybir.dt.float32
BF16 = mybir.dt.bfloat16
FP16 = mybir.dt.float16
I32 = mybir.dt.int32
ALU = mybir.AluOpType
ACT = mybir.ActivationFunctionType
AX = mybir.AxisListType

P = 125
N = 3125
E = 100000
T = E // P
NT = N // P
C = 32
GMAX = 8
QW = 782
HW = QW // 2
NP4 = 4 * QW
KN = 125
KR = 100
LB = 100
NB = T // LB

NORM0 = sqrt(4 * pi) / sqrt(16.0)
NORM1 = sqrt(4 * pi) * sqrt(3.0) / sqrt(32.0)
Y0 = 0.5 / sqrt(pi)
C1 = sqrt(3.0 / (4.0 * pi))
PATH_00 = NORM0 * Y0
PATH_01 = NORM0 * C1 / sqrt(3.0)
PATH_10 = NORM1 * C1 / sqrt(3.0)
PATH_11_0 = NORM1 * Y0 / sqrt(3.0)
PATH_11_1 = NORM1 * C1 / sqrt(6.0)
PATH_11_2 = NORM1 * 0.5 * sqrt(15.0 / pi) / sqrt(10.0)


def build(nc, A, out):
    with ExitStack() as ctx:
        def sb(name, shape, dt=F32):
            return ctx.enter_context(nc.sbuf_tensor(name, shape, dt))

        def sem(name):
            return ctx.enter_context(nc.semaphore(name))

        def dram(name, shape, dt=F32):
            return nc.dram_tensor(name, shape, dt, kind="Internal").ap()

        h0_tab = dram("h0_tab", (N, C))
        z2_tab = dram("z2_tab", (N * KR, 128))
        z3_tab = dram("z3_tab", (N * KR, 64))
        t_tab = dram("t_tab", (N, 3))
        zl2_tab = dram("zl2_tab", (N, 288))
        y3_tab = dram("y3_tab", (N, 34))

        X = sb("X", [P, NT, C])
        H = sb("H", [P, NT, C])
        srcf = sb("srcf", [P, T])
        dstf = sb("dstf", [P, T])
        src_q, src_r = sb("src_q", [P, T]), sb("src_r", [P, T])
        dst_q, dst_r = sb("dst_q", [P, T]), sb("dst_r", [P, T])
        idx2 = sb("idx2", [P, T, 2], I32)
        idxk = sb("idxk", [P, T], I32)
        idx1s = sb("idx1s", [P, T], I32)
        idx1d = sb("idx1d", [P, T], I32)
        att3 = sb("att3", [P, T, 3])
        basis = sb("basis", [P, T * 9])
        unit = basis[:, 0:T * 5].rearrange("p (t k) -> p t k", k=5)
        basis8 = basis[:, 0:T * 8].rearrange("p (t k) -> p t k", k=8)
        basis9 = basis[:, :].rearrange("p (t k) -> p t k", k=9)
        ident = sb("ident", [128, 128])
        iota_h = sb("iota_h", [P, QW], FP16)
        quads = sb("quads", [P, GMAX, 4, C])
        zeros = sb("zeros", [P, 392], BF16)
        nodeT = sb("nodeT", [65, NP4])
        rdegT = sb("rdegT", [64, NP4])
        deg_s = sb("deg_s", [P, NT])
        deg_d = sb("deg_d", [P, NT])
        st1, st2, st3 = sb("st1", [P, NT]), sb("st2", [P, NT]), sb("st3", [P, NT])
        wbias = sb("wbias", [64, 4])
        WORK = 23600
        work = sb("work", [128, WORK])

        ps = ctx.enter_context(nc.psum_tensor("ps", [128, 8, 512], F32))

        at = [0]

        def carve(parts, shape, dt=F32):
            n = 1
            for d in shape:
                n *= d
            words = n if dt in (F32, I32) else (n + 1) // 2
            a = work[0:parts, at[0]:at[0] + words]
            at[0] += words
            assert at[0] <= WORK, at[0]
            if dt != F32:
                a = a.bitcast(dt)
            if len(shape) > 1:
                names = "abcde"[:len(shape)]
                a = a.rearrange("p (%s) -> p %s" % (" ".join(names), " ".join(names)),
                                **{k: d for k, d in zip(names, shape)})
            return a

        def bc(ap, shape):
            return ap.broadcast_to(shape)

        at[0] = 0
        stage_i = carve(LB, [2, NB, P], I32)
        iota_i = carve(P, [QW], I32)
        quads_i = carve(P, [4, C], I32)
        stage_f = carve(LB, [2, NB, P])
        stage3 = carve(LB, [NB, P * 3])
        with nc.Block() as block:
            s = {k: sem("set_" + k) for k in ("load", "index", "const", "float", "turned", "copied", "quad", "step", "unit")}

            @block.sync
            def _(sp):
                for k, a in enumerate(("src", "dst")):
                    sp.dma_start(stage_i[:, k], A[a].rearrange("(b r p) -> r b p", r=LB, p=P)).then_inc(s["index"], 16)
                sp.dma_start(stage3, A["edge_attr_3"].rearrange("(b r p) c -> r b (p c)", r=LB, p=P)).then_inc(s["load"], 16)
                sp.dma_start(X[:, :, :], A["x"].rearrange("(j p) c -> p j c", p=P)).then_inc(s["load"], 16)
                for k, a in enumerate(("L1_gnn_stn1_b", "L1_gnn_stn2_b", "L1_gnn_stn3_b")):
                    sp.dma_start(wbias[:, k:k + 1], A[a].rearrange("(n a) -> n a", a=1)).then_inc(s["load"], 16)
                sp.wait_ge(s["load"], 80)

            @block.gpsimd
            def _(gp):
                gp.iota(iota_i, [[1, QW]], base=0, channel_multiplier=0).then_inc(s["const"], 1)
                gp.iota(quads_i, [[1, 4], [0, C]], base=0, channel_multiplier=0).then_inc(s["const"], 1)
                gp.memset(ident[:, :], 0.0).then_inc(s["const"], 1)
                gp.wait_ge(s["const"], 3)
                gp.affine_select(out=ident[:, :], in_=ident[:, :], compare_op=ALU.not_equal, fill=1.0,
                                 base=0, pattern=[[-1, 128]], channel_multiplier=1).then_inc(s["const"], 1)

            @block.tensor
            def _(pe):
                pe.wait_ge(s["const"], 4)
                pe.wait_ge(s["float"], 1)
                for k in range(5):
                    if k == 2:
                        pe.wait_ge(s["load"], 80)
                    if k >= 4:
                        pe.wait_ge(s["copied"], k - 3)
                    for b in range(NB):
                        src = stage_f[:, k, b, :] if k < 2 else stage3[:, b, k - 2::3]
                        mm = pe.transpose(ps[0:P, 2 * (k % 4) + b // 4, (b % 4) * LB:(b % 4 + 1) * LB], src, ident[0:LB, 0:LB])
                    mm.then_inc(s["turned"], 1)

            @block.vector
            def _(v):
                v.wait_ge(s["index"], 32)
                v.tensor_copy(stage_f, stage_i).then_inc(s["float"], 1)
                v.wait_ge(s["const"], 4)
                v.tensor_copy(iota_h[:, :], iota_i)
                v.tensor_copy(quads[:, :, :, :], bc(quads_i[:, None], [P, GMAX, 4, C]))
                v.memset(zeros[:, :], 0.0)
                for k in range(5):
                    v.wait_ge(s["turned"], k + 1)
                    src = ps[0:P, 2 * (k % 4):2 * (k % 4) + 2, 0:4 * LB]
                    to = (srcf[:, :], dstf[:, :], att3[:, :, 0], att3[:, :, 1], att3[:, :, 2])[k]
                    v.tensor_copy(to.rearrange("p (a b) -> p a b", a=2), src).then_inc(s["copied"], 1)
                v.wait_ge(s["copied"], 5)
                n = 0
                for f, q, r, i in ((srcf, src_q, src_r, idx1s), (dstf, dst_q, dst_r, idx1d)):
                    v.tensor_copy(i[:, :], f[:, :])
                    v.tensor_scalar(q[:, :], f[:, :], float(QW), None, ALU.is_ge).then_inc(s["quad"], 1)
                    for m in (2, 3):
                        n += 1
                        v.wait_ge(s["quad"], n)
                        v.scalar_tensor_tensor(q[:, :], f[:, :], float(m * QW), q[:, :], ALU.is_ge, ALU.add).then_inc(s["quad"], 1)
                    n += 1
                    v.wait_ge(s["quad"], n)
                    v.scalar_tensor_tensor(r[:, :], q[:, :], -float(QW), f[:, :], ALU.mult, ALU.add)

        def layer_norm(name):
            s = sem(name + "_steps")
            r = sem(name + "_root")
            sq = carve(P, [NT, C])

            def vec(v):
                v.tensor_reduce(st1[:, :], X[:, :, :], AX.X, ALU.add).then_inc(s, 1)
                v.wait_ge(s, 1)
                v.tensor_scalar(st2[:, :], st1[:, :], 1.0 / C, None, ALU.mult).then_inc(s, 1)
                v.wait_ge(s, 2)
                v.tensor_tensor(H[:, :, :], X[:, :, :], bc(st2[:, :, None], [P, NT, C]), ALU.subtract).then_inc(s, 1)
                v.wait_ge(s, 3)
                v.tensor_tensor(sq, H[:, :, :], H[:, :, :], ALU.mult).then_inc(s, 1)
                v.wait_ge(s, 4)
                v.tensor_reduce(st1[:, :], sq, AX.X, ALU.add).then_inc(s, 1)
                v.wait_ge(s, 5)
                v.tensor_scalar(st1[:, :], st1[:, :], 1.0 / C, 1e-5, ALU.mult, ALU.add).then_inc(s, 1)
                v.wait_ge(r, 1)
                v.reciprocal(st3[:, :], st2[:, :]).then_inc(s, 1)
                v.wait_ge(s, 7)
                v.tensor_tensor(H[:, :, :], H[:, :, :], bc(st3[:, :, None], [P, NT, C]), ALU.mult).then_inc(s, 1)
                v.wait_ge(s, 8)
                v.tensor_scalar(H[:, :, :], H[:, :, :], 0.0, None, ALU.max).then_inc(s, 1)

            def sca(a):
                a.wait_ge(s, 6)
                a.activation(st2[:, :], st1[:, :], ACT.Sqrt).then_inc(r, 1)

            return s, vec, sca

        def spline_weights(v, s, base, pseudo, with_node, spline_tmp):
            cnt = [base]

            def done(ins):
                ins.then_inc(s, 1)
                cnt[0] += 1
                v.wait_ge(s, cnt[0])

            pos, i0, fr, b01, kn = spline_tmp
            done(v.tensor_scalar(pos, pseudo, 4.0, None, ALU.mult))
            done(v.tensor_scalar(i0, pos, 1.0, None, ALU.is_ge))
            for m in (2.0, 3.0):
                done(v.scalar_tensor_tensor(i0, pos, m, i0, ALU.is_ge, ALU.add))
            done(v.tensor_tensor(fr[:, :, :, 1], pos, i0, ALU.subtract))
            done(v.tensor_scalar(fr[:, :, :, 0], fr[:, :, :, 1], -1.0, 1.0, ALU.mult, ALU.add))
            done(v.tensor_tensor(b01, bc(fr[:, :, 0, None, :], [P, T, 2, 2]), bc(fr[:, :, 1, :, None], [P, T, 2, 2]), ALU.mult))
            for d1 in range(2):
                for d2 in range(2):
                    done(v.tensor_tensor(basis8[:, :, 4 * d1 + 2 * d2:4 * d1 + 2 * d2 + 2], b01[:, :, d1],
                                         bc(fr[:, :, 2, d2:d2 + 1], [P, T, 2]), ALU.mult))
            done(v.scalar_tensor_tensor(kn, i0[:, :, 0], 5.0, i0[:, :, 1], ALU.mult, ALU.add))
            done(v.scalar_tensor_tensor(kn, kn, 5.0, i0[:, :, 2], ALU.mult, ALU.add))
            if with_node:
                done(v.scalar_tensor_tensor(kn, dstf[:, :], float(KR), kn, ALU.mult, ALU.add))
            done(v.tensor_copy(idxk[:, :] if with_node else idx2[:, :, 0], kn))
            if not with_node:
                done(v.tensor_scalar(idx2[:, :, 1], kn, 25.0, None, ALU.add))
            return cnt[0]

        def two_step(eng, pairs, first, second, lead):
            if first is None:
                with eng.Fori(0, pairs) as i:
                    for x in range(2):
                        second(x, i)
                return
            first(0, 0)
            if lead == 2:
                first(1, 0)
            with eng.Fori(0, pairs - 1) as i:
                first(*((1, i) if lead == 1 else (0, i + 1)))
                second(0, i)
                first(*((0, i + 1) if lead == 1 else (1, i + 1)))
                second(1, i)
            if lead == 1:
                first(1, pairs - 1)
            second(0, pairs - 1)
            second(1, pairs - 1)

        edge_sems = {k: sem("edge_" + k) for k in ["window", "products"] + [
            f"{k}{x}" for k in ("message", "high", "residual", "middle", "low", "quads", "ready", "scattered",
                                "hidden", "radial", "radial_used") for x in (0, 1)]}

        def zero_edge_sems(sp):
            for k in edge_sems.values():
                sp.sem_clear(k)

        def edge_phase(name, G, gathers, F, extra, quad, rest, more):
            at[0] = keep
            PAIRS = T // G // 2
            U = F // 32
            FM = F + (2 if extra == "pair" else 0)
            NPASS = 3 * U + (1 if extra == "pair" else 0)
            s = dict(edge_sems)
            rows, wins = {}, {}
            for key, table, idx, ng, run in gathers:
                rows[key] = carve(P, [2, G * ng, run])
                wins[key] = carve(P, [2, G * ng], I32)
                for x in range(2):
                    s[f"{key}{x}"] = sem(f"{name}_{key}{x}")
            msg = carve(P, [2, G, FM])
            res = carve(P, [G, FM])
            part = carve(P, [2, 3, G, FM], BF16)
            stat = carve(P, [2, NPASS, G, 128], BF16)
            ohq = carve(P, [2, G, 128], BF16)
            ohr = carve(P, [2, G, QW], BF16)
            nacc = U + (1 if extra else 0)
            env = dict(rows=rows, F=F, G=G, PAIRS=PAIRS, msg=msg, s=s, name=name)
            more(env)
            with nc.Block() as block:
                @block.gpsimd
                def _(gp):
                    def gather(x, i):
                        for key, table, idx, ng, run in gathers:
                            o = gp.tensor_copy(wins[key][:, x, :], idx[:, bass.ds((2 * i + x) * (G * ng), G * ng)])
                        o.then_inc(s["window"], 1)
                        gp.wait_ge(s["window"], 2 * i + (x + 1))
                        gp.nop(nofuse=True)
                        for key, table, idx, ng, run in gathers:
                            for k in range(G * ng):
                                gp.indirect_dma_start(rows[key][:, x, k, :], None, table, bass.IndirectOffsetOnAxis(
                                    ap=wins[key][:, x, k:k + 1], axis=0)).then_inc(s[f"{key}{x}"], 16)

                    for x in range(2):
                        gather(x, 0)
                    with gp.Fori(1, PAIRS) as i:
                        for x in range(2):
                            gp.wait_ge(s[f"message{x}"], i)
                            gather(x, i)

                @block.vector
                def _(v):
                    if "v_begin" in env:
                        env["v_begin"](v)
                    if extra == "pair":
                        v.memset(stat[:, :, 3 * U, :, :], 0.0)
                    by_quad = lambda a: a.rearrange("p g (q c) -> p g q c", c=C)

                    def split(x, i):
                        g = 2 * i + x
                        v.wait_ge(s[f"scattered{x}"], i + 1)
                        v.tensor_tensor(by_quad(ohq[:, x]), quads[:, 0:G], bc(quad[:, bass.ds(g * G, G)][:, :, None, None], [P, G, 4, C]),
                                        ALU.is_equal).then_inc(s[f"quads{x}"], 1)
                        v.wait_ge(s[f"high{x}"], i + 1)
                        v.tensor_tensor(res, msg[:, x], part[:, x, 0], ALU.subtract).then_inc(s[f"residual{x}"], 1)
                        for k in range(G):
                            v.tensor_scalar(ohr[:, x, k, :], iota_h[:, :], rest[:, bass.ds(g * G + k, 1)], None, ALU.is_equal)
                        v.wait_ge(s[f"quads{x}"], i + 1)

                        def spread(k, last=False):
                            for u in range(U):
                                o = v.tensor_tensor(by_quad(stat[:, x, 3 * u + k]), by_quad(ohq[:, x]),
                                                    bc(part[:, x, k, :, None, 32 * u:32 * u + 32], [P, G, 4, C]), ALU.mult)
                            if extra == "pair":
                                o = v.tensor_tensor(by_quad(stat[:, x, 3 * U])[:, :, :, 2 * k:2 * k + 2], by_quad(ohq[:, x])[:, :, :, 0:2],
                                                    bc(part[:, x, k, :, None, F:F + 2], [P, G, 4, 2]), ALU.mult)
                            if last:
                                o.then_inc(s[f"ready{x}"], 1)

                        v.wait_ge(s[f"middle{x}"], i + 1)
                        v.tensor_tensor(part[:, x, 2], res, part[:, x, 1], ALU.subtract).then_inc(s[f"low{x}"], 1)
                        spread(0)
                        spread(1)
                        v.wait_ge(s[f"low{x}"], i + 1)
                        spread(2, last=True)

                    two_step(v, PAIRS, lambda x, i: env["message"](v, env, x, i), split, 1)

                @block.scalar
                def _(a):
                    def round_parts(x, i):
                        a.wait_ge(s[f"message{x}"], i + 1)
                        a.activation(part[:, x, 0], msg[:, x], ACT.Copy).then_inc(s[f"high{x}"], 1)
                        a.wait_ge(s[f"residual{x}"], i + 1)
                        a.activation(part[:, x, 1], res, ACT.Copy).then_inc(s[f"middle{x}"], 1)

                    first = env.get("a_first")
                    two_step(a, PAIRS, first and (lambda x, i: first(a, x, i)), round_parts, 2)

                @block.tensor
                def _(pe):
                    def scatter(x, i):
                        pe.wait_ge(s[f"ready{x}"], i + 1)
                        for k in range(G):
                            jobs = [(p // 3, stat[:, x, p, k, :]) for p in range(3 * U)]
                            if extra == "pair":
                                jobs.append((U, stat[:, x, 3 * U, k, :]))
                            if extra == "ones":
                                jobs.append((U, ohq[:, x, k, :]))
                            for u, w in jobs:
                                for h in range(2):
                                    mm = pe.matmul(ps[:, 2 * u + h, 0:HW], w, ohr[:, x, k, h * HW:(h + 1) * HW],
                                                   start=False, stop=False, skip_group_check=True)
                        mm.then_inc(s[f"scattered{x}"], 1)

                    for b in range(2 * nacc):
                        mm = pe.matmul(ps[:, b, 0:HW], zeros[:, 0:128], zeros[:, 0:HW], start=True, stop=False, skip_group_check=True)
                        if b < 2:
                            mm.then_inc(s[f"scattered{b}"], 1)
                    first = env.get("pe_first")
                    two_step(pe, PAIRS, first and (lambda x, i: first(pe, x, i)), scatter, 2)
                    for b in range(2 * nacc):
                        pe.matmul(ps[:, b, 0:HW], zeros[:, 0:128], zeros[:, 0:HW], start=False, stop=True, skip_group_check=True)

                if "sp" in env:
                    @block.sync
                    def _(sp):
                        env["sp"](sp)

        def unit_to_rows(eng, bank, dst, row):
            for q in range(4):
                for h in range(2):
                    c0 = q * QW + h * HW
                    o = eng(dst[row:row + 32, c0:c0 + HW], ps[32 * q:32 * q + 32, bank + h, 0:HW])
            return o

        def turn_to_nodes(pe, table, bank):
            for j in range(NT):
                mm = pe.transpose(ps[0:P, bank + j // 16, (j % 16) * 32:(j % 16) * 32 + 32], table[0:32, j * P:(j + 1) * P],
                                  ident[0:32, 0:32])
            return mm

        def nodes_of(bank):
            return ps[0:P, bank:bank + 2, :].rearrange("p b (j c) -> p (b j) c", c=32)[:, 0:NT, :]

        def turn_to_features(pe, nodes):
            for j in range(NT):
                mm = pe.transpose(ps[0:32, j // 4, (j % 4) * P:(j % 4 + 1) * P], nodes[:, j, :], ident[0:P, 0:P])
            return mm

        def copy_features(v, dst):
            v.tensor_copy(dst[0:32, 0:24 * P].rearrange("p (b n) -> p b n", b=6), ps[0:32, 0:6, 0:4 * P])
            return v.tensor_copy(dst[0:32, 24 * P:N], ps[0:32, 6, 0:P])

        at[0] = 0
        spline_tmp = (carve(P, [T, 3]), carve(P, [T, 3]), carve(P, [T, 3, 2]), carve(P, [T, 2, 2]), carve(P, [T]))
        with nc.Block() as block:
            weights_done = sem("spline1")

            @block.vector
            def _(v):
                spline_weights(v, weights_done, 0, att3[:, :, :], False, spline_tmp)

        def spline_conv(env):
            s, F, G, msg, rows = env["s"], env["F"], env["G"], env["msg"], env["rows"]["z"]
            runs = rows.shape[2] // G
            prods = carve(P, [2, G, 8, F])

            def message(v, env, x, i):
                g = 2 * i + x
                weights = basis8[:, bass.ds(g * G, G), :]
                prod = prods[:, x]
                v.wait_ge(s[f"z{x}"], runs * 16 * G * i + runs * 16 * G)
                for d1 in range(2):
                    if runs == 1:
                        o = v.tensor_tensor(prod[:, :, 4 * d1:4 * d1 + 4], rows[:, x, :, 10 * F * d1:10 * F * d1 + 4 * F].rearrange(
                            "p g (k f) -> p g k f", k=4), bc(weights[:, :, 4 * d1:4 * d1 + 4, None], [P, G, 4, F]), ALU.mult)
                        continue
                    for d0 in range(2):
                        run = rows[:, x].rearrange("p (g d) n -> p g d n", d=2)[:, :, d0, 5 * F * d1:5 * F * d1 + 2 * F]
                        o = v.tensor_tensor(prod[:, :, 4 * d1 + d0:4 * d1 + 4:2], run.rearrange("p g (k f) -> p g k f", k=2),
                                            bc(weights[:, :, 4 * d1 + d0:4 * d1 + 4:2, None], [P, G, 2, F]), ALU.mult)
                o.then_inc(s["products"], 1)
                v.wait_ge(s["products"], g + 1)
                v.tensor_reduce(msg[:, x], prod.rearrange("p g k f -> p g f k"), AX.X, ALU.add).then_inc(s[f"message{x}"], 1)

            env["message"] = message

        def elu(s, table, rows, bias):
            low = carve(rows, [NP4])

            def sca(a, start):
                a.wait_ge(s, start)
                a.activation(table[0:rows, :], table[0:rows, :], ACT.Identity, bias=bias).then_inc(s, 1)
                a.wait_ge(s, start + 2)
                a.activation(low, low, ACT.Exp).then_inc(s, 1)

            def vec(v, start):
                v.wait_ge(s, start + 1)
                v.tensor_scalar(low, table[0:rows, :], 0.0, None, ALU.min).then_inc(s, 1)
                v.wait_ge(s, start + 3)
                v.tensor_scalar(table[0:rows, :], table[0:rows, :], 0.0, None, ALU.max).then_inc(s, 1)
                v.wait_ge(s, start + 4)
                v.scalar_tensor_tensor(table[0:rows, :], low, -1.0, table[0:rows, :], ALU.add, ALU.add).then_inc(s, 1)

            return sca, vec

        keep = 0
        edge_phase("e1", 4, (("z", A["L1_gnn_stn1_w"].rearrange("k a o -> k (a o)"), idx2[:, :, :].rearrange("p t k -> p (t k)"),
                             2, 7 * 64),), 64, "ones", src_q, src_r, spline_conv)

        at[0] = 0
        with nc.Block() as block:
            s = {k: sem("n1_" + k) for k in ("sum0", "sum1", "turned", "elu")}
            elu_a, elu_v = elu(s["elu"], nodeT, 64, wbias[:, 0:1])

            @block.sync
            def _(sp):
                zero_edge_sems(sp)

            @block.scalar
            def _(a):
                unit_to_rows(lambda o, i: a.activation(o, i, ACT.Copy), 0, nodeT, 0)
                unit_to_rows(lambda o, i: a.activation(o, i, ACT.Copy), 4, rdegT, 0).then_inc(s["sum0"], 1)
                elu_a(a, 1)

            @block.tensor
            def _(pe):
                pe.wait_ge(s["sum0"], 1)
                turn_to_nodes(pe, rdegT, 6).then_inc(s["turned"], 1)

            @block.vector
            def _(v):
                unit_to_rows(lambda o, i: v.tensor_copy(o, i), 2, nodeT, 32)
                v.wait_ge(s["sum0"], 1)
                v.tensor_copy(rdegT[32:64, :], rdegT[0:32, :]).then_inc(s["sum1"], 1)
                v.wait_ge(s["turned"], 1)
                v.wait_ge(s["sum1"], 1)
                v.tensor_copy(deg_s[:, :], nodes_of(6)[:, :, 0])
                v.tensor_scalar(rdegT[:, :], rdegT[:, :], 1.0, None, ALU.max).then_inc(s["sum1"], 1)
                v.wait_ge(s["sum1"], 2)
                v.reciprocal(rdegT[:, :], rdegT[:, :]).then_inc(s["sum1"], 1)
                v.wait_ge(s["sum1"], 3)
                v.tensor_tensor(nodeT[0:64, :], nodeT[0:64, :], rdegT[:, :], ALU.mult).then_inc(s["elu"], 1)
                elu_v(v, 1)

        def table_block(name, F, weight, z_tab, more_v=None):
            cuts = [0, 7, 13, 19, 25] if F == 64 else [0, 13, 25]
            chunks = [(k0, a, b) for k0 in range(5) for a, b in zip(cuts, cuts[1:])]
            per = len(chunks)
            half = [3 * (len(cuts) - 1), per]
            BANKS = 5
            at[0] = 0
            wbig = carve(F, [KN * F])
            zst = carve(P, [4, 25, 2, F])
            hj = carve(F, [P])
            z = z_tab.rearrange("(n k) o -> n (k o)", k=KR)
            with nc.Block() as block:
                s = {k: sem(name + "_" + k) for k in ("weight", "tile", "product", "out_a", "out_v", "stored0", "stored1")}
                outs = ("out_a", "out_v")

                @block.sync
                def _(sp):
                    sp.dma_start(wbig.rearrange("i (k o) -> i k o", k=KN), weight.rearrange("k i o -> i k o")).then_inc(s["weight"], 16)
                    with sp.Fori(0, NT) as j:
                        for h in range(2):
                            for e in range(2):
                                sp.wait_ge(s[outs[e]], j * (per // 2) + (3 + (half[h] + 1 - e) // 2))
                            sp.nop(nofuse=True)
                            sp.dma_start(z[bass.ds(j * P, P), h * 100 * F:(h + 1) * 100 * F],
                                         zst[:, 2 * h:2 * h + 2].rearrange("p a b c f -> p (a b c f)")).then_inc(s[f"stored{h}"], 16)
                    for h in range(2):
                        sp.wait_ge(s[f"stored{h}"], 16 * NT)

                @block.tensor
                def _(pe):
                    for e in outs:
                        pe.sem_inc(s[e], 3)
                    pe.wait_ge(s["weight"], 16)
                    with pe.Fori(0, NT) as j:
                        pe.wait_ge(s["tile"], j + 1)
                        for c, (k0, a, b) in enumerate(chunks):
                            pe.wait_ge(s[outs[(c - BANKS) % 2]], j * (per // 2) + ((c - BANKS) // 2 + 4))
                            pe.matmul(ps[0:P, c % BANKS, 0:(b - a) * F], hj, wbig[:, (25 * k0 + a) * F:(25 * k0 + b) * F],
                                      start=True, stop=True, skip_group_check=True).then_inc(s["product"], 1)

                def copy_out(eng, copy, e, j, first):
                    free = 0
                    for c, (k0, a, b) in enumerate(chunks):
                        if c % 2 != e:
                            continue
                        while not first and free < 2 and k0 >= (0, 2)[free]:
                            eng.wait_ge(s[f"stored{free}"], 16 * j)
                            free += 1
                        eng.wait_ge(s["product"], j * per + (c + 1))
                        src = ps[0:P, c % BANKS, 0:(b - a) * F].rearrange("p (k f) -> p k f", f=F)
                        if k0 > 0:
                            o = copy(zst[:, k0 - 1, a:b, 1, :], src)
                        if k0 < 4:
                            o = copy(zst[:, k0, a:b, 0, :], src)
                        o.then_inc(s[outs[e]], 1)

                @block.scalar
                def _(a):
                    copy = lambda o, i: a.activation(o, i, ACT.Copy)
                    copy(hj, nodeT[0:F, 0:P]).then_inc(s["tile"], 1)
                    copy_out(a, copy, 0, 0, True)
                    with a.Fori(1, NT) as j:
                        a.wait_ge(s["product"], j * per)
                        copy(hj, nodeT[0:F, bass.ds(j * P, P)]).then_inc(s["tile"], 1)
                        copy_out(a, copy, 0, j, False)

                @block.vector
                def _(v):
                    if more_v:
                        more_v(v)
                    copy = lambda o, i: v.tensor_copy(o, i)
                    copy_out(v, copy, 1, 0, True)
                    with v.Fori(1, NT) as j:
                        copy_out(v, copy, 1, j, False)

        def add_node(v):
            v.scalar_tensor_tensor(idxk[:, :], dstf[:, :], float(KR), idx2[:, :, 0], ALU.mult, ALU.add)

        table_block("z2", 64, A["L1_gnn_stn2_w"], z2_tab, add_node)
        keep = 0
        edge_phase("e2", 4, (("z", z2_tab, idxk[:, :], 1, 7 * 128),), 64, None, src_q, src_r, spline_conv)

        at[0] = 0
        w3, w4, h3 = carve(64, [64]), carve(65, [3]), carve(65, [NP4])
        tn = carve(P, [NT, 3])
        with nc.Block() as block:
            s = {k: sem("n2_" + k) for k in ("load", "sum0", "sum1", "elu", "h3", "product", "ones", "t", "tn", "stored")}
            elu_a, elu_v = elu(s["elu"], nodeT, 64, wbias[:, 1:2])
            elu3_a, elu3_v = elu(s["h3"], h3, 64, wbias[:, 2:3])

            @block.sync
            def _(sp):
                zero_edge_sems(sp)
                sp.dma_start(w3, A["L1_gnn_stn3_w"]).then_inc(s["load"], 16)
                sp.dma_start(w4[0:64, :], A["L1_gnn_stn4_w"]).then_inc(s["load"], 16)
                sp.dma_start(w4[64:65, :], A["L1_gnn_stn4_b"].rearrange("(a n) -> a n", a=1)).then_inc(s["load"], 16)
                sp.wait_ge(s["tn"], 1)
                sp.dma_start(t_tab.rearrange("(j p) c -> p j c", p=P), tn).then_inc(s["stored"], 16)
                sp.wait_ge(s["stored"], 16)

            @block.scalar
            def _(a):
                unit_to_rows(lambda o, i: a.activation(o, i, ACT.Copy), 0, nodeT, 0).then_inc(s["sum0"], 1)
                elu_a(a, 1)
                a.wait_ge(s["product"], 1)
                a.activation(h3[0:64, :].rearrange("p (b n) -> p b n", b=8), ps[0:64, :, 0:HW], ACT.Copy).then_inc(s["h3"], 1)
                elu3_a(a, 1)

            @block.tensor
            def _(pe):
                pe.wait_ge(s["load"], 48)
                pe.wait_ge(s["elu"], 6)
                for b in range(8):
                    mm = pe.matmul(ps[0:64, b, 0:HW], w3, nodeT[0:64, b * HW:(b + 1) * HW], start=True, stop=True)
                mm.then_inc(s["product"], 1)
                pe.wait_ge(s["ones"], 1)
                pe.wait_ge(s["h3"], 6)
                for j in range(NT):
                    mm = pe.matmul(ps[0:P, 0, 3 * j:3 * j + 3], h3[:, j * P:(j + 1) * P], w4, start=True, stop=True)
                mm.then_inc(s["t"], 1)

            @block.vector
            def _(v):
                v.memset(h3[64:65, :], 1.0).then_inc(s["ones"], 1)
                unit_to_rows(lambda o, i: v.tensor_copy(o, i), 2, nodeT, 32).then_inc(s["sum1"], 1)
                v.wait_ge(s["sum0"], 1)
                v.wait_ge(s["sum1"], 1)
                v.tensor_tensor(nodeT[0:64, :], nodeT[0:64, :], rdegT[:, :], ALU.mult).then_inc(s["elu"], 1)
                elu_v(v, 1)
                elu3_v(v, 1)
                v.wait_ge(s["t"], 1)
                v.tensor_copy(tn, ps[0:P, 0, 0:3 * NT].rearrange("p (j c) -> p j c", c=3)).then_inc(s["tn"], 1)

        at[0] = 0
        w2mix = carve(65, [384])
        w1c = carve(64, [2])
        G0 = 4
        hid = carve(65, [2, G0 * P])
        wrow = carve(64, [2, G0 * P])
        keep = at[0]
        w2all = carve(65, [384])
        norm2, square = carve(P, [T]), carve(P, [T])
        with nc.Block() as block:
            ns, vec_norm, sca_norm = layer_norm("norm0")
            s = {k: sem("l0_" + k) for k in ("weights", "unit", "root", "store", "mix")}

            @block.sync
            def _(sp):
                sp.dma_start(w2all[0:64, :], A["L0_gnn_w2"]).then_inc(s["weights"], 16)
                sp.dma_start(w2all[64:65, :], A["L0_gnn_b2"].rearrange("(a n) -> a n", a=1)).then_inc(s["weights"], 16)
                sp.dma_start(w1c[:, 0:1], A["L0_gnn_w1"].rearrange("a n -> n a")).then_inc(s["weights"], 16)
                sp.dma_start(w1c[:, 1:2], A["L0_gnn_b1"].rearrange("(n a) -> n a", a=1)).then_inc(s["weights"], 16)
                sp.wait_ge(ns, 9)
                sp.dma_start(h0_tab.rearrange("(j p) c -> p j c", p=P), H[:, :, :]).then_inc(s["store"], 16)
                sp.wait_ge(s["store"], 16)

            @block.scalar
            def _(a):
                sca_norm(a)
                a.wait_ge(s["unit"], 5)
                a.activation(square, norm2, ACT.Sqrt).then_inc(s["root"], 1)

            @block.vector
            def _(v):
                vec_norm(v)
                v.tensor_copy(idx2[:, :, 0], dstf[:, :])
                v.tensor_copy(idx2[:, :, 1], srcf[:, :])
                v.memset(hid[64:65, :, :], 1.0)
                n = 0
                v.tensor_tensor(norm2, att3[:, :, 0], att3[:, :, 0], ALU.mult).then_inc(s["unit"], 1)
                for k in (1, 2):
                    n += 1
                    v.wait_ge(s["unit"], n)
                    v.tensor_tensor(square, att3[:, :, k], att3[:, :, k], ALU.mult).then_inc(s["unit"], 1)
                    n += 1
                    v.wait_ge(s["unit"], n)
                    v.tensor_tensor(norm2, norm2, square, ALU.add).then_inc(s["unit"], 1)
                v.wait_ge(s["root"], 1)
                v.reciprocal(norm2, square).then_inc(s["unit"], 1)
                v.wait_ge(s["unit"], 6)
                for to, k in enumerate((1, 2, 0, 1, 2)):
                    v.tensor_tensor(unit[:, :, to], att3[:, :, k], norm2, ALU.mult)
                v.wait_ge(s["weights"], 64)
                w01 = w2all[:, 0:192].rearrange("h (b u w) -> h b u w", b=3, u=8)
                w11 = w2all[:, 192:384].rearrange("h (u w k) -> h u w k", u=8, k=3)
                m1 = w2mix[:, 0:256].rearrange("h (r u x w) -> h r u x w", r=2, u=8, x=2)
                m2 = w2mix[:, 256:384].rearrange("h (r u w) -> h r u w", r=2, u=8)
                v.tensor_scalar(m1[:, 0, :, 0, :], w01[:, 0], PATH_00, None, ALU.mult)
                v.tensor_scalar(m1[:, 0, :, 1, :], w01[:, 1], PATH_01, None, ALU.mult)
                v.tensor_scalar(m1[:, 1, :, 0, :], w01[:, 2], PATH_10, None, ALU.mult)
                v.tensor_scalar(m1[:, 1, :, 1, :], w11[:, :, :, 2], PATH_11_2, None, ALU.mult)
                v.tensor_scalar(m2[:, 1], w11[:, :, :, 1], PATH_11_1, None, ALU.mult)
                v.tensor_scalar(m2[:, 0], w11[:, :, :, 2], -PATH_11_2 / 3.0, None, ALU.mult).then_inc(s["mix"], 1)
                v.wait_ge(s["mix"], 1)
                v.scalar_tensor_tensor(m2[:, 0], w11[:, :, :, 0], PATH_11_0, m2[:, 0], ALU.mult, ALU.add)

        def layer0(env):
            s, name, G, PAIRS = env["s"], env["name"], env["G"], env["PAIRS"]
            x16 = carve(P, [G, 16])
            dots = carve(P, [G, 8, 3])
            prod1 = carve(P, [G, 16, 16])
            prod2 = carve(P, [G, 16, 3, 8])
            red = carve(P, [G, 64])
            hx = carve(P, [G, 8, 5])
            c1, c2, c3 = carve(P, [G, 8, 3]), carve(P, [G, 8, 3]), carve(P, [G, 8, 3])
            for x in range(2):
                s[f"weight_row{x}"] = sem(f"weight_row{x}")
            we = A["edge_weight"].rearrange("(a n) -> a n", a=1)

            def sp_prog(sp):
                for x in range(2):
                    sp.dma_start(wrow[:, x, :], we[:, x * G * P:(x + 1) * G * P].broadcast_to([64, G * P])
                                 ).then_inc(s[f"weight_row{x}"], 16)
                with sp.Fori(1, PAIRS) as i:
                    for x in range(2):
                        sp.wait_ge(s[f"hidden{x}"], i)
                        sp.nop(nofuse=True)
                        sp.dma_start(wrow[:, x, :], we[:, bass.ds((2 * i + x) * (G * P), G * P)].broadcast_to([64, G * P])
                                     ).then_inc(s[f"weight_row{x}"], 16)

            def hidden(a, x, i):
                a.wait_ge(s[f"weight_row{x}"], 16 * i + 16)
                a.wait_ge(s[f"radial{x}"], 2 * i + 2)
                a.activation(hid[0:64, x, :], wrow[:, x, :], ACT.Relu, bias=w1c[:, 1:2], scale=w1c[:, 0:1]
                             ).then_inc(s[f"hidden{x}"], 1)

            def radial(pe, x, i):
                pe.wait_ge(s[f"hidden{x}"], i + 1)
                for half in range(2):
                    pe.wait_ge(s[f"radial_used{half}"], 2 * i + (x + 1))
                    for k in (2 * half, 2 * half + 1):
                        mm = pe.matmul(ps[0:P, 4 + k, 0:384], hid[:, x, k * P:(k + 1) * P], w2mix, start=True, stop=True,
                                       skip_group_check=True)
                    mm.then_inc(s[f"radial{x}"], 1)

            def v_begin(v):
                for x in range(2):
                    v.sem_inc(s[f"radial{x}"], 2)
                    v.sem_inc(s[f"radial_used{x}"], 1)

            def message(v, env, x, i):
                g = 2 * i + x
                n = [0]
                per = 7

                def done(ins):
                    ins.then_inc(s["products"], 1)
                    n[0] += 1
                    v.wait_ge(s["products"], g * per + n[0])

                rows = env["rows"]["h"][:, x]
                f1 = rows[:, :, 8:32].rearrange("p g (w o) -> p g w o", o=3)
                r = unit[:, bass.ds(g * G, G), :]
                v.wait_ge(s[f"h{x}"], 16 * G * i + 16 * G)
                v.tensor_copy(x16[:, :, 0:8], rows[:, :, 0:8])
                done(v.tensor_tensor(dots, f1, bc(r[:, :, None, 0:3], [P, G, 8, 3]), ALU.mult))
                done(v.tensor_reduce(x16[:, :, 8:16], dots, AX.X, ALU.add))
                for half in range(2):
                    t2 = slice(2 * half, 2 * half + 2)
                    v.wait_ge(s[f"radial{x}"], 2 * i + (3 + half))
                    rad = ps[0:P, 4 + 2 * half:6 + 2 * half, :]
                    v.tensor_tensor(prod1[:, t2], rad[:, :, 0:256].rearrange("p t (r c) -> p t r c", c=16),
                                    bc(x16[:, t2, None, :], [P, 2, 16, 16]), ALU.mult)
                    for t in range(2):
                        k = 2 * half + t
                        o = v.tensor_tensor(prod2[:, k], bc(rad[:, t, 256:384].rearrange("p (r c) -> p r c", c=8)[:, :, None, :],
                                                            [P, 16, 3, 8]),
                                            bc(f1[:, k].rearrange("p w o -> p o w")[:, None, :, :], [P, 16, 3, 8]), ALU.mult)
                    o.then_inc(s[f"radial_used{half}"], 1)
                for half in range(2):
                    v.wait_ge(s[f"radial_used{half}"], g + 2)
                v.tensor_reduce(red[:, :, 0:16], prod1, AX.X, ALU.add)
                done(v.tensor_reduce(red[:, :, 16:64], prod2.rearrange("p g r o w -> p g (r o) w"), AX.X, ALU.add))
                gu = red[:, :, 16:40].rearrange("p g (u o) -> p g u o", o=3)
                hu = red[:, :, 40:64].rearrange("p g (u o) -> p g u o", o=3)
                qu = red[:, :, 8:16]
                v.tensor_copy(env["msg"][:, x, :, 0:8], red[:, :, 0:8])
                v.tensor_copy(hx[:, :, :, 0:3], hu)
                v.tensor_tensor(c3, bc(qu[:, :, :, None], [P, G, 8, 3]), bc(r[:, :, None, 0:3], [P, G, 8, 3]), ALU.mult)
                done(v.tensor_copy(hx[:, :, :, 3:5], hu[:, :, :, 0:2]))
                v.tensor_tensor(c1, bc(r[:, :, None, 1:4], [P, G, 8, 3]), hx[:, :, :, 2:5], ALU.mult)
                done(v.tensor_tensor(c2, bc(r[:, :, None, 2:5], [P, G, 8, 3]), hx[:, :, :, 1:4], ALU.mult))
                v.tensor_tensor(c3, c3, gu, ALU.add)
                done(v.tensor_tensor(c1, c1, c2, ALU.subtract))
                ts = env["rows"]["t"][:, x].rearrange("p (g k) c -> p g k c", k=2)
                a3 = att3[:, bass.ds(g * G, G), :]
                v.wait_ge(s[f"t{x}"], 32 * G * i + 32 * G)
                done(v.tensor_tensor(a3, a3, ts[:, :, 0], ALU.add))
                v.tensor_tensor(a3, a3, ts[:, :, 1], ALU.subtract)
                v.tensor_tensor(env["msg"][:, x, :, 8:32].rearrange("p g (u o) -> p g u o", o=3), c1, c3, ALU.add
                                ).then_inc(s[f"message{x}"], 1)
                assert n[0] == per

            env.update(sp=sp_prog, a_first=hidden, v_begin=v_begin, pe_first=radial, message=message)

        edge_phase("e0", G0, (("h", h0_tab, idx1s[:, :], 1, C), ("t", t_tab, idx2[:, :, :].rearrange("p t k -> p (t k)"), 2, 3)),
                   32, "ones", dst_q, dst_r, layer0)

        at[0] = 0
        spline_tmp = (carve(P, [T, 3]), carve(P, [T, 3]), carve(P, [T, 3, 2]), carve(P, [T, 2, 2]), carve(P, [T]))
        degT = carve(32, [NP4])
        with nc.Block() as block:
            ns, vec_norm, sca_norm = layer_norm("norm1")
            s = {k: sem("n0_" + k) for k in ("sum", "deg", "turned", "features", "spline")}

            @block.sync
            def _(sp):
                zero_edge_sems(sp)

            @block.scalar
            def _(a):
                unit_to_rows(lambda o, i: a.activation(o, i, ACT.Copy), 0, nodeT, 0).then_inc(s["sum"], 1)
                sca_norm(a)

            @block.tensor
            def _(pe):
                pe.wait_ge(s["sum"], 1)
                turn_to_nodes(pe, nodeT, 4).then_inc(s["turned"], 1)
                pe.wait_ge(s["deg"], 1)
                turn_to_nodes(pe, degT, 6).then_inc(s["turned"], 1)
                pe.wait_ge(ns, 9)
                turn_to_features(pe, H).then_inc(s["features"], 1)

            @block.vector
            def _(v):
                unit_to_rows(lambda o, i: v.tensor_copy(o, i), 2, degT, 0).then_inc(s["deg"], 1)
                v.wait_ge(s["turned"], 2)
                v.tensor_copy(deg_d[:, :], nodes_of(6)[:, :, 0])
                v.tensor_tensor(X[:, :, :], X[:, :, :], nodes_of(4), ALU.add).then_inc(s["turned"], 1)
                v.wait_ge(s["turned"], 3)
                vec_norm(v)
                v.tensor_scalar(att3[:, :, :], att3[:, :, :], 0.0, 1.0, ALU.max, ALU.min).then_inc(s["spline"], 1)
                v.wait_ge(s["spline"], 1)
                spline_weights(v, s["spline"], 1, att3[:, :, :], True, spline_tmp)
                v.wait_ge(s["features"], 1)
                copy_features(v, nodeT)

        table_block("z3", 32, A["L1_gnn_conv_w"], z3_tab)
        keep = 0
        edge_phase("e3", 8, (("z", z3_tab, idxk[:, :], 1, 7 * 64),), 32, None, src_q, src_r, spline_conv)

        at[0] = 0
        cb = carve(P, [C])
        wl2 = carve(33, [320])
        zl = carve(P, [NT, 288])
        root = carve(P, [NT, C])
        stage2 = carve(LB, [NB, P * 2])
        att2 = carve(P, [T, 2])
        hats = carve(P, [T, 2, 3])
        with nc.Block() as block:
            ns, vec_norm, sca_norm = layer_norm("norm2")
            s = {k: sem("n4_" + k) for k in ("load", "sum", "mean", "turned", "added", "features", "product", "copied",
                                              "stored", "att", "att_in", "hat")}

            @block.sync
            def _(sp):
                zero_edge_sems(sp)
                sp.dma_start(stage2, A["edge_attr_2"].rearrange("(b r p) c -> r b (p c)", r=LB, p=P)).then_inc(s["load"], 16)
                sp.dma_start(cb, A["L1_gnn_conv_b"].rearrange("(a n) -> a n", a=1).broadcast_to([P, C])).then_inc(s["load"], 16)
                sp.dma_start(wl2[0:32, 0:288].rearrange("i (k o) -> i k o", k=9), A["L2_gnn_weight"].rearrange("k i o -> i k o")
                             ).then_inc(s["load"], 16)
                sp.dma_start(wl2[0:32, 288:320], A["L2_gnn_root_w"]).then_inc(s["load"], 16)
                sp.dma_start(wl2[32:33, 288:320], A["L2_gnn_root_b"].rearrange("(a n) -> a n", a=1)).then_inc(s["load"], 16)
                sp.wait_ge(s["copied"], NT)
                sp.dma_start(zl2_tab.rearrange("(j p) c -> p j c", p=P), zl).then_inc(s["stored"], 16)
                sp.wait_ge(s["stored"], 16)

            @block.scalar
            def _(a):
                unit_to_rows(lambda o, i: a.activation(o, i, ACT.Copy), 0, nodeT, 0).then_inc(s["sum"], 1)
                sca_norm(a)

            @block.tensor
            def _(pe):
                pe.wait_ge(s["mean"], 1)
                turn_to_nodes(pe, nodeT, 4).then_inc(s["turned"], 1)
                pe.wait_ge(ns, 9)
                turn_to_features(pe, H).then_inc(s["turned"], 1)
                pe.wait_ge(s["features"], 1)
                pe.wait_ge(s["load"], 80)
                for j in range(NT):
                    if j >= 8:
                        pe.wait_ge(s["copied"], j - 7)
                    pe.matmul(ps[0:P, j % 8, 0:320], nodeT[0:33, j * P:(j + 1) * P], wl2, start=True, stop=True).then_inc(s["product"], 1)
                pe.wait_ge(s["copied"], NT)
                for k in range(2):
                    for b in range(NB):
                        mm = pe.transpose(ps[0:P, 2 * k + b // 4, (b % 4) * LB:(b % 4 + 1) * LB], stage2[:, b, k::2], ident[0:LB, 0:LB])
                    mm.then_inc(s["att"], 1)

            @block.vector
            def _(v):
                v.wait_ge(s["sum"], 1)
                v.tensor_tensor(nodeT[0:32, :], nodeT[0:32, :], rdegT[0:32, :], ALU.mult).then_inc(s["mean"], 1)
                v.wait_ge(s["load"], 80)
                v.tensor_tensor(X[:, :, :], X[:, :, :], bc(cb[:, None, :], [P, NT, C]), ALU.add).then_inc(s["added"], 1)
                v.wait_ge(s["added"], 1)
                v.wait_ge(s["turned"], 1)
                v.tensor_tensor(X[:, :, :], X[:, :, :], nodes_of(4), ALU.add).then_inc(s["added"], 1)
                v.wait_ge(s["added"], 2)
                vec_norm(v)
                v.memset(wl2[32:33, 0:288], 0.0)
                v.memset(nodeT[32:33, :], 1.0)
                v.wait_ge(s["turned"], 2)
                copy_features(v, nodeT).then_inc(s["features"], 1)
                for j in range(NT):
                    v.wait_ge(s["product"], j + 1)
                    v.tensor_copy(root[:, j, :], ps[0:P, j % 8, 288:320])
                    v.tensor_copy(zl[:, j, :], ps[0:P, j % 8, 0:288]).then_inc(s["copied"], 1)
                for k in range(2):
                    v.wait_ge(s["att"], k + 1)
                    v.tensor_copy(att2[:, :, k].rearrange("p (a b) -> p a b", a=2), ps[0:P, 2 * k:2 * k + 2, 0:4 * LB]).then_inc(s["att_in"], 1)
                v.wait_ge(s["att_in"], 2)
                v.tensor_scalar(att2, att2, 0.0, 1.0, ALU.max, ALU.min).then_inc(s["hat"], 1)
                v.wait_ge(s["hat"], 1)
                for k in range(3):
                    o = v.tensor_scalar(hats[:, :, :, k], att2, -0.5 * k, 2.0, ALU.add, ALU.mult)
                o.then_inc(s["hat"], 1)
                v.wait_ge(s["hat"], 2)
                v.scalar_tensor_tensor(hats, hats, -1.0, hats, ALU.mult, ALU.max).then_inc(s["hat"], 1)
                v.wait_ge(s["hat"], 3)
                v.tensor_scalar(hats, hats, -1.0, 1.0, ALU.mult, ALU.add).then_inc(s["hat"], 1)
                v.wait_ge(s["hat"], 4)
                v.tensor_scalar(hats, hats, 0.0, None, ALU.max).then_inc(s["hat"], 1)
                v.wait_ge(s["hat"], 5)
                for k in range(3):
                    v.tensor_tensor(basis9[:, :, 3 * k:3 * k + 3], hats[:, :, 1], bc(hats[:, :, 0, k:k + 1], [P, T, 3]), ALU.mult)
                v.tensor_copy(H[:, :, :], root)

        def nine_kernels(env):
            msg, s, G, rows = env["msg"], env["s"], env["G"], env["rows"]["z"]
            prods = carve(P, [2, G * 9, C])

            def message(v, env, x, i):
                g = 2 * i + x
                weights = basis9[:, bass.ds(g * G, G), :].rearrange("p g k -> p (g k)")
                prod = prods[:, x]
                v.wait_ge(s[f"z{x}"], 16 * G * i + 16 * G)
                v.tensor_tensor(prod, rows[:, x].rearrange("p g (k f) -> p (g k) f", k=9), bc(weights[:, :, None], [P, G * 9, C]),
                                ALU.mult).then_inc(s["products"], 1)
                v.wait_ge(s["products"], g + 1)
                v.tensor_reduce(msg[:, x], prod.rearrange("p (g k) f -> p g f k", k=9), AX.X, ALU.add).then_inc(s[f"message{x}"], 1)

            env["message"] = message

        keep = 0
        edge_phase("e4", 8, (("z", zl2_tab, idx1s[:, :], 1, 288),), 32, None, dst_q, dst_r, nine_kernels)

        at[0] = 0
        mask = carve(P, [NT])
        dis, dis_m, rd = carve(P, [NT]), carve(P, [NT]), carve(P, [NT])
        y3 = carve(P, [NT, 34])
        with nc.Block() as block:
            ns, vec_norm, sca_norm = layer_norm("norm3")
            s = {k: sem("n5_" + k) for k in ("load", "sum", "turned", "rd", "root", "dis", "added", "guard", "table", "stored")}

            @block.sync
            def _(sp):
                zero_edge_sems(sp)
                sp.dma_start(mask, A["node_vec1"]).then_inc(s["load"], 16)
                sp.wait_ge(s["table"], 1)
                sp.dma_start(y3_tab.rearrange("(j p) c -> p j c", p=P), y3).then_inc(s["stored"], 16)
                sp.wait_ge(s["stored"], 16)

            @block.scalar
            def _(a):
                unit_to_rows(lambda o, i: a.activation(o, i, ACT.Copy), 0, nodeT, 0).then_inc(s["sum"], 1)
                a.wait_ge(s["dis"], 1)
                a.activation(dis_m, dis, ACT.Sqrt).then_inc(s["root"], 1)
                sca_norm(a)

            @block.tensor
            def _(pe):
                pe.wait_ge(s["sum"], 1)
                turn_to_nodes(pe, nodeT, 4).then_inc(s["turned"], 1)

            @block.vector
            def _(v):
                v.tensor_scalar(dis, deg_s[:, :], 1.0, None, ALU.max).then_inc(s["dis"], 1)
                v.tensor_scalar(rd, deg_d[:, :], 1.0, None, ALU.max).then_inc(s["rd"], 1)
                v.tensor_tensor(X[:, :, :], X[:, :, :], H[:, :, :], ALU.add).then_inc(s["added"], 1)
                v.wait_ge(s["rd"], 1)
                v.reciprocal(rd, rd).then_inc(s["rd"], 1)
                v.wait_ge(s["root"], 1)
                v.reciprocal(dis, dis_m).then_inc(s["dis"], 1)
                v.wait_ge(s["dis"], 2)
                v.scalar_tensor_tensor(dis, deg_s[:, :], 0.0, dis, ALU.is_gt, ALU.mult).then_inc(s["dis"], 1)
                v.wait_ge(s["dis"], 3)
                v.wait_ge(s["load"], 16)
                v.tensor_tensor(dis_m, dis, mask, ALU.mult).then_inc(s["dis"], 1)
                v.wait_ge(s["rd"], 2)
                v.wait_ge(s["turned"], 1)
                v.tensor_tensor(H[:, :, :], nodes_of(4), bc(rd[:, :, None], [P, NT, C]), ALU.mult).then_inc(s["added"], 1)
                v.wait_ge(s["added"], 2)
                v.tensor_tensor(X[:, :, :], X[:, :, :], H[:, :, :], ALU.add).then_inc(s["added"], 1)
                v.wait_ge(s["added"], 3)
                vec_norm(v)
                v.wait_ge(ns, 9)
                big = 3.4028234663852886e38
                v.tensor_scalar(H[:, :, :], H[:, :, :], -big, big, ALU.max, ALU.min).then_inc(s["guard"], 1)
                v.wait_ge(s["guard"], 1)
                v.wait_ge(s["dis"], 4)
                v.tensor_copy(y3[:, :, 32], dis)
                v.tensor_copy(y3[:, :, 33], dis_m)
                v.tensor_tensor(y3[:, :, 0:32], H[:, :, :], bc(dis_m[:, :, None], [P, NT, C]), ALU.mult).then_inc(s["table"], 1)

        def plain(env):
            G = env["G"]

            def message(v, env, x, i):
                v.wait_ge(env["s"][f"y{x}"], 16 * G * i + 16 * G)
                v.tensor_copy(env["msg"][:, x], env["rows"]["y"][:, x]).then_inc(env["s"][f"message{x}"], 1)

            env["message"] = message

        edge_phase("e5", 8, (("y", y3_tab, idx1d[:, :], 1, 34),), 32, "pair", src_q, src_r, plain)

        at[0] = 0
        dis2, dis_2, num, den, zero = (carve(P, [NT]) for _ in range(5))
        wl3, b3 = carve(32, [C]), carve(P, [C])
        res = carve(P, [NT, C])
        with nc.Block() as block:
            s = {k: sem("n6_" + k) for k in ("load", "sum", "pair", "turned", "step", "root", "ratio", "features", "product",
                                              "out", "stored")}

            @block.sync
            def _(sp):
                sp.dma_start(wl3, A["L3_gnn_W"]).then_inc(s["load"], 16)
                sp.dma_start(b3, A["L3_gnn_b"].rearrange("(a n) -> a n", a=1).broadcast_to([P, C])).then_inc(s["load"], 16)
                sp.wait_ge(s["out"], 3)
                sp.dma_start(out.rearrange("(j p) c -> p j c", p=P), X[:, :, :]).then_inc(s["stored"], 16)
                sp.wait_ge(s["stored"], 16)

            @block.scalar
            def _(a):
                unit_to_rows(lambda o, i: a.activation(o, i, ACT.Copy), 0, nodeT, 0).then_inc(s["sum"], 1)
                a.wait_ge(s["step"], 1)
                a.activation(dis_2, dis2, ACT.Sqrt).then_inc(s["root"], 1)

            @block.tensor
            def _(pe):
                pe.wait_ge(s["sum"], 1)
                turn_to_nodes(pe, nodeT, 4).then_inc(s["turned"], 1)
                pe.wait_ge(s["pair"], 1)
                turn_to_nodes(pe, rdegT, 6).then_inc(s["turned"], 1)
                pe.wait_ge(s["ratio"], 1)
                turn_to_features(pe, H).then_inc(s["turned"], 1)
                pe.wait_ge(s["features"], 1)
                pe.wait_ge(s["load"], 32)
                for j in range(NT):
                    mm = pe.matmul(ps[0:P, j // 16, (j % 16) * 32:(j % 16) * 32 + 32], nodeT[0:32, j * P:(j + 1) * P], wl3,
                                   start=True, stop=True)
                mm.then_inc(s["product"], 1)

            @block.vector
            def _(v):
                n = [0]

                def done(ins):
                    ins.then_inc(s["step"], 1)
                    n[0] += 1
                    v.wait_ge(s["step"], n[0])

                unit_to_rows(lambda o, i: v.tensor_copy(o, i), 2, rdegT, 0).then_inc(s["pair"], 1)
                done(v.tensor_scalar(dis2, deg_s[:, :], 1.0, None, ALU.max))
                v.wait_ge(s["root"], 1)
                done(v.reciprocal(dis2, dis_2))
                done(v.scalar_tensor_tensor(dis2, deg_s[:, :], 0.0, dis2, ALU.is_gt, ALU.mult))
                v.wait_ge(s["turned"], 2)
                pair = nodes_of(6)
                done(v.tensor_reduce(num, pair[:, :, 0:6:2], AX.X, ALU.add))
                done(v.tensor_reduce(den, pair[:, :, 1:6:2], AX.X, ALU.add))
                done(v.tensor_tensor(num, num, dis2, ALU.mult))
                done(v.tensor_tensor(den, den, dis2, ALU.mult))
                done(v.tensor_scalar(zero, den, 0.0, None, ALU.is_equal))
                done(v.tensor_tensor(den, den, zero, ALU.add))
                done(v.reciprocal(den, den))
                done(v.tensor_tensor(H[:, :, :], nodes_of(4), bc(dis2[:, :, None], [P, NT, C]), ALU.mult))
                done(v.tensor_tensor(H[:, :, :], H[:, :, :], bc(num[:, :, None], [P, NT, C]), ALU.mult))
                done(v.tensor_tensor(H[:, :, :], H[:, :, :], bc(den[:, :, None], [P, NT, C]), ALU.mult))
                done(v.tensor_scalar(zero, zero, -1.0, 1.0, ALU.mult, ALU.add))
                v.tensor_tensor(H[:, :, :], H[:, :, :], bc(zero[:, :, None], [P, NT, C]), ALU.mult).then_inc(s["ratio"], 1)
                v.wait_ge(s["turned"], 3)
                copy_features(v, nodeT).then_inc(s["features"], 1)
                v.wait_ge(s["load"], 32)
                v.tensor_tensor(X[:, :, :], X[:, :, :], bc(b3[:, None, :], [P, NT, C]), ALU.add).then_inc(s["out"], 1)
                v.wait_ge(s["product"], 1)
                v.wait_ge(s["out"], 1)
                v.tensor_tensor(X[:, :, :], X[:, :, :], nodes_of(0), ALU.add).then_inc(s["out"], 2)


NAMES = ["x", "src", "dst", "edge_attr_2", "edge_attr_3", "edge_weight", "node_vec1", "L0_gnn_w1", "L0_gnn_b1", "L0_gnn_w2",
         "L0_gnn_b2", "L1_gnn_stn1_w", "L1_gnn_stn1_b", "L1_gnn_stn2_w", "L1_gnn_stn2_b", "L1_gnn_stn3_w", "L1_gnn_stn3_b",
         "L1_gnn_stn4_w", "L1_gnn_stn4_b", "L1_gnn_conv_w", "L1_gnn_conv_b", "L2_gnn_weight", "L2_gnn_root_w", "L2_gnn_root_b",
         "L3_gnn_W", "L3_gnn_b"]


def kernel(**inputs):
    import numpy as _np
    import concourse.bacc as _bacc
    from concourse import mybir as _mybir
    from concourse.bass_utils import run_bass_kernel_spmd as _run

    nc = _bacc.Bacc("TRN2", target_bir_lowering=False, num_devices=1)
    arrays, tensors = {}, {}
    for name in NAMES:
        a = inputs[name]
        if name in ("L2_gnn_root_w", "L3_gnn_W"):
            a = _np.asarray(a).T
        if name == "node_vec1":
            a = _np.asarray(a).reshape(NT, P).T
        a = _np.ascontiguousarray(a)
        arrays[f"in_{name}"] = a
        tensors[name] = nc.dram_tensor(f"in_{name}", a.shape, _mybir.dt.from_np(a.dtype), kind="ExternalInput").ap()
    out = nc.dram_tensor("out_0", (N, C), _mybir.dt.float32, kind="ExternalOutput").ap()
    build(nc, tensors, out)
    r = _run(nc, [arrays], core_ids=[0])
    return r.results[0]["out_0"]
```

```python
from contextlib import ExitStack
from math import pi, sqrt

import concourse.bass as bass
from concourse import mybir

F32 = mybir.dt.float32
BF16 = mybir.dt.bfloat16
FP16 = mybir.dt.float16
I32 = mybir.dt.int32
ALU = mybir.AluOpType
ACT = mybir.ActivationFunctionType
AX = mybir.AxisListType

P = 125
N = 3125
E = 100000
T = E // P
NT = N // P
C = 32
GMAX = 8
QW = 782
HW = QW // 2
NP4 = 4 * QW
KN = 125
KR = 100
LB = 100
NB = T // LB

NORM0 = sqrt(4 * pi) / sqrt(16.0)
NORM1 = sqrt(4 * pi) * sqrt(3.0) / sqrt(32.0)
Y0 = 0.5 / sqrt(pi)
C1 = sqrt(3.0 / (4.0 * pi))
PATH_00 = NORM0 * Y0
PATH_01 = NORM0 * C1 / sqrt(3.0)
PATH_10 = NORM1 * C1 / sqrt(3.0)
PATH_11_0 = NORM1 * Y0 / sqrt(3.0)
PATH_11_1 = NORM1 * C1 / sqrt(6.0)
PATH_11_2 = NORM1 * 0.5 * sqrt(15.0 / pi) / sqrt(10.0)


def build(nc, A, out):
    with ExitStack() as ctx:
        def sb(name, shape, dt=F32):
            return ctx.enter_context(nc.sbuf_tensor(name, shape, dt))

        def sem(name):
            return ctx.enter_context(nc.semaphore(name))

        def dram(name, shape, dt=F32):
            return nc.dram_tensor(name, shape, dt, kind="Internal").ap()

        h0_tab = dram("h0_tab", (N, C + 3))
        z2_tab = dram("z2_tab", (N * KN, 64))
        z3_tab = dram("z3_tab", (N * KR, 64))
        t_tab = dram("t_tab", (N, 3))
        zl2_tab = dram("zl2_tab", (N, 288))
        y3_tab = dram("y3_tab", (N, 34))

        s1_tab = [dram(f"s1_tab{k}", (N + P, 65)) for k in range(8)]

        X = sb("X", [P, NT, C])
        H = sb("H", [P, NT, C])
        srcf = sb("srcf", [P, T])
        dstf = sb("dstf", [P, T])
        src_q, src_r = sb("src_q", [P, T]), sb("src_r", [P, T])
        dst_q, dst_r = sb("dst_q", [P, T]), sb("dst_r", [P, T])
        idx2 = sb("idx2", [P, T, 2], I32)
        idxk = sb("idxk", [P, T], I32)
        idx1s = sb("idx1s", [P, T], I32)
        idx1d = sb("idx1d", [P, T], I32)
        att3 = sb("att3", [P, T, 3])
        basis = sb("basis", [P, T * 9])
        unit = basis[:, 0:T * 5].rearrange("p (t k) -> p t k", k=5)
        basis8 = basis[:, 0:T * 8].rearrange("p (t k) -> p t k", k=8)
        basis9 = basis[:, :].rearrange("p (t k) -> p t k", k=9)
        ident = sb("ident", [128, 128])
        iota_h = sb("iota_h", [P, QW], FP16)
        quads = sb("quads", [P, GMAX, 4, C])
        zeros = sb("zeros", [P, 392], BF16)
        nodeT = sb("nodeT", [65, NP4])
        rdegT = sb("rdegT", [64, NP4])
        deg_s = sb("deg_s", [P, NT])
        deg_d = sb("deg_d", [P, NT])
        tn = sb("tn", [P, NT, 3])
        st1, st2, st3 = sb("st1", [P, NT]), sb("st2", [P, NT]), sb("st3", [P, NT])
        wbias = sb("wbias", [64, 4])
        WORK = 23600
        work = sb("work", [128, WORK])

        ps = ctx.enter_context(nc.psum_tensor("ps", [128, 8, 512], F32))

        at = [0]

        def carve(parts, shape, dt=F32):
            n = 1
            for d in shape:
                n *= d
            words = n if dt in (F32, I32) else (n + 1) // 2
            a = work[0:parts, at[0]:at[0] + words]
            at[0] += words
            assert at[0] <= WORK, at[0]
            if dt != F32:
                a = a.bitcast(dt)
            if len(shape) > 1:
                names = "abcde"[:len(shape)]
                a = a.rearrange("p (%s) -> p %s" % (" ".join(names), " ".join(names)),
                                **{k: d for k, d in zip(names, shape)})
            return a

        def bc(ap, shape):
            return ap.broadcast_to(shape)

        at[0] = 0
        stage_i = carve(LB, [2, NB, P], I32)
        iota_i = carve(P, [QW], I32)
        quads_i = carve(P, [4, C], I32)
        stage_f = carve(LB, [2, NB, P])
        stage3 = carve(LB, [NB, P * 3])
        zero_rows = carve(P, [(N // P + 1) * 65])
        with nc.Block() as block:
            s = {k: sem("set_" + k) for k in ("load", "index", "const", "zero", "zeroed", "float", "turned", "copied", "quad", "step", "unit")}

            @block.sync
            def _(sp):
                for k, a in enumerate(("src", "dst")):
                    sp.dma_start(stage_i[:, k], A[a].rearrange("(b r p) -> r b p", r=LB, p=P)).then_inc(s["index"], 16)
                sp.dma_start(stage3, A["edge_attr_3"].rearrange("(b r p) c -> r b (p c)", r=LB, p=P)).then_inc(s["load"], 16)
                sp.dma_start(X[:, :, :], A["x"].rearrange("(j p) c -> p j c", p=P)).then_inc(s["load"], 16)
                for k, a in enumerate(("L1_gnn_stn1_b", "L1_gnn_stn2_b", "L1_gnn_stn3_b")):
                    sp.dma_start(wbias[:, k:k + 1], A[a].rearrange("(n a) -> n a", a=1)).then_inc(s["load"], 16)
                sp.wait_ge(s["load"], 80)
                sp.wait_ge(s["zero"], 1)
                for t in s1_tab:
                    sp.dma_start(t.rearrange("(p j) c -> p (j c)", p=P), zero_rows).then_inc(s["zeroed"], 16)
                sp.wait_ge(s["zeroed"], 16 * len(s1_tab))

            @block.gpsimd
            def _(gp):
                gp.iota(iota_i, [[1, QW]], base=0, channel_multiplier=0).then_inc(s["const"], 1)
                gp.iota(quads_i, [[1, 4], [0, C]], base=0, channel_multiplier=0).then_inc(s["const"], 1)
                gp.memset(ident[:, :], 0.0).then_inc(s["const"], 1)
                gp.wait_ge(s["const"], 3)
                gp.affine_select(out=ident[:, :], in_=ident[:, :], compare_op=ALU.not_equal, fill=1.0,
                                 base=0, pattern=[[-1, 128]], channel_multiplier=1).then_inc(s["const"], 1)

            @block.tensor
            def _(pe):
                pe.wait_ge(s["const"], 4)
                pe.wait_ge(s["float"], 1)
                for k in range(5):
                    if k == 2:
                        pe.wait_ge(s["load"], 80)
                    if k >= 4:
                        pe.wait_ge(s["copied"], k - 3)
                    for b in range(NB):
                        src = stage_f[:, k, b, :] if k < 2 else stage3[:, b, k - 2::3]
                        mm = pe.transpose(ps[0:P, 2 * (k % 4) + b // 4, (b % 4) * LB:(b % 4 + 1) * LB], src, ident[0:LB, 0:LB])
                    mm.then_inc(s["turned"], 1)

            @block.vector
            def _(v):
                v.memset(zero_rows, 0.0).then_inc(s["zero"], 1)
                v.wait_ge(s["index"], 32)
                v.tensor_copy(stage_f, stage_i).then_inc(s["float"], 1)
                v.wait_ge(s["const"], 4)
                v.tensor_copy(iota_h[:, :], iota_i)
                v.tensor_copy(quads[:, :, :, :], bc(quads_i[:, None], [P, GMAX, 4, C]))
                v.memset(zeros[:, :], 0.0)
                for k in range(5):
                    v.wait_ge(s["turned"], k + 1)
                    src = ps[0:P, 2 * (k % 4):2 * (k % 4) + 2, 0:4 * LB]
                    to = (srcf[:, :], dstf[:, :], att3[:, :, 0], att3[:, :, 1], att3[:, :, 2])[k]
                    v.tensor_copy(to.rearrange("p (a b) -> p a b", a=2), src).then_inc(s["copied"], 1)
                v.wait_ge(s["copied"], 5)
                n = 0
                for f, q, r, i in ((srcf, src_q, src_r, idx1s), (dstf, dst_q, dst_r, idx1d)):
                    v.tensor_copy(i[:, :], f[:, :])
                    v.tensor_scalar(q[:, :], f[:, :], float(QW), None, ALU.is_ge).then_inc(s["quad"], 1)
                    for m in (2, 3):
                        n += 1
                        v.wait_ge(s["quad"], n)
                        v.scalar_tensor_tensor(q[:, :], f[:, :], float(m * QW), q[:, :], ALU.is_ge, ALU.add).then_inc(s["quad"], 1)
                    n += 1
                    v.wait_ge(s["quad"], n)
                    v.scalar_tensor_tensor(r[:, :], q[:, :], -float(QW), f[:, :], ALU.mult, ALU.add)

        norm_steps, norm_root = sem("norm_steps"), sem("norm_root")

        def layer_norm(layer):
            s, r, n = norm_steps, norm_root, 9 * layer
            sq = carve(P, [NT, C])

            def vec(v):
                v.tensor_reduce(st1[:, :], X[:, :, :], AX.X, ALU.add).then_inc(s, 1)
                v.wait_ge(s, n + 1)
                v.tensor_scalar(st2[:, :], st1[:, :], 1.0 / C, None, ALU.mult).then_inc(s, 1)
                v.wait_ge(s, n + 2)
                v.tensor_tensor(H[:, :, :], X[:, :, :], bc(st2[:, :, None], [P, NT, C]), ALU.subtract).then_inc(s, 1)
                v.wait_ge(s, n + 3)
                v.tensor_tensor(sq, H[:, :, :], H[:, :, :], ALU.mult).then_inc(s, 1)
                v.wait_ge(s, n + 4)
                v.tensor_reduce(st1[:, :], sq, AX.X, ALU.add).then_inc(s, 1)
                v.wait_ge(s, n + 5)
                v.tensor_scalar(st1[:, :], st1[:, :], 1.0 / C, 1e-5, ALU.mult, ALU.add).then_inc(s, 1)
                v.wait_ge(r, layer + 1)
                v.reciprocal(st3[:, :], st2[:, :]).then_inc(s, 1)
                v.wait_ge(s, n + 7)
                v.tensor_tensor(H[:, :, :], H[:, :, :], bc(st3[:, :, None], [P, NT, C]), ALU.mult).then_inc(s, 1)
                v.wait_ge(s, n + 8)
                v.tensor_scalar(H[:, :, :], H[:, :, :], 0.0, None, ALU.max).then_inc(s, 1)

            def sca(a):
                a.wait_ge(s, n + 6)
                a.activation(st2[:, :], st1[:, :], ACT.Sqrt).then_inc(r, 1)

            return vec, sca

        def spline_weights(v, s, base, pseudo, with_node, spline_tmp):
            cnt = [base]

            def done(ins):
                ins.then_inc(s, 1)
                cnt[0] += 1
                v.wait_ge(s, cnt[0])

            pos, i0, fr, b01, kn = spline_tmp
            done(v.tensor_scalar(pos, pseudo, 4.0, None, ALU.mult))
            done(v.tensor_scalar(i0, pos, 1.0, None, ALU.is_ge))
            for m in (2.0, 3.0):
                done(v.scalar_tensor_tensor(i0, pos, m, i0, ALU.is_ge, ALU.add))
            done(v.tensor_tensor(fr[:, :, :, 1], pos, i0, ALU.subtract))
            done(v.tensor_scalar(fr[:, :, :, 0], fr[:, :, :, 1], -1.0, 1.0, ALU.mult, ALU.add))
            done(v.tensor_tensor(b01, bc(fr[:, :, 0, None, :], [P, T, 2, 2]), bc(fr[:, :, 1, :, None], [P, T, 2, 2]), ALU.mult))
            for d1 in range(2):
                for d2 in range(2):
                    done(v.tensor_tensor(basis8[:, :, 4 * d1 + 2 * d2:4 * d1 + 2 * d2 + 2], b01[:, :, d1],
                                         bc(fr[:, :, 2, d2:d2 + 1], [P, T, 2]), ALU.mult))
            done(v.scalar_tensor_tensor(kn, i0[:, :, 0], 5.0, i0[:, :, 1], ALU.mult, ALU.add))
            done(v.scalar_tensor_tensor(kn, kn, 5.0, i0[:, :, 2], ALU.mult, ALU.add))
            if with_node:
                done(v.scalar_tensor_tensor(kn, dstf[:, :], float(KR), kn, ALU.mult, ALU.add))
            done(v.tensor_copy(idxk[:, :] if with_node else idx2[:, :, 0], kn))
            if not with_node:
                done(v.tensor_scalar(idx2[:, :, 1], kn, 25.0, None, ALU.add))
            return cnt[0]

        def two_step(eng, pairs, first, second, lead):
            if first is None:
                with eng.Fori(0, pairs) as i:
                    for x in range(2):
                        second(x, i)
                return
            first(0, 0)
            if lead == 2:
                first(1, 0)
            with eng.Fori(0, pairs - 1) as i:
                first(*((1, i) if lead == 1 else (0, i + 1)))
                second(0, i)
                first(*((0, i + 1) if lead == 1 else (1, i + 1)))
                second(1, i)
            if lead == 1:
                first(1, pairs - 1)
            second(0, pairs - 1)
            second(1, pairs - 1)

        edge_sems = {k: sem("edge_" + k) for k in ["window", "products", "squared", "onehot", "placed"] + [
            f"{k}{x}" for k in ("message", "high", "residual", "middle", "low", "quads", "ready", "scattered",
                                "hidden", "radial", "radial_used") for x in (0, 1)]}

        def zero_edge_sems(sp):
            for k in edge_sems.values():
                sp.sem_clear(k)

        def edge_phase(name, G, on_act, on_act_s, gathers, F, extra, quad, rest, more):
            at[0] = keep
            PAIRS = T // G // 2
            U = F // 32
            FM = F + (2 if extra == "pair" else 0)
            NPASS = 3 * U + (1 if extra == "pair" else 0)
            s = dict(edge_sems)
            rows, wins = {}, {}
            for key, table, idx, ng, run in gathers:
                rows[key] = carve(P, [2, G * ng, run])
                wins[key] = carve(P, [2, G * ng], I32)
                for x in range(2):
                    s[f"{key}{x}"] = sem(f"{name}_{key}{x}")
            msg = carve(P, [2, G, FM])
            res = carve(P, [G, FM])
            part = carve(P, [2, 3, G, FM], BF16)
            stat = carve(P, [2, NPASS, G, 128], BF16)
            GV = G - on_act_s
            GQ = G if extra == "ones" else GV
            ohq = carve(P, [2, GQ, 128], BF16)
            ohr = carve(P, [2, G, QW], BF16)
            square = carve(P, [QW], BF16)
            quad4 = carve(P, [2, G, 4])
            nacc = U + (1 if extra else 0)
            env = dict(rows=rows, F=F, G=G, PAIRS=PAIRS, msg=msg, s=s, name=name)
            more(env)
            with nc.Block() as block:
                @block.gpsimd
                def _(gp):
                    def gather(x, i):
                        for key, table, idx, ng, run in gathers:
                            o = gp.tensor_copy(wins[key][:, x, :], idx[:, bass.ds((2 * i + x) * (G * ng), G * ng)])
                        o.then_inc(s["window"], 1)
                        gp.wait_ge(s["window"], 2 * i + (x + 1))
                        gp.nop(nofuse=True)
                        for key, table, idx, ng, run in gathers:
                            for k in range(G * ng):
                                gp.indirect_dma_start(rows[key][:, x, k, :], None, table, bass.IndirectOffsetOnAxis(
                                    ap=wins[key][:, x, k:k + 1], axis=0)).then_inc(s[f"{key}{x}"], 16)

                    for x in range(2):
                        gather(x, 0)
                    with gp.Fori(1, PAIRS) as i:
                        for x in range(2):
                            gp.wait_ge(s[f"message{x}"], i)
                            gather(x, i)

                @block.vector
                def _(v):
                    if "v_begin" in env:
                        env["v_begin"](v)
                    if extra == "pair":
                        v.memset(stat[:, :, 3 * U, :, :], 0.0)
                    by_quad = lambda a: a.rearrange("p g (q c) -> p g q c", c=C)

                    def split(x, i):
                        g = 2 * i + x
                        v.wait_ge(s[f"high{x}"], i + 1)
                        v.tensor_tensor(res, msg[:, x], part[:, x, 0], ALU.subtract).then_inc(s[f"residual{x}"], 1)
                        v.wait_ge(s[f"scattered{x}"], i + 1)
                        v.tensor_tensor(quad4[:, x], quads[:, 0:G, :, 0], bc(quad[:, bass.ds(g * G, G)][:, :, None], [P, G, 4]), ALU.is_equal)
                        v.tensor_tensor(by_quad(ohq[:, x, 0:GQ]), quads[:, 0:GQ], bc(quad[:, bass.ds(g * G, GQ)][:, :, None, None],
                                        [P, GQ, 4, C]), ALU.is_equal).then_inc(s[f"quads{x}"], 1)
                        for k in range(on_act, G):
                            v.tensor_scalar(ohr[:, x, k, :], iota_h[:, :], rest[:, bass.ds(g * G + k, 1)], None, ALU.is_equal)
                        v.wait_ge(s[f"quads{x}"], i + 1)

                        def spread(k, last=False):
                            for u in range(U):
                                o = v.tensor_tensor(by_quad(stat[:, x, 3 * u + k, 0:GV]), by_quad(ohq[:, x, 0:GV]),
                                                    bc(part[:, x, k, 0:GV, None, 32 * u:32 * u + 32], [P, GV, 4, C]), ALU.mult)
                            if extra == "pair":
                                o = v.tensor_tensor(by_quad(stat[:, x, 3 * U])[:, :, :, 2 * k:2 * k + 2], bc(quad4[:, x, :, :, None], [P, G, 4, 2]),
                                                    bc(part[:, x, k, :, None, F:F + 2], [P, G, 4, 2]), ALU.mult)
                            if last:
                                o.then_inc(s[f"ready{x}"], 1)

                        spread(0)
                        v.wait_ge(s[f"middle{x}"], i + 1)
                        v.tensor_tensor(part[:, x, 2], res, part[:, x, 1], ALU.subtract).then_inc(s[f"low{x}"], 1)
                        spread(1)
                        v.wait_ge(s[f"low{x}"], i + 1)
                        spread(2, last=True)

                    two_step(v, PAIRS, lambda x, i: env["message"](v, env, x, i), split, 1)

                @block.scalar
                def _(a):
                    def high(x, i, start=False):
                        a.wait_ge(s[f"message{x}"], i + 1)
                        if on_act_s and not start:
                            a.wait_ge(s["placed"], 2 * i + x)
                        a.activation(part[:, x, 0], msg[:, x], ACT.Copy).then_inc(s[f"high{x}"], 1)

                    def onehots(x, i):
                        g = 2 * i + x
                        a.wait_ge(s[f"scattered{x}"], i + 1)
                        for k in range(on_act):
                            a.activation(square, iota_h[:, :], ACT.Square, bias=rest[:, bass.ds(g * G + k, 1)], scale=-1.0
                                         ).then_inc(s["squared"], 1)
                            a.wait_ge(s["squared"], g * on_act + (k + 1))
                            a.activation(ohr[:, x, k, :], square, ACT.Relu, bias=1.0, scale=-1.0).then_inc(s["onehot"], 1)
                            a.wait_ge(s["onehot"], g * on_act + (k + 1))

                    def middle(x, i):
                        a.wait_ge(s[f"residual{x}"], i + 1)
                        a.activation(part[:, x, 1], res, ACT.Copy).then_inc(s[f"middle{x}"], 1)

                    def place(x, i):
                        if on_act_s:
                            a.wait_ge(s[f"low{x}"], i + 1)
                            for k in range(GV, G):
                                for q in range(4):
                                    o = a.activation(stat[:, x, 0:3, k, C * q:C * q + C], part[:, x, :, k, :][:, :, 0:C], ACT.Copy,
                                                     scale=quad4[:, x, k, q:q + 1])
                            o.then_inc(s["placed"], 1)

                    if on_act_s:
                        a.sem_inc(s["placed"], 1)
                    first = env.get("a_first", lambda a, x, i: None)
                    first(a, 0, 0)
                    first(a, 1, 0)
                    high(0, 0, True)
                    with a.Fori(0, PAIRS - 1) as i:
                        for x, y, j in ((0, 1, i), (1, 0, i + 1)):
                            first(a, x, i + 1)
                            middle(x, i)
                            high(y, j)
                            onehots(x, i)
                            place(x, i)
                    middle(0, PAIRS - 1)
                    high(1, PAIRS - 1)
                    onehots(0, PAIRS - 1)
                    place(0, PAIRS - 1)
                    middle(1, PAIRS - 1)
                    onehots(1, PAIRS - 1)
                    place(1, PAIRS - 1)

                @block.tensor
                def _(pe):
                    def scatter(x, i):
                        pe.wait_ge(s[f"ready{x}"], i + 1)
                        for k in range(G):
                            if k < on_act:
                                pe.wait_ge(s["onehot"], (2 * i + x) * on_act + (k + 1))
                            if on_act_s and k == GV:
                                pe.wait_ge(s["placed"], 2 * i + (x + 2))
                            jobs = [(p // 3, stat[:, x, p, k, :]) for p in range(3 * U)]
                            if extra == "pair":
                                jobs.append((U, stat[:, x, 3 * U, k, :]))
                            if extra == "ones":
                                jobs.append((U, ohq[:, x, k, :]))
                            for u, w in jobs:
                                for h in range(2):
                                    mm = pe.matmul(ps[:, 2 * u + h, 0:HW], w, ohr[:, x, k, h * HW:(h + 1) * HW],
                                                   start=False, stop=False, skip_group_check=True)
                        mm.then_inc(s[f"scattered{x}"], 1)

                    for b in range(2 * nacc):
                        mm = pe.matmul(ps[:, b, 0:HW], zeros[:, 0:128], zeros[:, 0:HW], start=True, stop=False, skip_group_check=True)
                        if b < 2:
                            mm.then_inc(s[f"scattered{b}"], 1)
                    first = env.get("pe_first")
                    two_step(pe, PAIRS, first and (lambda x, i: first(pe, x, i)), scatter, 2)
                    for b in range(2 * nacc):
                        pe.matmul(ps[:, b, 0:HW], zeros[:, 0:128], zeros[:, 0:HW], start=False, stop=True, skip_group_check=True)

                if "sp" in env:
                    @block.sync
                    def _(sp):
                        env["sp"](sp)

        def unit_to_rows(eng, bank, dst, row):
            for q in range(4):
                for h in range(2):
                    c0 = q * QW + h * HW
                    o = eng(dst[row:row + 32, c0:c0 + HW], ps[32 * q:32 * q + 32, bank + h, 0:HW])
            return o

        def turn_to_nodes(pe, table, bank):
            for j in range(NT):
                mm = pe.transpose(ps[0:P, bank + j // 16, (j % 16) * 32:(j % 16) * 32 + 32], table[0:32, j * P:(j + 1) * P],
                                  ident[0:32, 0:32])
            return mm

        def nodes_of(bank):
            return ps[0:P, bank:bank + 2, :].rearrange("p b (j c) -> p (b j) c", c=32)[:, 0:NT, :]

        def turn_to_features(pe, nodes):
            for j in range(NT):
                mm = pe.transpose(ps[0:32, j // 4, (j % 4) * P:(j % 4 + 1) * P], nodes[:, j, :], ident[0:P, 0:P])
            return mm

        def copy_features(v, dst):
            v.tensor_copy(dst[0:32, 0:24 * P].rearrange("p (b n) -> p b n", b=6), ps[0:32, 0:6, 0:4 * P])
            return v.tensor_copy(dst[0:32, 24 * P:N], ps[0:32, 6, 0:P])

        at[0] = 0
        corner = carve(P, [T, 3])
        frac = carve(P, [T, 3, 2])
        hats = carve(P, [T, 3, 5])
        after_hats = at[0]
        dup_consts = carve(P, [P + 2])
        home = carve(P, [T])
        dup_ints = carve(P, [P + 2], I32)
        hat_tmp = carve(P, [T, 3])
        at[0] = T * 9
        spline_tmp = (carve(P, [T, 3]), corner, frac, carve(P, [T, 2, 2]), carve(P, [T]))
        with nc.Block() as block:
            weights_done = sem("spline1")
            consts_done = sem("spline1_consts")

            @block.gpsimd
            def _(gp):
                gp.iota(dup_ints[:, 0:P], [[-1, P]], base=P, channel_multiplier=0).then_inc(consts_done, 1)
                gp.iota(dup_ints[:, P:P + 1], [[0, 1]], base=P, channel_multiplier=-1).then_inc(consts_done, 1)
                gp.iota(dup_ints[:, P + 1:P + 2], [[0, 1]], base=N, channel_multiplier=1).then_inc(consts_done, 1)

            @block.vector
            def _(v):
                n = spline_weights(v, weights_done, 0, att3[:, :, :], False, spline_tmp)

                def done(ins):
                    nonlocal n
                    ins.then_inc(weights_done, 1)
                    n += 1
                    v.wait_ge(weights_done, n)

                v.memset(hats[:, :, :, 4], 0.0)
                for k in range(4):
                    o = v.scalar_tensor_tensor(hats[:, :, :, k], corner, float(k), frac[:, :, :, 0], ALU.is_equal, ALU.mult)
                done(o)
                for k in range(4):
                    done(v.scalar_tensor_tensor(hat_tmp, corner, float(k), frac[:, :, :, 1], ALU.is_equal, ALU.mult))
                    done(v.tensor_tensor(hats[:, :, :, k + 1], hats[:, :, :, k + 1], hat_tmp, ALU.add))
                v.wait_ge(consts_done, 3)
                done(v.tensor_copy(dup_consts, dup_ints))
                v.tensor_scalar(home, srcf[:, :], dup_consts[:, P + 1:P + 2], None, ALU.subtract)

        D1 = 8
        row = 65
        PAIRS1 = T // D1 // 2
        at[0] = 0
        src_row = carve(128, [2, D1 * P], I32)
        eq = carve(P, [2, D1, P])
        bask = carve(P, [2, D1, KN])
        ranked = carve(P, [D1, P])
        bask2 = carve(P, [D1, 25])
        assert at[0] <= T * 9
        at[0] = after_hats + P + 2 + T
        turned = carve(P, [2, D1, P])
        sums = carve(P, [2, D1, row])
        win1 = carve(P, [2, D1], I32)
        first_rank = carve(P, [2, D1])
        w1 = carve(KN, [64])
        one = carve(P, [1])
        with nc.Block() as block:
            s = {f"{k}{x}": sem(f"c1_{k}{x}") for k in ("src_row", "ready", "step", "turned", "copied", "summed", "rows", "index") for x in range(2)}
            s["weight"], s["one"], s["window"] = sem("c1_weight"), sem("c1_one"), sem("c1_window")
            added = [sem(f"c1_added{k}") for k in range(D1)]
            srcs = A["src"].rearrange("(a n) -> a n", a=1)

            @block.sync
            def _(sp):
                sp.dma_start(w1, A["L1_gnn_stn1_w"].rearrange("k a o -> k (a o)")).then_inc(s["weight"], 16)
                for x in range(2):
                    sp.dma_start(src_row[:, x, :], srcs[:, x * D1 * P:(x + 1) * D1 * P].broadcast_to([128, D1 * P])).then_inc(s[f"src_row{x}"], 16)
                with sp.Fori(1, PAIRS1) as i:
                    for x in range(2):
                        sp.wait_ge(s[f"ready{x}"], i)
                        sp.nop(nofuse=True)
                        sp.dma_start(src_row[:, x, :], srcs[:, bass.ds((2 * i + x) * (D1 * P), D1 * P)].broadcast_to([128, D1 * P])
                                     ).then_inc(s[f"src_row{x}"], 16)

            @block.vector
            def _(v):
                def group(x, i, first=False):
                    g = 2 * i + x
                    here = bass.ds(g * D1, D1)
                    v.wait_ge(s[f"src_row{x}"], 16 * i + 16)
                    if not first:
                        v.wait_ge(s[f"summed{x}"], i)
                    v.tensor_tensor(bask2.rearrange("p g (a b) -> p g a b", b=5), bc(hats[:, here, 0, :, None], [P, D1, 5, 5]),
                                    bc(hats[:, here, 1, None, :], [P, D1, 5, 5]), ALU.mult).then_inc(s[f"step{x}"], 1)
                    v.tensor_tensor(eq[:, x], src_row[0:P, x, :].rearrange("p (g e) -> p g e", g=D1),
                                    bc(srcf[:, here][:, :, None], [P, D1, P]), ALU.is_equal).then_inc(s[f"step{x}"], 1)
                    v.wait_ge(s[f"step{x}"], 4 * i + 1)
                    v.tensor_tensor(bask[:, x].rearrange("p g (a b) -> p g a b", b=5), bc(bask2[:, :, :, None], [P, D1, 25, 5]),
                                    bc(hats[:, here, 2, None, :], [P, D1, 25, 5]), ALU.mult).then_inc(s[f"ready{x}"], 1)
                    v.wait_ge(s[f"step{x}"], 4 * i + 2)
                    v.tensor_tensor(ranked, eq[:, x], bc(dup_consts[:, None, 0:P], [P, D1, P]), ALU.mult).then_inc(s[f"step{x}"], 1)
                    v.wait_ge(s[f"step{x}"], 4 * i + 3)
                    v.tensor_reduce(first_rank[:, x], ranked, AX.X, ALU.max).then_inc(s[f"step{x}"], 1)
                    v.wait_ge(s[f"step{x}"], 4 * i + 4)
                    v.scalar_tensor_tensor(first_rank[:, x], first_rank[:, x], dup_consts[:, P:P + 1], home[:, here],
                                           ALU.is_equal, ALU.mult).then_inc(s["one"], 1)
                    v.wait_ge(s["one"], g + 2)
                    v.tensor_scalar(idxk[:, here], first_rank[:, x], dup_consts[:, P + 1:P + 2], None, ALU.add).then_inc(s[f"index{x}"], 1)

                v.memset(one, 1.0).then_inc(s["one"], 1)
                for x in range(2):
                    group(x, 0, True)
                with v.Fori(1, PAIRS1) as i:
                    for x in range(2):
                        group(x, i)

            @block.tensor
            def _(pe):
                def turn(x, i):
                    pe.wait_ge(s[f"ready{x}"], i + 1)
                    for k in range(D1):
                        mm = pe.matmul(ps[0:KN, 2 * x + k // 4, (k % 4) * P:(k % 4 + 1) * P], bask[:, x, k, :], eq[:, x, k, :],
                                       start=True, stop=True, skip_group_check=True)
                    mm.then_inc(s[f"turned{x}"], 1)

                def multiply(x, i):
                    pe.wait_ge(s[f"copied{x}"], i + 1)
                    pe.wait_ge(s[f"rows{x}"], i + 1)
                    for k in range(D1):
                        pe.matmul(ps[0:P, 4 + x, 64 * k:64 * k + 64], turned[:, x, k, :], w1, start=True, stop=True, skip_group_check=True)
                        mm = pe.matmul(ps[0:P, 6 + x, k:k + 1], eq[:, x, k, :], one, start=True, stop=True, skip_group_check=True)
                    mm.then_inc(s[f"summed{x}"], 1)

                pe.wait_ge(s["weight"], 16)
                pe.wait_ge(s["one"], 1)
                for x in range(2):
                    pe.sem_inc(s[f"rows{x}"], 1)
                two_step(pe, PAIRS1, turn, multiply, 1)

            @block.scalar
            def _(a):
                def copy_turned(x, i):
                    a.wait_ge(s[f"turned{x}"], i + 1)
                    for h in range(2):
                        o = a.activation(turned[:, x, 4 * h:4 * h + 4, :], ps[0:KN, 2 * x + h, 0:4 * P].rearrange("p (g e) -> p g e", g=4), ACT.Copy)
                    o.then_inc(s[f"copied{x}"], 1)

                def rows(x, i, first=False):
                    a.wait_ge(s[f"summed{x}"], i + 1)
                    if not first:
                        for k in range(D1):
                            a.wait_ge(added[k], 32 * i + (16 * x - 16))
                    a.activation(sums[:, x, :, 64], ps[0:P, 6 + x, 0:D1], ACT.Copy)
                    a.activation(sums[:, x, :, 0:64], ps[0:P, 4 + x, :].rearrange("p (g f) -> p g f", g=D1), ACT.Copy).then_inc(s[f"rows{x}"], 1)

                copy_turned(0, 0)
                copy_turned(1, 0)
                rows(0, 0, True)
                copy_turned(0, 1)
                rows(1, 0, True)
                with a.Fori(1, PAIRS1 - 1) as i:
                    copy_turned(1, i)
                    rows(0, i)
                    copy_turned(0, i + 1)
                    rows(1, i)
                copy_turned(1, PAIRS1 - 1)
                rows(0, PAIRS1 - 1)
                rows(1, PAIRS1 - 1)

            @block.gpsimd
            def _(gp):
                def add(x, i, first=False):
                    g = 2 * i + x
                    gp.wait_ge(s[f"index{x}"], i + 1)
                    gp.tensor_copy(win1[:, x, :], idxk[:, bass.ds(g * D1, D1)]).then_inc(s["window"], 1)
                    gp.wait_ge(s["window"], g + 1)
                    gp.wait_ge(s[f"rows{x}"], i + 2)
                    gp.nop(nofuse=True)
                    for k in range(D1):
                        if not first:
                            gp.wait_ge(added[k], 32 * i + 16 * x)
                            gp.nop(nofuse=True)
                        gp.indirect_dma_start(s1_tab[k], bass.IndirectOffsetOnAxis(ap=win1[:, x, k:k + 1], axis=0), sums[:, x, k, :], None,
                                              compute_op=ALU.add).then_inc(added[k], 16)

                add(0, 0, True)
                add(1, 0)
                with gp.Fori(1, PAIRS1) as i:
                    for x in range(2):
                        add(x, i)
                for k in range(D1):
                    gp.wait_ge(added[k], 16 * (T // D1))

        def spline_conv(env):
            s, F, G, msg, rows = env["s"], env["F"], env["G"], env["msg"], env["rows"]["z"]
            runs = rows.shape[2] // G
            prods = carve(P, [2, G, 8, F])

            def message(v, env, x, i):
                g = 2 * i + x
                weights = basis8[:, bass.ds(g * G, G), :]
                prod = prods[:, x]
                v.wait_ge(s[f"z{x}"], runs * 16 * G * i + runs * 16 * G)
                for d1 in range(2):
                    if runs == 1:
                        o = v.tensor_tensor(prod[:, :, 4 * d1:4 * d1 + 4], rows[:, x, :, 10 * F * d1:10 * F * d1 + 4 * F].rearrange(
                            "p g (k f) -> p g k f", k=4), bc(weights[:, :, 4 * d1:4 * d1 + 4, None], [P, G, 4, F]), ALU.mult)
                        continue
                    for d0 in range(2):
                        run = rows[:, x].rearrange("p (g d) n -> p g d n", d=2)[:, :, d0, 5 * F * d1:5 * F * d1 + 2 * F]
                        o = v.tensor_tensor(prod[:, :, 4 * d1 + d0:4 * d1 + 4:2], run.rearrange("p g (k f) -> p g k f", k=2),
                                            bc(weights[:, :, 4 * d1 + d0:4 * d1 + 4:2, None], [P, G, 2, F]), ALU.mult)
                o.then_inc(s["products"], 1)
                v.wait_ge(s["products"], g + 1)
                v.tensor_reduce(msg[:, x], prod.rearrange("p g k f -> p g f k"), AX.X, ALU.add).then_inc(s[f"message{x}"], 1)

            env["message"] = message

        def elu(s, table, rows, bias):
            low = carve(rows, [NP4])

            def sca(a, start):
                a.wait_ge(s, start)
                a.activation(table[0:rows, :], table[0:rows, :], ACT.Identity, bias=bias).then_inc(s, 1)
                a.wait_ge(s, start + 2)
                a.activation(low, low, ACT.Exp).then_inc(s, 1)

            def vec(v, start):
                v.wait_ge(s, start + 1)
                v.tensor_scalar(low, table[0:rows, :], 0.0, None, ALU.min).then_inc(s, 1)
                v.wait_ge(s, start + 3)
                v.tensor_scalar(table[0:rows, :], table[0:rows, :], 0.0, None, ALU.max).then_inc(s, 1)
                v.wait_ge(s, start + 4)
                v.scalar_tensor_tensor(table[0:rows, :], low, -1.0, table[0:rows, :], ALU.add, ALU.add).then_inc(s, 1)

            return sca, vec

        at[0] = 0
        parts = carve(P, [D1, NT, row])
        mean = carve(P, [NT, 64])
        rdeg = carve(P, [NT])
        at_elu = at[0]
        at[0] = 0
        with nc.Block() as block:
            s = {k: sem("n1_" + k) for k in ("load", "sum", "mean", "turned", "copied", "elu")}
            elu_a, elu_v = elu(s["elu"], nodeT, 64, wbias[:, 0:1])

            @block.sync
            def _(sp):
                for k in range(D1):
                    sp.dma_start(parts[:, k], s1_tab[k][0:N, :].rearrange("(j p) c -> p j c", p=P)).then_inc(s["load"], 16)
                sp.wait_ge(s["load"], 16 * D1)

            @block.vector
            def _(v):
                n = [0]

                def done(ins):
                    ins.then_inc(s["sum"], 1)
                    n[0] += 1
                    v.wait_ge(s["sum"], n[0])

                v.wait_ge(s["load"], 16 * D1)
                for step in (4, 2, 1):
                    done(v.tensor_tensor(parts[:, 0:step], parts[:, 0:step], parts[:, step:2 * step], ALU.add))
                total = parts[:, 0]
                v.tensor_copy(deg_s[:, :], total[:, :, 64])
                done(v.tensor_scalar(rdeg, total[:, :, 64], 1.0, None, ALU.max))
                done(v.reciprocal(rdeg, rdeg))
                v.tensor_tensor(mean, total[:, :, 0:64], bc(rdeg[:, :, None], [P, NT, 64]), ALU.mult).then_inc(s["mean"], 1)
                v.wait_ge(s["turned"], 1)
                v.tensor_copy(nodeT[0:64, 0:24 * P].rearrange("p (b n) -> p b n", b=6), ps[0:64, 0:6, 0:4 * P])
                v.tensor_copy(nodeT[0:64, 24 * P:N], ps[0:64, 6, 0:P])
                v.memset(nodeT[0:64, N:NP4], 0.0).then_inc(s["copied"], 1)
                v.tensor_scalar(mean, bc(rdeg[:, :, None], [P, NT, 64]), 1.0, None, ALU.mult).then_inc(s["mean"], 1)
                v.wait_ge(s["turned"], 2)
                v.tensor_copy(rdegT[0:64, 0:24 * P].rearrange("p (b n) -> p b n", b=6), ps[0:64, 0:6, 0:4 * P])
                v.tensor_copy(rdegT[0:64, 24 * P:N], ps[0:64, 6, 0:P])
                v.memset(rdegT[0:64, N:NP4], 1.0).then_inc(s["copied"], 1)
                v.wait_ge(s["copied"], 2)
                v.sem_inc(s["elu"], 1)
                elu_v(v, 1)

            @block.tensor
            def _(pe):
                for k in range(2):
                    pe.wait_ge(s["mean"], k + 1)
                    if k:
                        pe.wait_ge(s["copied"], 1)
                    for j in range(NT):
                        mm = pe.transpose(ps[0:64, j // 4, (j % 4) * P:(j % 4 + 1) * P], mean[:, j, :], ident[0:P, 0:P])
                    mm.then_inc(s["turned"], 1)

            @block.scalar
            def _(a):
                elu_a(a, 1)

        table_sems = {k: sem("table_" + k) for k in ("product", "out_a", "out_v", "high", "residual", "middle", "low", "placed_a",
                                               "placed_v")}

        def table_block(name, F, weight, z_tab, paired, more_v=None):
            cuts = [0, 7, 13, 19, 25] if F == 64 else [0, 13, 25]
            chunks = [(k0, a, b) for k0 in range(5) for a, b in zip(cuts, cuts[1:])]
            per = len(chunks)
            half = [3 * (len(cuts) - 1), per]
            KH = 50 if paired else 75
            W = 2 * F if paired else F
            BANKS = 5
            passes = [[(0, 0), (0, 1)], [(1, 0), (1, 1)], [(0, 2), (2, 0)]] if F == 64 else \
                     [[(0, 0), (1, 0), (2, 0), (0, 1)], [(1, 1), (0, 2)]]
            stacks = []
            for p in passes:
                if [w for _, w in p] not in stacks:
                    stacks.append([w for _, w in p])
            side = [stacks.index([w for _, w in p]) for p in passes]
            CH = KN // 5 * F
            at[0] = 0
            wst = carve(128, [len(stacks), KN * F], BF16)
            hp_at = at[0]
            hst = carve(128, [len(passes), NP4], BF16)
            zst_at = at[0]
            zst = carve(P, [100 if paired else KN, W])
            at[0] = zst_at
            wraw = carve(F, [KN * F])
            at[0] = zst_at
            h_res, h_part = carve(F, [NP4]), carve(F, [3, NP4], BF16)
            at[0] = hp_at
            w_res, w_part = carve(F, [CH]), carve(F, [3, CH], BF16)
            cuts_w = range(0, KN * F, CH)
            splits = [(wraw[:, c:c + CH], w_part, w_res,
                       [(wst[b * F:(b + 1) * F, u, c:c + CH], w) for u, st in enumerate(stacks) for b, w in enumerate(st)]) for c in cuts_w]
            splits.append((nodeT[0:F, :], h_part, h_res,
                           [(hst[b * F:(b + 1) * F, u, :], h) for u, st in enumerate(passes) for b, (h, _) in enumerate(st)]))
            z = z_tab.rearrange("(n k) o -> n k o", n=N)
            with nc.Block() as block:
                s = dict(table_sems, **{k: sem(name + "_" + k) for k in ("weight", "stored0", "stored1")})
                outs = ("out_a", "out_v")

                @block.sync
                def _(sp):
                    sp.dma_start(wraw.rearrange("i (k o) -> i k o", k=KN), weight.rearrange("k i o -> i k o")).then_inc(s["weight"], 16)
                    with sp.Fori(0, NT) as j:
                        for h in range(2):
                            for e in range(2):
                                sp.wait_ge(s[outs[e]], j * (per // 2) + (3 + (half[h] + 1 - e) // 2))
                            sp.nop(nofuse=True)
                            rows = slice(0, KH) if h == 0 else slice(KH, zst.shape[1])
                            for first, many in ((0, 112), (112, P - 112)):
                                sp.dma_start(z[bass.ds(j * P + first, many), rows, :], zst[first:first + many, rows, :]
                                             ).then_inc(s[f"stored{h}"], 16)
                    for h in range(2):
                        sp.wait_ge(s[f"stored{h}"], 32 * NT)

                @block.tensor
                def _(pe):
                    for e in outs:
                        pe.sem_inc(s[e], 3)
                    pe.wait_ge(s["low"], len(splits))
                    pe.wait_ge(s["placed_a"], len(splits))
                    pe.wait_ge(s["placed_v"], len(splits))
                    with pe.Fori(0, NT) as j:
                        for c, (k0, a, b) in enumerate(chunks):
                            pe.wait_ge(s[outs[(c - BANKS) % 2]], j * (per // 2) + ((c - BANKS) // 2 + 4))
                            for n, p in enumerate(passes):
                                K = len(p) * F
                                mm = pe.matmul(ps[0:P, c % BANKS, 0:(b - a) * F], hst[0:K, n, bass.ds(j * P, P)],
                                               wst[0:K, side[n], (25 * k0 + a) * F:(25 * k0 + b) * F],
                                               start=n == 0, stop=n == len(passes) - 1, skip_group_check=True)
                            mm.then_inc(s["product"], 1)

                def copy_out(eng, copy, e, j, first):
                    free = 0
                    for c, (k0, a, b) in enumerate(chunks):
                        if c % 2 != e:
                            continue
                        while not first and free < 2 and k0 >= (0, 2 if paired else 3)[free]:
                            eng.wait_ge(s[f"stored{free}"], 32 * j)
                            free += 1
                        eng.wait_ge(s["product"], j * per + (c + 1))
                        src = ps[0:P, c % BANKS, 0:(b - a) * F].rearrange("p (k f) -> p k f", f=F)
                        if paired and k0 > 0:
                            o = copy(zst[:, 25 * (k0 - 1) + a:25 * (k0 - 1) + b, F:2 * F], src)
                        if not paired or k0 < 4:
                            o = copy(zst[:, 25 * k0 + a:25 * k0 + b, 0:F], src)
                        o.then_inc(s[outs[e]], 1)

                @block.scalar
                def _(a):
                    copy = lambda o, i: a.activation(o, i, ACT.Copy)
                    a.wait_ge(s["weight"], 16)
                    for n, (src, part, res, places) in enumerate(splits):
                        if n:
                            a.wait_ge(s["placed_v"], n)
                            a.wait_ge(s["placed_a"], n)
                        copy(part[:, 0], src).then_inc(s["high"], 1)
                        a.wait_ge(s["residual"], n + 1)
                        copy(part[:, 1], res).then_inc(s["middle"], 1)
                        a.wait_ge(s["low"], n + 1)
                        for to, k in places[0::2]:
                            o = copy(to, part[:, k])
                        o.then_inc(s["placed_a"], 1)
                    a.wait_ge(s["placed_a"], len(splits))
                    a.wait_ge(s["placed_v"], len(splits))
                    copy_out(a, copy, 0, 0, True)
                    with a.Fori(1, NT) as j:
                        copy_out(a, copy, 0, j, False)

                @block.vector
                def _(v):
                    if more_v:
                        more_v(v)
                    copy = lambda o, i: v.tensor_copy(o, i)
                    for n, (src, part, res, places) in enumerate(splits):
                        v.wait_ge(s["high"], n + 1)
                        v.tensor_tensor(res, src, part[:, 0], ALU.subtract).then_inc(s["residual"], 1)
                        v.wait_ge(s["middle"], n + 1)
                        v.tensor_tensor(part[:, 2], res, part[:, 1], ALU.subtract).then_inc(s["low"], 1)
                        v.wait_ge(s["low"], n + 1)
                        for to, k in places[1::2]:
                            o = copy(to, part[:, k])
                        o.then_inc(s["placed_v"], 1)
                    v.wait_ge(s["placed_a"], len(splits))
                    v.wait_ge(s["placed_v"], len(splits))
                    copy_out(v, copy, 1, 0, True)
                    with v.Fori(1, NT) as j:
                        copy_out(v, copy, 1, j, False)

        def add_node(v):
            for k in range(2):
                v.scalar_tensor_tensor(idx2[:, :, k], dstf[:, :], float(KN), idx2[:, :, k], ALU.mult, ALU.add)

        table_block("z2", 64, A["L1_gnn_stn2_w"], z2_tab, False, add_node)
        keep = 0
        edge_phase("e2", 4, 2, 0, (("z", z2_tab, idx2[:, :, :].rearrange("p t k -> p (t k)"), 2, 7 * 64),), 64, None, src_q, src_r, spline_conv)

        at[0] = 0
        w3, w4, h3 = carve(64, [64]), carve(65, [3]), carve(65, [NP4])
        with nc.Block() as block:
            s = {k: sem("n2_" + k) for k in ("load", "sum0", "sum1", "elu", "h3", "product", "ones", "t", "tn", "stored")}
            elu_a, elu_v = elu(s["elu"], nodeT, 64, wbias[:, 1:2])
            elu3_a, elu3_v = elu(s["h3"], h3, 64, wbias[:, 2:3])

            @block.sync
            def _(sp):
                zero_edge_sems(sp)
                for k in table_sems.values():
                    sp.sem_clear(k)
                sp.dma_start(w3, A["L1_gnn_stn3_w"]).then_inc(s["load"], 16)
                sp.dma_start(w4[0:64, :], A["L1_gnn_stn4_w"]).then_inc(s["load"], 16)
                sp.dma_start(w4[64:65, :], A["L1_gnn_stn4_b"].rearrange("(a n) -> a n", a=1)).then_inc(s["load"], 16)
                sp.wait_ge(s["tn"], 1)
                sp.dma_start(t_tab.rearrange("(j p) c -> p j c", p=P), tn[:, :, :]).then_inc(s["stored"], 16)
                sp.wait_ge(s["stored"], 16)

            @block.scalar
            def _(a):
                unit_to_rows(lambda o, i: a.activation(o, i, ACT.Copy), 0, nodeT, 0).then_inc(s["sum0"], 1)
                elu_a(a, 1)
                a.wait_ge(s["product"], 1)
                a.activation(h3[0:64, :].rearrange("p (b n) -> p b n", b=8), ps[0:64, :, 0:HW], ACT.Copy).then_inc(s["h3"], 1)
                elu3_a(a, 1)

            @block.tensor
            def _(pe):
                pe.wait_ge(s["load"], 48)
                pe.wait_ge(s["elu"], 6)
                for b in range(8):
                    mm = pe.matmul(ps[0:64, b, 0:HW], w3, nodeT[0:64, b * HW:(b + 1) * HW], start=True, stop=True)
                mm.then_inc(s["product"], 1)
                pe.wait_ge(s["ones"], 1)
                pe.wait_ge(s["h3"], 6)
                for j in range(NT):
                    mm = pe.matmul(ps[0:P, 0, 3 * j:3 * j + 3], h3[:, j * P:(j + 1) * P], w4, start=True, stop=True)
                mm.then_inc(s["t"], 1)

            @block.vector
            def _(v):
                v.memset(h3[64:65, :], 1.0).then_inc(s["ones"], 1)
                unit_to_rows(lambda o, i: v.tensor_copy(o, i), 2, nodeT, 32).then_inc(s["sum1"], 1)
                v.wait_ge(s["sum0"], 1)
                v.wait_ge(s["sum1"], 1)
                v.tensor_tensor(nodeT[0:64, :], nodeT[0:64, :], rdegT[:, :], ALU.mult).then_inc(s["elu"], 1)
                elu_v(v, 1)
                elu3_v(v, 1)
                v.wait_ge(s["t"], 1)
                v.tensor_copy(tn[:, :, :], ps[0:P, 0, 0:3 * NT].rearrange("p (j c) -> p j c", c=3)).then_inc(s["tn"], 1)

        at[0] = 0
        w2mix = carve(65, [384])
        w1c = carve(64, [2])
        G0 = 8
        hid = carve(65, [2, G0 * P])
        wrow = carve(64, [2, G0 * P])
        keep = at[0]
        w2all = carve(65, [384])
        norm2, square = carve(P, [T]), carve(P, [T])
        with nc.Block() as block:
            vec_norm, sca_norm = layer_norm(0)
            s = {k: sem("l0_" + k) for k in ("weights", "unit", "root", "store", "mix")}

            @block.sync
            def _(sp):
                sp.dma_start(w2all[0:64, :], A["L0_gnn_w2"]).then_inc(s["weights"], 16)
                sp.dma_start(w2all[64:65, :], A["L0_gnn_b2"].rearrange("(a n) -> a n", a=1)).then_inc(s["weights"], 16)
                sp.dma_start(w1c[:, 0:1], A["L0_gnn_w1"].rearrange("a n -> n a")).then_inc(s["weights"], 16)
                sp.dma_start(w1c[:, 1:2], A["L0_gnn_b1"].rearrange("(n a) -> n a", a=1)).then_inc(s["weights"], 16)
                sp.wait_ge(norm_steps, 9)
                sp.dma_start(h0_tab[:, 0:C].rearrange("(j p) c -> p j c", p=P), H[:, :, :]).then_inc(s["store"], 16)
                sp.dma_start(h0_tab[:, C:C + 3].rearrange("(j p) c -> p j c", p=P), tn[:, :, :]).then_inc(s["store"], 16)
                sp.wait_ge(s["store"], 32)

            @block.scalar
            def _(a):
                sca_norm(a)
                a.wait_ge(s["unit"], 5)
                a.activation(square, norm2, ACT.Sqrt).then_inc(s["root"], 1)

            @block.vector
            def _(v):
                vec_norm(v)
                v.memset(hid[64:65, :, :], 1.0)
                n = 0
                v.tensor_tensor(norm2, att3[:, :, 0], att3[:, :, 0], ALU.mult).then_inc(s["unit"], 1)
                for k in (1, 2):
                    n += 1
                    v.wait_ge(s["unit"], n)
                    v.tensor_tensor(square, att3[:, :, k], att3[:, :, k], ALU.mult).then_inc(s["unit"], 1)
                    n += 1
                    v.wait_ge(s["unit"], n)
                    v.tensor_tensor(norm2, norm2, square, ALU.add).then_inc(s["unit"], 1)
                v.wait_ge(s["root"], 1)
                v.reciprocal(norm2, square).then_inc(s["unit"], 1)
                v.wait_ge(s["unit"], 6)
                for to, k in enumerate((1, 2, 0, 1, 2)):
                    v.tensor_tensor(unit[:, :, to], att3[:, :, k], norm2, ALU.mult)
                v.wait_ge(s["weights"], 64)
                w01 = w2all[:, 0:192].rearrange("h (b u w) -> h b u w", b=3, u=8)
                w11 = w2all[:, 192:384].rearrange("h (u w k) -> h u w k", u=8, k=3)
                m1 = w2mix[:, 0:256].rearrange("h (r u x w) -> h r u x w", r=2, u=8, x=2)
                m2 = w2mix[:, 256:384].rearrange("h (r u w) -> h r u w", r=2, u=8)
                v.tensor_scalar(m1[:, 0, :, 0, :], w01[:, 0], PATH_00, None, ALU.mult)
                v.tensor_scalar(m1[:, 0, :, 1, :], w01[:, 1], PATH_01, None, ALU.mult)
                v.tensor_scalar(m1[:, 1, :, 0, :], w01[:, 2], PATH_10, None, ALU.mult)
                v.tensor_scalar(m1[:, 1, :, 1, :], w11[:, :, :, 2], PATH_11_2, None, ALU.mult)
                v.tensor_scalar(m2[:, 1], w11[:, :, :, 1], PATH_11_1, None, ALU.mult)
                v.tensor_scalar(m2[:, 0], w11[:, :, :, 2], -PATH_11_2 / 3.0, None, ALU.mult).then_inc(s["mix"], 1)
                v.wait_ge(s["mix"], 1)
                v.scalar_tensor_tensor(m2[:, 0], w11[:, :, :, 0], PATH_11_0, m2[:, 0], ALU.mult, ALU.add)

        def layer0(env):
            s, name, G, PAIRS = env["s"], env["name"], env["G"], env["PAIRS"]
            x16 = carve(P, [G, 16])
            dots = carve(P, [G, 8, 3])
            prod1_at = at[0]
            prod1 = carve(P, [G, 16, 16])
            prod2 = carve(P, [G, 16, 3, 8])
            red = carve(P, [G, 64])
            end, at[0] = at[0], prod1_at
            hx = carve(P, [G, 8, 5])
            c1, c2, c3 = carve(P, [G, 8, 3]), carve(P, [G, 8, 3]), carve(P, [G, 8, 3])
            at[0] = end
            for x in range(2):
                s[f"weight_row{x}"] = sem(f"weight_row{x}")
            we = A["edge_weight"].rearrange("(a n) -> a n", a=1)

            def sp_prog(sp):
                for x in range(2):
                    sp.dma_start(wrow[:, x, :], we[:, x * G * P:(x + 1) * G * P].broadcast_to([64, G * P])
                                 ).then_inc(s[f"weight_row{x}"], 16)
                with sp.Fori(1, PAIRS) as i:
                    for x in range(2):
                        sp.wait_ge(s[f"hidden{x}"], i)
                        sp.nop(nofuse=True)
                        sp.dma_start(wrow[:, x, :], we[:, bass.ds((2 * i + x) * (G * P), G * P)].broadcast_to([64, G * P])
                                     ).then_inc(s[f"weight_row{x}"], 16)

            def hidden(a, x, i):
                a.wait_ge(s[f"weight_row{x}"], 16 * i + 16)
                a.wait_ge(s[f"radial{x}"], (G // 2) * i + G // 2)
                a.activation(hid[0:64, x, :], wrow[:, x, :], ACT.Relu, bias=w1c[:, 1:2], scale=w1c[:, 0:1]
                             ).then_inc(s[f"hidden{x}"], 1)

            def radial(pe, x, i):
                pe.wait_ge(s[f"hidden{x}"], i + 1)
                for pair in range(G // 2):
                    pe.wait_ge(s[f"radial_used{pair % 2}"], (2 * i + x) * (G // 4) + (pair // 2 + 1))
                    for k in (2 * pair, 2 * pair + 1):
                        mm = pe.matmul(ps[0:P, 4 + k % 4, 0:384], hid[:, x, k * P:(k + 1) * P], w2mix, start=True, stop=True,
                                       skip_group_check=True)
                    mm.then_inc(s[f"radial{x}"], 1)

            def v_begin(v):
                for x in range(2):
                    v.sem_inc(s[f"radial{x}"], G // 2)
                    v.sem_inc(s[f"radial_used{x}"], 1)

            def message(v, env, x, i):
                g = 2 * i + x
                n = [0]
                per = 7

                def done(ins):
                    ins.then_inc(s["products"], 1)
                    n[0] += 1
                    v.wait_ge(s["products"], g * per + n[0])

                rows = env["rows"]["h"][:, x]
                f1 = rows[:, :, 8:32].rearrange("p g (w o) -> p g w o", o=3)
                r = unit[:, bass.ds(g * G, G), :]
                v.wait_ge(s[f"h{x}"], 16 * G * i + 16 * G)
                v.tensor_copy(x16[:, :, 0:8], rows[:, :, 0:8])
                done(v.tensor_tensor(dots, f1, bc(r[:, :, None, 0:3], [P, G, 8, 3]), ALU.mult))
                done(v.tensor_reduce(x16[:, :, 8:16], dots, AX.X, ALU.add))
                for pair in range(G // 2):
                    t2 = slice(2 * pair, 2 * pair + 2)
                    v.wait_ge(s[f"radial{x}"], (G // 2) * i + (G // 2 + pair + 1))
                    bank = 4 + 2 * (pair % 2)
                    rad = ps[0:P, bank:bank + 2, :]
                    v.tensor_tensor(prod1[:, t2], rad[:, :, 0:256].rearrange("p t (r c) -> p t r c", c=16),
                                    bc(x16[:, t2, None, :], [P, 2, 16, 16]), ALU.mult)
                    for t in range(2):
                        k = 2 * pair + t
                        o = v.tensor_tensor(prod2[:, k], bc(rad[:, t, 256:384].rearrange("p (r c) -> p r c", c=8)[:, :, None, :],
                                                            [P, 16, 3, 8]),
                                            bc(f1[:, k].rearrange("p w o -> p o w")[:, None, :, :], [P, 16, 3, 8]), ALU.mult)
                    o.then_inc(s[f"radial_used{pair % 2}"], 1)
                for half in range(2):
                    v.wait_ge(s[f"radial_used{half}"], g * (G // 4) + (G // 4 + 1))
                v.tensor_reduce(red[:, :, 0:16], prod1, AX.X, ALU.add)
                done(v.tensor_reduce(red[:, :, 16:64], prod2.rearrange("p g r o w -> p g (r o) w"), AX.X, ALU.add))
                gu = red[:, :, 16:40].rearrange("p g (u o) -> p g u o", o=3)
                hu = red[:, :, 40:64].rearrange("p g (u o) -> p g u o", o=3)
                qu = red[:, :, 8:16]
                v.tensor_copy(env["msg"][:, x, :, 0:8], red[:, :, 0:8])
                v.tensor_copy(hx[:, :, :, 0:3], hu)
                v.tensor_tensor(c3, bc(qu[:, :, :, None], [P, G, 8, 3]), bc(r[:, :, None, 0:3], [P, G, 8, 3]), ALU.mult)
                done(v.tensor_copy(hx[:, :, :, 3:5], hu[:, :, :, 0:2]))
                v.tensor_tensor(c1, bc(r[:, :, None, 1:4], [P, G, 8, 3]), hx[:, :, :, 2:5], ALU.mult)
                done(v.tensor_tensor(c2, bc(r[:, :, None, 2:5], [P, G, 8, 3]), hx[:, :, :, 1:4], ALU.mult))
                v.tensor_tensor(c3, c3, gu, ALU.add)
                done(v.tensor_tensor(c1, c1, c2, ALU.subtract))
                a3 = att3[:, bass.ds(g * G, G), :]
                v.wait_ge(s[f"t{x}"], 16 * G * i + 16 * G)
                done(v.tensor_tensor(a3, a3, env["rows"]["t"][:, x], ALU.add))
                v.tensor_tensor(a3, a3, rows[:, :, 32:35], ALU.subtract)
                v.tensor_tensor(env["msg"][:, x, :, 8:32].rearrange("p g (u o) -> p g u o", o=3), c1, c3, ALU.add
                                ).then_inc(s[f"message{x}"], 1)
                assert n[0] == per

            env.update(sp=sp_prog, a_first=hidden, v_begin=v_begin, pe_first=radial, message=message)

        edge_phase("e0", G0, 4, 6, (("h", h0_tab, idx1s[:, :], 1, C + 3), ("t", t_tab, idx1d[:, :], 1, 3)),
                   32, "ones", dst_q, dst_r, layer0)

        at[0] = 0
        spline_tmp = (carve(P, [T, 3]), carve(P, [T, 3]), carve(P, [T, 3, 2]), carve(P, [T, 2, 2]), carve(P, [T]))
        degT = carve(32, [NP4])
        with nc.Block() as block:
            vec_norm, sca_norm = layer_norm(1)
            s = {k: sem("n0_" + k) for k in ("sum", "deg", "turned", "features", "spline")}

            @block.sync
            def _(sp):
                zero_edge_sems(sp)

            @block.scalar
            def _(a):
                unit_to_rows(lambda o, i: a.activation(o, i, ACT.Copy), 0, nodeT, 0).then_inc(s["sum"], 1)
                sca_norm(a)

            @block.tensor
            def _(pe):
                pe.wait_ge(s["sum"], 1)
                turn_to_nodes(pe, nodeT, 4).then_inc(s["turned"], 1)
                pe.wait_ge(s["deg"], 1)
                turn_to_nodes(pe, degT, 6).then_inc(s["turned"], 1)
                pe.wait_ge(norm_steps, 18)
                turn_to_features(pe, H).then_inc(s["features"], 1)

            @block.vector
            def _(v):
                unit_to_rows(lambda o, i: v.tensor_copy(o, i), 2, degT, 0).then_inc(s["deg"], 1)
                v.wait_ge(s["turned"], 2)
                v.tensor_copy(deg_d[:, :], nodes_of(6)[:, :, 0])
                v.tensor_tensor(X[:, :, :], X[:, :, :], nodes_of(4), ALU.add).then_inc(s["turned"], 1)
                v.wait_ge(s["turned"], 3)
                vec_norm(v)
                v.tensor_scalar(att3[:, :, :], att3[:, :, :], 0.0, 1.0, ALU.max, ALU.min).then_inc(s["spline"], 1)
                v.wait_ge(s["spline"], 1)
                spline_weights(v, s["spline"], 1, att3[:, :, :], True, spline_tmp)
                v.wait_ge(s["features"], 1)
                copy_features(v, nodeT)

        table_block("z3", 32, A["L1_gnn_conv_w"], z3_tab, True)
        keep = 0
        edge_phase("e3", 8, 1, 5, (("z", z3_tab, idxk[:, :], 1, 7 * 64),), 32, None, src_q, src_r, spline_conv)

        at[0] = 0
        cb = carve(P, [C])
        wl2 = carve(33, [320])
        zl = carve(P, [NT, 288])
        root = carve(P, [NT, C])
        stage2 = carve(LB, [NB, P * 2])
        att2 = carve(P, [T, 2])
        hats = carve(P, [T, 2, 3])
        with nc.Block() as block:
            vec_norm, sca_norm = layer_norm(2)
            s = {k: sem("n4_" + k) for k in ("load", "sum", "mean", "turned", "added", "features", "product", "copied",
                                              "stored", "att", "att_in", "hat")}

            @block.sync
            def _(sp):
                zero_edge_sems(sp)
                sp.dma_start(stage2, A["edge_attr_2"].rearrange("(b r p) c -> r b (p c)", r=LB, p=P)).then_inc(s["load"], 16)
                sp.dma_start(cb, A["L1_gnn_conv_b"].rearrange("(a n) -> a n", a=1).broadcast_to([P, C])).then_inc(s["load"], 16)
                sp.dma_start(wl2[0:32, 0:288].rearrange("i (k o) -> i k o", k=9), A["L2_gnn_weight"].rearrange("k i o -> i k o")
                             ).then_inc(s["load"], 16)
                sp.dma_start(wl2[0:32, 288:320], A["L2_gnn_root_w"]).then_inc(s["load"], 16)
                sp.dma_start(wl2[32:33, 288:320], A["L2_gnn_root_b"].rearrange("(a n) -> a n", a=1)).then_inc(s["load"], 16)
                sp.wait_ge(s["copied"], NT)
                sp.dma_start(zl2_tab.rearrange("(j p) c -> p j c", p=P), zl).then_inc(s["stored"], 16)
                sp.wait_ge(s["stored"], 16)

            @block.scalar
            def _(a):
                unit_to_rows(lambda o, i: a.activation(o, i, ACT.Copy), 0, nodeT, 0).then_inc(s["sum"], 1)
                sca_norm(a)

            @block.tensor
            def _(pe):
                pe.wait_ge(s["mean"], 1)
                turn_to_nodes(pe, nodeT, 4).then_inc(s["turned"], 1)
                pe.wait_ge(norm_steps, 27)
                turn_to_features(pe, H).then_inc(s["turned"], 1)
                pe.wait_ge(s["features"], 1)
                pe.wait_ge(s["load"], 80)
                for j in range(NT):
                    if j >= 8:
                        pe.wait_ge(s["copied"], j - 7)
                    pe.matmul(ps[0:P, j % 8, 0:320], nodeT[0:33, j * P:(j + 1) * P], wl2, start=True, stop=True).then_inc(s["product"], 1)
                pe.wait_ge(s["copied"], NT)
                for k in range(2):
                    for b in range(NB):
                        mm = pe.transpose(ps[0:P, 2 * k + b // 4, (b % 4) * LB:(b % 4 + 1) * LB], stage2[:, b, k::2], ident[0:LB, 0:LB])
                    mm.then_inc(s["att"], 1)

            @block.vector
            def _(v):
                v.wait_ge(s["sum"], 1)
                v.tensor_tensor(nodeT[0:32, :], nodeT[0:32, :], rdegT[0:32, :], ALU.mult).then_inc(s["mean"], 1)
                v.wait_ge(s["load"], 80)
                v.tensor_tensor(X[:, :, :], X[:, :, :], bc(cb[:, None, :], [P, NT, C]), ALU.add).then_inc(s["added"], 1)
                v.wait_ge(s["added"], 1)
                v.wait_ge(s["turned"], 1)
                v.tensor_tensor(X[:, :, :], X[:, :, :], nodes_of(4), ALU.add).then_inc(s["added"], 1)
                v.wait_ge(s["added"], 2)
                vec_norm(v)
                v.memset(wl2[32:33, 0:288], 0.0)
                v.memset(nodeT[32:33, :], 1.0)
                v.wait_ge(s["turned"], 2)
                copy_features(v, nodeT).then_inc(s["features"], 1)
                for j in range(NT):
                    v.wait_ge(s["product"], j + 1)
                    v.tensor_copy(root[:, j, :], ps[0:P, j % 8, 288:320])
                    v.tensor_copy(zl[:, j, :], ps[0:P, j % 8, 0:288]).then_inc(s["copied"], 1)
                for k in range(2):
                    v.wait_ge(s["att"], k + 1)
                    v.tensor_copy(att2[:, :, k].rearrange("p (a b) -> p a b", a=2), ps[0:P, 2 * k:2 * k + 2, 0:4 * LB]).then_inc(s["att_in"], 1)
                v.wait_ge(s["att_in"], 2)
                v.tensor_scalar(att2, att2, 0.0, 1.0, ALU.max, ALU.min).then_inc(s["hat"], 1)
                v.wait_ge(s["hat"], 1)
                for k in range(3):
                    o = v.tensor_scalar(hats[:, :, :, k], att2, -0.5 * k, 2.0, ALU.add, ALU.mult)
                o.then_inc(s["hat"], 1)
                v.wait_ge(s["hat"], 2)
                v.scalar_tensor_tensor(hats, hats, -1.0, hats, ALU.mult, ALU.max).then_inc(s["hat"], 1)
                v.wait_ge(s["hat"], 3)
                v.tensor_scalar(hats, hats, -1.0, 1.0, ALU.mult, ALU.add).then_inc(s["hat"], 1)
                v.wait_ge(s["hat"], 4)
                v.tensor_scalar(hats, hats, 0.0, None, ALU.max).then_inc(s["hat"], 1)
                v.wait_ge(s["hat"], 5)
                for k in range(3):
                    v.tensor_tensor(basis9[:, :, 3 * k:3 * k + 3], hats[:, :, 1], bc(hats[:, :, 0, k:k + 1], [P, T, 3]), ALU.mult)
                v.tensor_copy(H[:, :, :], root)

        def nine_kernels(env):
            msg, s, G, rows = env["msg"], env["s"], env["G"], env["rows"]["z"]
            prods = carve(P, [2, G * 9, C])

            def message(v, env, x, i):
                g = 2 * i + x
                weights = basis9[:, bass.ds(g * G, G), :].rearrange("p g k -> p (g k)")
                prod = prods[:, x]
                v.wait_ge(s[f"z{x}"], 16 * G * i + 16 * G)
                v.tensor_tensor(prod, rows[:, x].rearrange("p g (k f) -> p (g k) f", k=9), bc(weights[:, :, None], [P, G * 9, C]),
                                ALU.mult).then_inc(s["products"], 1)
                v.wait_ge(s["products"], g + 1)
                v.tensor_reduce(msg[:, x], prod.rearrange("p (g k) f -> p g f k", k=9), AX.X, ALU.add).then_inc(s[f"message{x}"], 1)

            env["message"] = message

        keep = 0
        edge_phase("e4", 8, 1, 5, (("z", zl2_tab, idx1s[:, :], 1, 288),), 32, None, dst_q, dst_r, nine_kernels)

        at[0] = 0
        mask = carve(P, [NT])
        dis, dis_m, rd = carve(P, [NT]), carve(P, [NT]), carve(P, [NT])
        y3 = carve(P, [NT, 34])
        with nc.Block() as block:
            vec_norm, sca_norm = layer_norm(3)
            s = {k: sem("n5_" + k) for k in ("load", "sum", "turned", "rd", "root", "dis", "added", "guard", "table", "stored")}

            @block.sync
            def _(sp):
                zero_edge_sems(sp)
                sp.dma_start(mask, A["node_vec1"]).then_inc(s["load"], 16)
                sp.wait_ge(s["table"], 1)
                sp.dma_start(y3_tab.rearrange("(j p) c -> p j c", p=P), y3).then_inc(s["stored"], 16)
                sp.wait_ge(s["stored"], 16)

            @block.scalar
            def _(a):
                unit_to_rows(lambda o, i: a.activation(o, i, ACT.Copy), 0, nodeT, 0).then_inc(s["sum"], 1)
                a.wait_ge(s["dis"], 1)
                a.activation(dis_m, dis, ACT.Sqrt).then_inc(s["root"], 1)
                sca_norm(a)

            @block.tensor
            def _(pe):
                pe.wait_ge(s["sum"], 1)
                turn_to_nodes(pe, nodeT, 4).then_inc(s["turned"], 1)

            @block.vector
            def _(v):
                v.tensor_scalar(dis, deg_s[:, :], 1.0, None, ALU.max).then_inc(s["dis"], 1)
                v.tensor_scalar(rd, deg_d[:, :], 1.0, None, ALU.max).then_inc(s["rd"], 1)
                v.tensor_tensor(X[:, :, :], X[:, :, :], H[:, :, :], ALU.add).then_inc(s["added"], 1)
                v.wait_ge(s["rd"], 1)
                v.reciprocal(rd, rd).then_inc(s["rd"], 1)
                v.wait_ge(s["root"], 1)
                v.reciprocal(dis, dis_m).then_inc(s["dis"], 1)
                v.wait_ge(s["dis"], 2)
                v.scalar_tensor_tensor(dis, deg_s[:, :], 0.0, dis, ALU.is_gt, ALU.mult).then_inc(s["dis"], 1)
                v.wait_ge(s["dis"], 3)
                v.wait_ge(s["load"], 16)
                v.tensor_tensor(dis_m, dis, mask, ALU.mult).then_inc(s["dis"], 1)
                v.wait_ge(s["rd"], 2)
                v.wait_ge(s["turned"], 1)
                v.tensor_tensor(H[:, :, :], nodes_of(4), bc(rd[:, :, None], [P, NT, C]), ALU.mult).then_inc(s["added"], 1)
                v.wait_ge(s["added"], 2)
                v.tensor_tensor(X[:, :, :], X[:, :, :], H[:, :, :], ALU.add).then_inc(s["added"], 1)
                v.wait_ge(s["added"], 3)
                vec_norm(v)
                v.wait_ge(norm_steps, 36)
                big = 3.4028234663852886e38
                v.tensor_scalar(H[:, :, :], H[:, :, :], -big, big, ALU.max, ALU.min).then_inc(s["guard"], 1)
                v.wait_ge(s["guard"], 1)
                v.wait_ge(s["dis"], 4)
                v.tensor_copy(y3[:, :, 32], dis)
                v.tensor_copy(y3[:, :, 33], dis_m)
                v.tensor_tensor(y3[:, :, 0:32], H[:, :, :], bc(dis_m[:, :, None], [P, NT, C]), ALU.mult).then_inc(s["table"], 1)

        def plain(env):
            G = env["G"]

            def message(v, env, x, i):
                v.wait_ge(env["s"][f"y{x}"], 16 * G * i + 16 * G)
                v.tensor_copy(env["msg"][:, x], env["rows"]["y"][:, x]).then_inc(env["s"][f"message{x}"], 1)

            env["message"] = message

        edge_phase("e5", 8, 0, 4, (("y", y3_tab, idx1d[:, :], 1, 34),), 32, "pair", src_q, src_r, plain)

        at[0] = 0
        dis2, dis_2, num, den, zero = (carve(P, [NT]) for _ in range(5))
        wl3, b3 = carve(32, [C]), carve(P, [C])
        res = carve(P, [NT, C])
        with nc.Block() as block:
            s = {k: sem("n6_" + k) for k in ("load", "sum", "pair", "turned", "step", "root", "ratio", "features", "product",
                                              "out", "stored")}

            @block.sync
            def _(sp):
                sp.dma_start(wl3, A["L3_gnn_W"]).then_inc(s["load"], 16)
                sp.dma_start(b3, A["L3_gnn_b"].rearrange("(a n) -> a n", a=1).broadcast_to([P, C])).then_inc(s["load"], 16)
                sp.wait_ge(s["out"], 3)
                sp.dma_start(out.rearrange("(j p) c -> p j c", p=P), X[:, :, :]).then_inc(s["stored"], 16)
                sp.wait_ge(s["stored"], 16)

            @block.scalar
            def _(a):
                unit_to_rows(lambda o, i: a.activation(o, i, ACT.Copy), 0, nodeT, 0).then_inc(s["sum"], 1)
                a.wait_ge(s["step"], 1)
                a.activation(dis_2, dis2, ACT.Sqrt).then_inc(s["root"], 1)

            @block.tensor
            def _(pe):
                pe.wait_ge(s["sum"], 1)
                turn_to_nodes(pe, nodeT, 4).then_inc(s["turned"], 1)
                pe.wait_ge(s["pair"], 1)
                turn_to_nodes(pe, rdegT, 6).then_inc(s["turned"], 1)
                pe.wait_ge(s["ratio"], 1)
                turn_to_features(pe, H).then_inc(s["turned"], 1)
                pe.wait_ge(s["features"], 1)
                pe.wait_ge(s["load"], 32)
                for j in range(NT):
                    mm = pe.matmul(ps[0:P, j // 16, (j % 16) * 32:(j % 16) * 32 + 32], nodeT[0:32, j * P:(j + 1) * P], wl3,
                                   start=True, stop=True)
                mm.then_inc(s["product"], 1)

            @block.vector
            def _(v):
                n = [0]

                def done(ins):
                    ins.then_inc(s["step"], 1)
                    n[0] += 1
                    v.wait_ge(s["step"], n[0])

                unit_to_rows(lambda o, i: v.tensor_copy(o, i), 2, rdegT, 0).then_inc(s["pair"], 1)
                done(v.tensor_scalar(dis2, deg_s[:, :], 1.0, None, ALU.max))
                v.wait_ge(s["root"], 1)
                done(v.reciprocal(dis2, dis_2))
                done(v.scalar_tensor_tensor(dis2, deg_s[:, :], 0.0, dis2, ALU.is_gt, ALU.mult))
                v.wait_ge(s["turned"], 2)
                pair = nodes_of(6)
                done(v.tensor_reduce(num, pair[:, :, 0:6:2], AX.X, ALU.add))
                done(v.tensor_reduce(den, pair[:, :, 1:6:2], AX.X, ALU.add))
                done(v.tensor_tensor(num, num, dis2, ALU.mult))
                done(v.tensor_tensor(den, den, dis2, ALU.mult))
                done(v.tensor_scalar(zero, den, 0.0, None, ALU.is_equal))
                done(v.tensor_tensor(den, den, zero, ALU.add))
                done(v.reciprocal(den, den))
                done(v.tensor_tensor(H[:, :, :], nodes_of(4), bc(dis2[:, :, None], [P, NT, C]), ALU.mult))
                done(v.tensor_tensor(H[:, :, :], H[:, :, :], bc(num[:, :, None], [P, NT, C]), ALU.mult))
                done(v.tensor_tensor(H[:, :, :], H[:, :, :], bc(den[:, :, None], [P, NT, C]), ALU.mult))
                done(v.tensor_scalar(zero, zero, -1.0, 1.0, ALU.mult, ALU.add))
                v.tensor_tensor(H[:, :, :], H[:, :, :], bc(zero[:, :, None], [P, NT, C]), ALU.mult).then_inc(s["ratio"], 1)
                v.wait_ge(s["turned"], 3)
                copy_features(v, nodeT).then_inc(s["features"], 1)
                v.wait_ge(s["load"], 32)
                v.tensor_tensor(X[:, :, :], X[:, :, :], bc(b3[:, None, :], [P, NT, C]), ALU.add).then_inc(s["out"], 1)
                v.wait_ge(s["product"], 1)
                v.wait_ge(s["out"], 1)
                v.tensor_tensor(X[:, :, :], X[:, :, :], nodes_of(0), ALU.add).then_inc(s["out"], 2)


NAMES = ["x", "src", "dst", "edge_attr_2", "edge_attr_3", "edge_weight", "node_vec1", "L0_gnn_w1", "L0_gnn_b1", "L0_gnn_w2",
         "L0_gnn_b2", "L1_gnn_stn1_w", "L1_gnn_stn1_b", "L1_gnn_stn2_w", "L1_gnn_stn2_b", "L1_gnn_stn3_w", "L1_gnn_stn3_b",
         "L1_gnn_stn4_w", "L1_gnn_stn4_b", "L1_gnn_conv_w", "L1_gnn_conv_b", "L2_gnn_weight", "L2_gnn_root_w", "L2_gnn_root_b",
         "L3_gnn_W", "L3_gnn_b"]


def kernel(**inputs):
    import numpy as _np
    import concourse.bacc as _bacc
    from concourse import mybir as _mybir
    from concourse.bass_utils import run_bass_kernel_spmd as _run

    nc = _bacc.Bacc("TRN2", target_bir_lowering=False, num_devices=1)
    arrays, tensors = {}, {}
    for name in NAMES:
        a = inputs[name]
        if name in ("L2_gnn_root_w", "L3_gnn_W"):
            a = _np.asarray(a).T
        if name == "node_vec1":
            a = _np.asarray(a).reshape(NT, P).T
        a = _np.ascontiguousarray(a)
        arrays[f"in_{name}"] = a
        tensors[name] = nc.dram_tensor(f"in_{name}", a.shape, _mybir.dt.from_np(a.dtype), kind="ExternalInput").ap()
    out = nc.dram_tensor("out_0", (N, C), _mybir.dt.float32, kind="ExternalOutput").ap()
    build(nc, tensors, out)
    r = _run(nc, [arrays], core_ids=[0])
    return r.results[0]["out_0"]
```
